# Optimizing a Trainium2 kernel written in Bass

```python
import numpy as np
import jax
import jax.numpy as jnp

def _softmax(x, axis=-1):
    return jax.nn.softmax(x, axis=axis)

def _gelu(x):
    return jax.nn.gelu(x, approximate=True)

def _silu(x):
    return jax.nn.silu(x)

def _sigmoid(x):
    return jax.nn.sigmoid(x)

def _layernorm(x, axis=-1, eps=1e-05):
    m = jnp.mean(x, axis=axis, keepdims=True)
    v = jnp.var(x, axis=axis, keepdims=True)
    return (x - m) / jnp.sqrt(v + eps)

def _scatter_add(tgt, idx, src, axis=0):
    return tgt.at[idx].add(src)

def _segment_sum(src, seg, n):
    return jax.ops.segment_sum(src, seg, n)
kernel_name = 'mk_metaformer_d1_conv_nchw256_r4_77b506'

def setup_inputs(seed: int=0):
    np.random.seed(seed)
    _w = jnp.asarray

    def _rec_inputs():
        import jax
        import jax.numpy as jnp
        _gk = jax.random.key(seed)
        x = -0.0003482 + 1 * jax.random.normal(jax.random.fold_in(_gk, 1), (32, 64, 48, 48), jnp.float32)
        return x
    x = _rec_inputs()

    def _L0_conv_setup():
        import jax, jax.numpy as jnp
        import numpy as np
        GAMMA = 2
        EPS = 1e-08
        key = jax.random.key(seed)
        k1, k2 = jax.random.split(key, 2)
        B, C, H, W = (32, 64, 48, 48)
        x = jax.random.normal(k1, (B, C, H, W), jnp.float32)
        Wc = jax.random.normal(k2, (C, C), jnp.float32) * (1.0 / np.sqrt(C))
        bc = jnp.zeros((C,), jnp.float32)
        return {'x': x, 'Wc': Wc, 'bc': bc}
    _L0_conv_all = _L0_conv_setup()
    _L0_conv_in = {k: v for k, v in _L0_conv_all.items() if k in ('Wc', 'bc')}
    del _L0_conv_all

    def _L0_ffn_setup():
        import jax, jax.numpy as jnp
        import numpy as np
        B, N, D = (16, 1024, 64)
        NUM_EXPERTS, TOP_K, HEADS = (4, 2, 4)
        N_EDGES = 262144
        LN_EPS = 1e-05

        def _layernorm(x, g, b):
            mu = x.mean(-1, keepdims=True)
            var = ((x - mu) ** 2).mean(-1, keepdims=True)
            return (x - mu) * jax.lax.rsqrt(var + LN_EPS) * g + b

        def _forward(x, edge_index, W_gat, att_src, att_dst, b_gat, ln_gamma, ln_beta, W1, b1, W2, b2):
            Bc, Nc, Dc = x.shape
            M = Bc * Nc
            x_flat = x.reshape(M, Dc)
            h = (x_flat @ W_gat).reshape(M, HEADS, NUM_EXPERTS)
            loops = jnp.arange(M, dtype=edge_index.dtype)
            src = jnp.concatenate([edge_index[0], loops])
            dst = jnp.concatenate([edge_index[1], loops])
            a_src = (h * att_src).sum(-1)
            a_dst = (h * att_dst).sum(-1)
            e = jax.nn.leaky_relu(a_src[src] + a_dst[dst], negative_slope=0.2)
            e_max = jax.ops.segment_max(e, dst, num_segments=M)
            ee = jnp.exp(e - e_max[dst])
            denom = jax.ops.segment_sum(ee, dst, num_segments=M)
            alpha = ee / (denom[dst] + 1e-16)
            msg = h[src] * alpha[:, :, None]
            agg = jax.ops.segment_sum(msg, dst, num_segments=M).reshape(M, HEADS * NUM_EXPERTS) + b_gat
            scores = _layernorm(agg, ln_gamma, ln_beta).reshape(M, HEADS, NUM_EXPERTS).mean(1)
            scores = scores.reshape(Bc, Nc, NUM_EXPERTS)
            topk_s, topk_i = jax.lax.top_k(scores, TOP_K)
            w = jax.nn.softmax(topk_s, axis=-1)
            out = jnp.zeros_like(x)
            for ei in range(NUM_EXPERTS):
                g = jnp.where(topk_i == ei, w, 0.0).sum(-1)
                hh = jax.nn.gelu(x @ W1[ei] + b1[ei], approximate=False)
                out = out + g[..., None] * (hh @ W2[ei] + b2[ei])
            return out
        key = jax.random.key(seed)
        ks = jax.random.split(key, 8)
        s = 0.05
        return {'x': jax.random.normal(ks[0], (B, N, D), jnp.float32), 'W_gat': jax.random.normal(ks[1], (D, HEADS * NUM_EXPERTS), jnp.float32) * s, 'att_src': jax.random.normal(ks[2], (HEADS, NUM_EXPERTS), jnp.float32) * s, 'att_dst': jax.random.normal(ks[3], (HEADS, NUM_EXPERTS), jnp.float32) * s, 'b_gat': jnp.zeros((HEADS * NUM_EXPERTS,), jnp.float32), 'ln_gamma': jnp.ones((HEADS * NUM_EXPERTS,), jnp.float32), 'ln_beta': jnp.zeros((HEADS * NUM_EXPERTS,), jnp.float32), 'W1': jax.random.normal(ks[4], (NUM_EXPERTS, D, 2 * D), jnp.float32) * s, 'b1': jnp.zeros((NUM_EXPERTS, 2 * D), jnp.float32), 'W2': jax.random.normal(ks[5], (NUM_EXPERTS, 2 * D, D), jnp.float32) * s, 'b2': jnp.zeros((NUM_EXPERTS, D), jnp.float32), 'edge_index': jax.random.randint(ks[6], (2, N_EDGES), 0, B * N, jnp.int32)}
    _L0_ffn_all = _L0_ffn_setup()
    _L0_ffn_in = {k: v for k, v in _L0_ffn_all.items() if k in ('W_gat', 'att_src', 'att_dst', 'b_gat', 'ln_gamma', 'ln_beta', 'W1', 'b1', 'W2', 'b2', 'edge_index')}
    del _L0_ffn_all
    return {'x': x, 'L0_conv_Wc': _L0_conv_in['Wc'], 'L0_conv_bc': _L0_conv_in['bc'], 'L0_ffn_W_gat': _L0_ffn_in['W_gat'], 'L0_ffn_att_src': _L0_ffn_in['att_src'], 'L0_ffn_att_dst': _L0_ffn_in['att_dst'], 'L0_ffn_b_gat': _L0_ffn_in['b_gat'], 'L0_ffn_ln_gamma': _L0_ffn_in['ln_gamma'], 'L0_ffn_ln_beta': _L0_ffn_in['ln_beta'], 'L0_ffn_W1': _L0_ffn_in['W1'], 'L0_ffn_b1': _L0_ffn_in['b1'], 'L0_ffn_W2': _L0_ffn_in['W2'], 'L0_ffn_b2': _L0_ffn_in['b2'], 'L0_ffn_edge_index': _L0_ffn_in['edge_index']}

def reference(x, L0_conv_Wc, L0_conv_bc, L0_ffn_W_gat, L0_ffn_att_src, L0_ffn_att_dst, L0_ffn_b_gat, L0_ffn_ln_gamma, L0_ffn_ln_beta, L0_ffn_W1, L0_ffn_b1, L0_ffn_W2, L0_ffn_b2, L0_ffn_edge_index):
    import jax
    import jax.numpy as jnp

    def _L0_conv_ref(x, Wc, bc):
        import jax, jax.numpy as jnp
        import numpy as np
        GAMMA = 2
        EPS = 1e-08
        B, C, H, W = x.shape
        P = H * W
        xf = x.reshape(B, C, P)
        nrm = jnp.maximum(jnp.sqrt(jnp.sum(xf * xf, axis=1)), EPS)
        xn = xf / nrm[:, None, :]
        s = jax.nn.relu(jnp.einsum('bcp,bcq->bpq', xn, xn)) ** GAMMA
        g = jnp.einsum('oc,bcp->bop', Wc, xf) + bc[None, :, None]
        out = jnp.einsum('bpq,bcq->bcp', s, g)
        return out.reshape(B, C, H, W)

    def _L0_ffn_ref(x, W_gat, att_src, att_dst, b_gat, ln_gamma, ln_beta, W1, b1, W2, b2, edge_index):
        import jax, jax.numpy as jnp
        import numpy as np
        B, N, D = (16, 1024, 64)
        NUM_EXPERTS, TOP_K, HEADS = (4, 2, 4)
        N_EDGES = 262144
        LN_EPS = 1e-05

        def _layernorm(x, g, b):
            mu = x.mean(-1, keepdims=True)
            var = ((x - mu) ** 2).mean(-1, keepdims=True)
            return (x - mu) * jax.lax.rsqrt(var + LN_EPS) * g + b

        def _forward(x, edge_index, W_gat, att_src, att_dst, b_gat, ln_gamma, ln_beta, W1, b1, W2, b2):
            Bc, Nc, Dc = x.shape
            M = Bc * Nc
            x_flat = x.reshape(M, Dc)
            h = (x_flat @ W_gat).reshape(M, HEADS, NUM_EXPERTS)
            loops = jnp.arange(M, dtype=edge_index.dtype)
            src = jnp.concatenate([edge_index[0], loops])
            dst = jnp.concatenate([edge_index[1], loops])
            a_src = (h * att_src).sum(-1)
            a_dst = (h * att_dst).sum(-1)
            e = jax.nn.leaky_relu(a_src[src] + a_dst[dst], negative_slope=0.2)
            e_max = jax.ops.segment_max(e, dst, num_segments=M)
            ee = jnp.exp(e - e_max[dst])
            denom = jax.ops.segment_sum(ee, dst, num_segments=M)
            alpha = ee / (denom[dst] + 1e-16)
            msg = h[src] * alpha[:, :, None]
            agg = jax.ops.segment_sum(msg, dst, num_segments=M).reshape(M, HEADS * NUM_EXPERTS) + b_gat
            scores = _layernorm(agg, ln_gamma, ln_beta).reshape(M, HEADS, NUM_EXPERTS).mean(1)
            scores = scores.reshape(Bc, Nc, NUM_EXPERTS)
            topk_s, topk_i = jax.lax.top_k(scores, TOP_K)
            w = jax.nn.softmax(topk_s, axis=-1)
            out = jnp.zeros_like(x)
            for ei in range(NUM_EXPERTS):
                g = jnp.where(topk_i == ei, w, 0.0).sum(-1)
                hh = jax.nn.gelu(x @ W1[ei] + b1[ei], approximate=False)
                out = out + g[..., None] * (hh @ W2[ei] + b2[ei])
            return out
        return _forward(x, edge_index, W_gat, att_src, att_dst, b_gat, ln_gamma, ln_beta, W1, b1, W2, b2)

    def _gn(v, G=32, eps=1e-05):
        B_, C_, H_, W_ = v.shape
        g = v.reshape(B_, G, C_ // G, H_, W_)
        m = jnp.mean(g, axis=(2, 3, 4), keepdims=True)
        s = jnp.var(g, axis=(2, 3, 4), keepdims=True)
        return ((g - m) / jnp.sqrt(s + eps)).reshape(v.shape)

    def _ln_c(v, eps=1e-06):
        m = jnp.mean(v, axis=1, keepdims=True)
        s = jnp.var(v, axis=1, keepdims=True)
        return (v - m) / jnp.sqrt(s + eps)

    def _ln_t(v, eps=1e-05):
        m = jnp.mean(v, axis=-1, keepdims=True)
        s = jnp.var(v, axis=-1, keepdims=True)
        return (v - m) / jnp.sqrt(s + eps)

    def _to_tokens(v):
        B_, C_, H_, W_ = v.shape
        return v.reshape(B_, C_, H_ * W_).transpose(0, 2, 1)

    def _from_tokens(t, like):
        B_, C_, H_, W_ = like.shape
        return t.transpose(0, 2, 1).reshape(B_, C_, H_, W_)
    x = x + _L0_conv_ref(_ln_c(x), L0_conv_Wc, L0_conv_bc)
    t = _to_tokens(x)
    t = t + _L0_ffn_ref(_ln_t(t), L0_ffn_W_gat, L0_ffn_att_src, L0_ffn_att_dst, L0_ffn_b_gat, L0_ffn_ln_gamma, L0_ffn_ln_beta, L0_ffn_W1, L0_ffn_b1, L0_ffn_W2, L0_ffn_b2, L0_ffn_edge_index)
    x = _from_tokens(t, x)
    return x

_drawn_inputs = setup_inputs


def setup_inputs(seed=0):
    import zlib

    import numpy as np

    out = dict(_drawn_inputs(seed))
    spreads = {'L0_conv_bc': (0.0, 0.1),
     'L0_ffn_b_gat': (0.0, 0.8),
     'L0_ffn_ln_gamma': (1.0, 0.6),
     'L0_ffn_ln_beta': (0.0, 0.8),
     'L0_ffn_b1': (0.0, 0.8),
     'L0_ffn_b2': (0.0, 0.613)}
    factors = {'L0_ffn_W_gat': 3.747,
     'L0_ffn_att_src': 8.0,
     'L0_ffn_att_dst': 8.0,
     'L0_ffn_W1': 3.382,
     'L0_ffn_W2': 3.12}
    for name, (base, spread) in spreads.items():
        noise = np.random.default_rng([zlib.crc32(name.encode()), seed]).standard_normal(out[name].shape)
        drawn = base * np.exp(spread * noise) if base else spread * noise
        out[name] = jnp.asarray(drawn.astype(out[name].dtype))
    for name, factor in factors.items():
        out[name] = (out[name] * factor).astype(out[name].dtype)
    return out
```

```python
from contextlib import ExitStack
import numpy as np
import concourse.bass as bass
import concourse.mybir as mybir

F32 = mybir.dt.float32
I32 = mybir.dt.int32
ALU = mybir.AluOpType
ACT = mybir.ActivationFunctionType
AX = mybir.AxisListType

P = 128
NEG = -1.0e30
FAR = 1.0e6


def chunks(n, size=512):
    return [(o, min(size, n - o)) for o in range(0, n, size)]


class Net:
    pass


def kernel_program(nc, x, Wc, bc, Wg, att_s, att_d, b_gat, gamma, beta, W1, b1, W2, b2, edges, out):
    B, C, H, W = x.shape
    NP = H * W
    M = B * NP
    E = edges.shape[1]
    HE = Wg.shape[1]
    NH, NX = att_s.shape
    HID = W1.shape[2]
    EC = E // P
    NT = M // P
    n = Net()
    n.B, n.C, n.NP, n.M, n.E, n.HE, n.NH, n.NX, n.HID, n.EC, n.NT = B, C, NP, M, E, HE, NH, NX, HID, EC, NT
    n.ROW = HE + 2 * NH
    n.x2 = nc.dram_tensor("x2_d", (B, C, NP), F32).ap()
    n.tn = nc.dram_tensor("tn_d", (B, C, NP), F32).ap()
    n.htab = nc.dram_tensor("htab_d", (M, HE), F32).ap()
    n.adtab = nc.dram_tensor("adtab_d", (M, NH), F32).ap()
    n.pos = nc.dram_tensor("pos_d", (M, 1), I32).ap()
    n.seg = nc.dram_tensor("seg_d", (E + 1, n.ROW), F32).ap()
    n.row = nc.dram_tensor("row_d", (P, 5 * (HE + NH)), F32).ap()
    n.gates = nc.dram_tensor("gates_d", (NX, M), F32).ap()
    n.xf = x.rearrange("b c h w -> b c (h w)")
    n.of = out.rearrange("b c h w -> b c (h w)")
    with ExitStack() as ctx:
        def sb(name, shape, dt=F32):
            return ctx.enter_context(nc.sbuf_tensor(name, shape, dt))
        n.dsti = sb("dsti", [P, EC], I32)
        n.srci = sb("srci", [P, EC], I32)
        n.start = sb("start", [P, EC])
        n.single = sb("single", [P, 4])
        n.ident = sb("ident", [P, P])
        images_and_sort(nc, n, Wc, bc, Wg, att_s, att_d, edges)
        segments(nc, n, att_s)
        gates(nc, n, att_s, att_d, b_gat, gamma, beta)
        experts(nc, n, W1, b1, W2, b2)


def images_and_sort(nc, n, Wc, bc, Wg, att_s, att_d, edges):
    B, C, NP, HE, NH, NX, EC, M = n.B, n.C, n.NP, n.HE, n.NH, n.NX, n.EC, n.M
    QT = NP // P
    CH = chunks(NP)
    NCH = len(CH)
    STEPS = NCH * QT
    LOG = int(np.log2(n.E))
    LC = int(np.log2(EC))
    with ExitStack() as ctx:
        def sb(name, shape, dt=F32):
            return ctx.enter_context(nc.sbuf_tensor(name, shape, dt))

        def pb(name):
            return ctx.enter_context(nc.psum_tensor(name, [P, 512], F32))

        def sem(name):
            return ctx.enter_context(nc.semaphore(name))
        xb = sb("xb", [C, 2, NP])
        cen = sb("cen", [C, NP])
        sq = sb("sq", [C, 512])
        sd = sb("sd", [C, 512])
        rstd = sb("rstd", [C, 512])
        r2 = sb("r2", [C, 512])
        n2 = sb("n2", [C, 512])
        nrm = sb("nrm", [C, 512])
        rn = sb("rn", [C, 512])
        xl = sb("xl", [C, NP])
        xn = sb("xn", [C, NP])
        gT = sb("gT", [P, QT, C])
        rel = sb("rel", [P, 4, 512])
        s2 = sb("s2", [P, 4, 512])
        half = sb("half", [C, 512])
        x2 = sb("x2", [C, NP])
        tn = sb("tn", [C, NP])
        hx = sb("hx", [P, QT, HE + NH])
        centre = sb("centre", [C, 2, C])
        mean = sb("mean", [C, 2, C])
        wcl = sb("wcl", [C, C])
        wcT = sb("wcT", [C, C])
        bcb = sb("bcb", [P, C])
        wgx = sb("wgx", [C, HE + NH])
        adb = sb("adb", [C, HE])
        wad = sb("wad", [C, HE])
        epsc = sb("epsc", [C, 2])
        KV = sb("KV", [P, 2, EC])
        PV = sb("PV", [P, 2, EC])
        DF = sb("DF", [P, 2, EC])
        MK = sb("MK", [P, EC])
        KK = sb("KK", [P, EC + 2])
        bits = sb("bits", [P, 8])
        sx = sb("sx", [P, 64])
        ei = PV[:, :, :].bitcast(I32)
        endi = ei[:, 0, :]
        posv = ei[:, 1, :]
        zero = KK[:, 0:M // P].bitcast(I32)
        gram = [pb(f"gram{i}") for i in range(4)]
        acc = [pb("acc0"), pb("acc1")]
        lnp = [pb("lnp0"), pb("lnp1")]
        w_in = sem("w_in")
        x_in = [sem("x_in0"), sem("x_in1")]
        xb_free = sem("xb_free")
        const_ready = sem("const_ready")
        wct_ps = sem("wct_ps")
        w_ready = sem("w_ready")
        pe_cen = sem("pe_cen")
        a_sq = sem("a_sq")
        pe_var = sem("pe_var")
        a_sd = sem("a_sd")
        v_n2 = sem("v_n2")
        a_nrm = sem("a_nrm")
        v_ln = sem("v_ln")
        v_r = sem("v_r")
        pe_gt = sem("pe_gt")
        v_gt = sem("v_gt")
        pe_gram = sem("pe_gram")
        a_rel = sem("a_rel")
        v_s2 = sem("v_s2")
        pe_acc = sem("pe_acc")
        v_x2 = sem("v_x2")
        pe_h = sem("pe_h")
        v_h = sem("v_h")
        o_x2 = sem("o_x2")
        o_h = sem("o_h")
        vc = sem("vc")
        e_in = sem("e_in")
        pc = sem("pc")
        kv_out = sem("kv_out")
        pv_in = sem("pv_in")
        z_out = sem("z_out")
        sc_out = [sem("sc_out0"), sem("sc_out1")]
        st = sem("st")
        passed = sem("passed")
        SW = min(64, EC // 2)
        stage = sb("stage", [P, 2, 2, SW], I32)
        block = ctx.enter_context(nc.Block())
        GB = (QT * C + 511) // 512
        GPB = 512 // C
        HPB = 512 // (HE + NH)
        NHB = -(-QT // HPB)
        NLN = 2 * NCH
        stages = [(L, d) for L in range(1, LOG + 1) for d in [1 << t for t in range(L - 1, -1, -1)]]

        def swaps(pd):
            if 2 * pd <= P // pd:
                got = []
                for r in range(pd):
                    a, b = slice(r, P, 2 * pd), slice(r + pd, P, 2 * pd)
                    got += [(a, b), (b, a)]
                return got
            got = []
            for g in range(0, P, 2 * pd):
                a, b = slice(g, g + pd), slice(g + pd, g + 2 * pd)
                got += [(a, b), (b, a)]
            return got

        @block.sync
        def _(sp):
            sp.dma_start(ei, edges.rearrange("a (p j) -> p a j", p=P)).then_inc(e_in, 16)
            sp.dma_start(wcl[:, :], Wc).then_inc(w_in, 16)
            sp.dma_start(bcb[:, :], bc.rearrange("(a c) -> a c", a=1).to_broadcast((P, C))).then_inc(w_in, 16)
            sp.dma_start(wgx[:, 0:HE], Wg).then_inc(w_in, 16)
            sp.dma_start(adb[:, :], att_d.rearrange("(a h) e -> a (h e)", a=1).to_broadcast((C, HE))).then_inc(w_in, 16)
            sp.wait_ge(z_out, 1)
            sp.dma_start(n.pos.rearrange("(p t) a -> p (t a)", p=P), zero).then_inc(z_out, 16)
            served = 0
            for L, d in stages:
                if d >= EC:
                    served += 1
                    sp.wait_ge(kv_out, served)
                    for a, b in swaps(d // EC):
                        sp.dma_start(PV[b, :, :], KV[a, :, :]).then_inc(pv_in, 16)
            sp.wait_ge(kv_out, served + 1)
            sp.dma_start(KK[1:P, 0:1], KV[0:P - 1, 0, EC - 1:EC]).then_inc(pv_in, 16)
            sp.dma_start(KK[0:P - 1, EC + 1:EC + 2], KV[1:P, 0, 0:1]).then_inc(pv_in, 16)

        @block.gpsimd
        def _(pool):
            done = [0]

            def step(ins):
                done[0] += 1
                ins.then_inc(pc, 1)
                pool.wait_ge(pc, done[0])
            step(pool.memset(n.ident[:, :], 0.0))
            step(pool.affine_select(out=n.ident[:, :], in_=n.ident[:, :], compare_op=ALU.not_equal, fill=1.0, base=0,
                                    pattern=[[-1, P]], channel_multiplier=1))
            step(pool.memset(mean[:, :, :], 1.0 / C))
            pool.tensor_tensor(centre[:, :, :], n.ident[0:C, 0:C].unsqueeze(1).to_broadcast([C, 2, C]), mean[:, :, :],
                               ALU.subtract).then_inc(const_ready, 1)
            pool.memset(epsc[:, 0:1], 1e-6).then_inc(const_ready, 1)
            pool.memset(epsc[:, 1:2], 1e-5).then_inc(const_ready, 1)
            pool.memset(zero, 0).then_inc(z_out, 1)
            for b in range(8):
                w = 1 << b
                v = MK[:, 0:P].rearrange("p (g two run) -> p g two run", two=2, run=w) if w < P else None
                step(pool.memset(MK[:, 0:P], 1.0))
                if v is not None:
                    step(pool.memset(v[:, :, 1, :], -1.0))
                step(pool.tensor_tensor(DF[:, 0, 0:P], MK[:, 0:P], n.ident[:, :], ALU.mult))
                step(pool.tensor_tensor(DF[:, 1, 0:64], DF[:, 0, 0:64], DF[:, 0, 64:128], ALU.add))
                w2 = 32
                while w2:
                    step(pool.tensor_tensor(DF[:, 1, 0:w2], DF[:, 1, 0:w2], DF[:, 1, w2:2 * w2], ALU.add))
                    w2 //= 2
                step(pool.tensor_copy(bits[:, b:b + 1], DF[:, 1, 0:1]))
            for b in range(8):
                step(pool.tensor_scalar(sx[:, 8 * b:8 * b + 8], bits[:, :], bits[:, b:b + 1], None, ALU.mult))
            pool.wait_ge(e_in, 16)
            step(pool.tensor_copy(KV[:, 0, :], ei[:, 1, :]))
            step(pool.tensor_copy(KV[:, 1, :], ei[:, 0, :]))
            served = arrived = 0
            for L, d in stages:
                if d >= EC:
                    served += 1
                    pool.sem_inc(kv_out, 1)
                    arrived += 16 * len(swaps(d // EC))
                    pool.wait_ge(pv_in, arrived)
                    col = 8 * (L - LC) + int(np.log2(d // EC))
                    step(pool.tensor_tensor(DF[:, :, :], PV[:, :, :], KV[:, :, :], ALU.subtract))
                    step(pool.tensor_scalar(MK[:, :], DF[:, 0, :], sx[:, col:col + 1], 0.0, ALU.mult, ALU.is_lt))
                    step(pool.tensor_tensor(DF[:, :, :], DF[:, :, :], MK[:, :].unsqueeze(1).to_broadcast([P, 2, EC]), ALU.mult))
                    step(pool.tensor_tensor(KV[:, :, :], KV[:, :, :], DF[:, :, :], ALU.add))
                    continue
                pair = KV[:, :, :].rearrange("p a (g two run) -> p a g two run", two=2, run=d)
                lo, hi = pair[:, :, :, 0, :], pair[:, :, :, 1, :]
                HC = EC // 2
                df = DF[:, :, 0:HC]
                dv = df.rearrange("p a (g run) -> p a g run", run=d)
                step(pool.tensor_tensor(dv, hi, lo, ALU.subtract))
                if L < LC:
                    t = DF[:, 0, 0:HC].rearrange("p (g two run) -> p g two run", two=2, run=1 << (L - 1))
                    u = MK[:, 0:HC].rearrange("p (g two run) -> p g two run", two=2, run=1 << (L - 1))
                    pool.tensor_scalar(u[:, :, 0, :], t[:, :, 0, :], 0.0, None, ALU.is_lt)
                    step(pool.tensor_scalar(u[:, :, 1, :], t[:, :, 1, :], 0.0, None, ALU.is_gt))
                else:
                    b = L - LC
                    step(pool.tensor_scalar(MK[:, 0:HC], DF[:, 0, 0:HC], bits[:, b:b + 1], 0.0, ALU.mult, ALU.is_lt))
                step(pool.tensor_tensor(df, df, MK[:, 0:HC].unsqueeze(1).to_broadcast([P, 2, HC]), ALU.mult))
                pool.tensor_tensor(lo, lo, dv, ALU.add)
                step(pool.tensor_tensor(hi, hi, dv, ALU.subtract))
            pool.wait_ge(z_out, 17)
            step(pool.memset(KK[:, :], -1.0))
            step(pool.tensor_copy(KK[:, 1:EC + 1], KV[:, 0, :]))
            pool.sem_inc(kv_out, 1)
            step(pool.tensor_copy(n.dsti[:, :], KV[:, 0, :]))
            step(pool.tensor_copy(n.srci[:, :], KV[:, 1, :]))
            pool.wait_ge(pv_in, arrived + 32)
            step(pool.tensor_tensor(n.start[:, :], KK[:, 0:EC], KK[:, 1:EC + 1], ALU.subtract))
            step(pool.tensor_scalar(n.start[:, :], n.start[:, :], 0.0, None, ALU.is_equal))
            step(pool.tensor_scalar(n.start[:, :], n.start[:, :], -1.0, -NEG, ALU.add, ALU.mult))
            step(pool.tensor_tensor(DF[:, 0, :], KK[:, 1:EC + 1], KK[:, 2:EC + 2], ALU.subtract))
            step(pool.tensor_scalar(DF[:, 0, :], DF[:, 0, :], 0.0, None, ALU.is_equal))
            step(pool.tensor_scalar(DF[:, 1, :], DF[:, 0, :], FAR, None, ALU.mult))
            step(pool.tensor_tensor(DF[:, 1, :], DF[:, 1, :], KK[:, 1:EC + 1], ALU.add))
            step(pool.tensor_copy(endi, DF[:, 1, :]))
            step(pool.iota(posv, pattern=[[1, EC]], base=1, channel_multiplier=EC))
            step(pool.tensor_copy(DF[:, 1, :], posv))
            step(pool.tensor_scalar(DF[:, 0, :], DF[:, 0, :], FAR, None, ALU.mult))
            step(pool.tensor_tensor(DF[:, 1, :], DF[:, 1, :], DF[:, 0, :], ALU.add))
            pool.sem_inc(kv_out, 1)
            with pool.Fori(0, EC // (2 * SW)) as it:
                for par in range(2):
                    k = it * 2 + par
                    pool.wait_ge(sc_out[par], it * 16 * SW)
                    pool.sem_inc(passed, 1)
                    pool.tensor_copy(stage[:, par, 0, :], endi[:, bass.ds(k * SW, SW)]).then_inc(st, 1)
                    pool.tensor_copy(stage[:, par, 1, :], posv[:, bass.ds(k * SW, SW)]).then_inc(st, 1)
                    pool.wait_ge(st, k * 2 + 2)
                    pool.sem_inc(passed, 1)
                    for j in range(SW):
                        pool.indirect_dma_start(out=n.pos, out_offset=bass.IndirectOffsetOnAxis(ap=stage[:, par, 0, j:j + 1], axis=0),
                                                in_=stage[:, par, 1, j:j + 1], in_offset=None, bounds_check=M - 1,
                                                oob_is_err=False).then_inc(sc_out[par], 16)
            for par in range(2):
                pool.wait_ge(sc_out[par], 16 * EC // 2)

        @block.tensor
        def _(pe):
            pe.wait_ge(const_ready, 3)
            pe.wait_ge(w_in, 64)
            pe.transpose(lnp[0][0:C, 0:C], wcl[:, :], n.ident[0:C, 0:C]).then_inc(wct_ps, 1)
            pe.wait_ge(w_ready, 2)
            with pe.Fori(0, B // 2) as ii:
                for par in range(2):
                    b = ii * 2 + par

                    def ln(src, first):
                        for c, (o, w) in enumerate(CH):
                            k = first + c
                            if c:
                                pe.wait_ge(v_ln, b * NLN + k)
                            pe.matmul(lnp[0][:, 0:w], centre[:, :, :].rearrange("p a c -> p (a c)"), src[:, o:o + w], start=True, stop=True).then_inc(pe_cen, 1)
                            pe.wait_ge(a_sq, b * NLN + k + 1)
                            pe.matmul(lnp[1][:, 0:w], mean[:, :, :].rearrange("p a c -> p (a c)"), sq[:, 0:w], start=True, stop=True).then_inc(pe_var, 1)
                    pe.wait_ge(x_in[par], (ii + 1) * 16)
                    pe.wait_ge(v_h, b * NHB)
                    ln(xb[:, par, :], 0)
                    pe.wait_ge(v_ln, b * NLN + NCH)
                    for gb in range(GB):
                        if gb:
                            pe.wait_ge(v_gt, b * GB + gb)
                        for k in range(min(GPB, QT - gb * GPB)):
                            q = gb * GPB + k
                            last = pe.matmul(lnp[0][:, k * C:(k + 1) * C], xl[:, q * P:(q + 1) * P], wcT[:, :], start=True, stop=True)
                        last.then_inc(pe_gt, 1)
                    pe.wait_ge(v_gt, (b + 1) * GB)
                    LAG = 2
                    for t in range(STEPS + LAG):
                        if t < STEPS:
                            c, q = divmod(t, QT)
                            o, w = CH[c]
                            if t >= 4:
                                pe.wait_ge(a_rel, b * STEPS + t - 3)
                            pe.matmul(gram[t % 4][:, 0:w], xn[:, q * P:(q + 1) * P], xn[:, o:o + w],
                                      start=True, stop=True).then_inc(pe_gram, 1)
                        u = t - LAG
                        if u >= 0:
                            c, q = divmod(u, QT)
                            o, w = CH[c]
                            h = C * (q % 2)
                            pe.wait_ge(v_s2, b * STEPS + u + 1)
                            if c >= 2 and q == 0:
                                pe.wait_ge(v_x2, b * NCH + c - 1)
                            pe.matmul(acc[c % 2][h:h + C, 0:w], gT[:, q, :], s2[:, u % 4, 0:w], start=q < 2,
                                      stop=q >= QT - 2).then_inc(pe_acc, 1)
                    pe.wait_ge(v_x2, (b + 1) * NCH)
                    ln(x2, NCH)
                    pe.wait_ge(v_ln, (b + 1) * NLN)
                    for hb in range(NHB):
                        if hb:
                            pe.wait_ge(v_h, b * NHB + hb)
                        for k in range(min(HPB, QT - hb * HPB)):
                            q = hb * HPB + k
                            last = pe.matmul(lnp[0][:, k * (HE + NH):(k + 1) * (HE + NH)], tn[:, q * P:(q + 1) * P],
                                             wgx[:, :], start=True, stop=True)
                        last.then_inc(pe_h, 1)

        @block.scalar
        def _(act):
            act.dma_start(xb[:, 0, :], n.xf[0]).then_inc(x_in[0], 16)
            act.dma_start(xb[:, 1, :], n.xf[1]).then_inc(x_in[1], 16)
            act.wait_ge(const_ready, 3)
            with act.Fori(0, B // 2) as ii:
                for par in range(2):
                    b = ii * 2 + par

                    def ln(first, eps):
                        for c, (o, w) in enumerate(CH):
                            k = first + c
                            act.wait_ge(pe_cen, b * NLN + k + 1)
                            act.activation(cen[:, o:o + w], lnp[0][0:C, 0:w], ACT.Copy)
                            act.activation(sq[:, 0:w], lnp[0][0:C, 0:w], ACT.Square).then_inc(a_sq, 1)
                            act.wait_ge(pe_var, b * NLN + k + 1)
                            act.activation(sd[:, 0:w], lnp[1][0:C, 0:w], ACT.Sqrt, bias=epsc[:, eps:eps + 1]).then_inc(a_sd, 1)
                            if first == 0:
                                act.wait_ge(v_n2, b * NCH + c + 1)
                                act.activation(nrm[:, 0:w], n2[:, 0:w], ACT.Sqrt).then_inc(a_nrm, 1)
                    ln(0, 0)
                    for t in range(STEPS):
                        c, q = divmod(t, QT)
                        w = CH[c][1]
                        act.wait_ge(pe_gram, b * STEPS + t + 1)
                        if t >= 4:
                            act.wait_ge(v_s2, b * STEPS + t - 3)
                        act.activation(rel[:, t % 4, 0:w], gram[t % 4][:, 0:w], ACT.Relu).then_inc(a_rel, 1)
                    ln(NCH, 1)
                    act.wait_ge(v_ln, (b + 1) * NLN)
                    act.dma_start(n.x2[bass.ds(b, 1), :, :].rearrange("a c p -> (a c) p"), x2[:, :]).then_inc(o_x2, 16)
                    act.dma_start(n.tn[bass.ds(b, 1), :, :].rearrange("a c p -> (a c) p"), tn[:, :]).then_inc(o_x2, 16)
                    act.wait_ge(v_h, (b + 1) * NHB)
                    act.dma_start(n.htab[bass.ds(b * NP, NP), :].rearrange("(q p) c -> p q c", p=P), hx[:, :, 0:HE]).then_inc(o_h, 16)
                    act.dma_start(n.adtab[bass.ds(b * NP, NP), :].rearrange("(q p) c -> p q c", p=P), hx[:, :, HE:HE + NH]).then_inc(o_h, 16)
                    nb = ii * 2 + par + 2
                    act.dma_start(xb[:, par, :], n.xf[bass.ds(nb % B, 1), :, :].rearrange("a c p -> (a c) p")).then_inc(x_in[par], 16)
            act.wait_ge(o_x2, 32 * B)
            act.wait_ge(o_h, 32 * B)
            act.wait_ge(x_in[0], 16 * (B // 2 + 1))
            act.wait_ge(x_in[1], 16 * (B // 2 + 1))

        @block.vector
        def _(dve):
            dve.wait_ge(w_in, 64)
            dve.wait_ge(wct_ps, 1)
            dve.tensor_copy(wcT[:, :], lnp[0][0:C, 0:C]).then_inc(w_ready, 1)
            dve.tensor_tensor(wad[:, :], wgx[:, 0:HE], adb[:, :], ALU.mult).then_inc(vc, 1)
            dve.wait_ge(vc, 1)
            dve.tensor_reduce(wgx[:, HE:HE + NH], wad[:, :].rearrange("p (h e) -> p h e", e=NX), AX.X, ALU.add).then_inc(w_ready, 1)
            with dve.Fori(0, B // 2) as ii:
                for par in range(2):
                    b = ii * 2 + par
                    cnt = [0]
                    NLINK = 3 * NCH + NCH + NCH

                    def link(ins):
                        cnt[0] += 1
                        ins.then_inc(vc, 1)
                        dve.wait_ge(vc, b * NLINK + cnt[0] + 1)
                    for c, (o, w) in enumerate(CH):
                        dve.wait_ge(a_sd, b * NLN + c + 1)
                        link(dve.reciprocal(rstd[:, 0:w], sd[:, 0:w]))
                        dve.tensor_tensor(xl[:, o:o + w], cen[:, o:o + w], rstd[:, 0:w], ALU.mult)
                        link(dve.tensor_tensor(r2[:, 0:w], rstd[:, 0:w], rstd[:, 0:w], ALU.mult))
                        link(dve.scalar_tensor_tensor(n2[:, 0:w], lnp[1][0:C, 0:w], float(C), r2[:, 0:w], ALU.mult, ALU.mult))
                        dve.tensor_scalar(n2[:, 0:w], n2[:, 0:w], 1e-16, None, ALU.max).then_inc(v_n2, 1)
                        dve.wait_ge(a_nrm, b * NCH + c + 1)
                        dve.reciprocal(rn[:, 0:w], nrm[:, 0:w]).then_inc(v_r, 1)
                        dve.wait_ge(v_r, b * NCH + c + 1)
                        dve.tensor_tensor(xn[:, o:o + w], xl[:, o:o + w], rn[:, 0:w], ALU.mult).then_inc(v_ln, 1)
                    for gb in range(GB):
                        k = min(GPB, QT - gb * GPB)
                        dve.wait_ge(pe_gt, b * GB + gb + 1)
                        dve.tensor_tensor(gT[:, gb * GPB:gb * GPB + k, :], lnp[0][:, 0:k * C].rearrange("p (k c) -> p k c", c=C),
                                          bcb[:, :].unsqueeze(1).to_broadcast([P, k, C]), ALU.add).then_inc(v_gt, 1)
                    for t in range(STEPS + 4):
                        if t < STEPS:
                            w = CH[t // QT][1]
                            dve.wait_ge(a_rel, b * STEPS + t + 1)
                            if t >= 4:
                                dve.wait_ge(pe_acc, b * STEPS + t - 3)
                            dve.tensor_tensor(s2[:, t % 4, 0:w], rel[:, t % 4, 0:w], rel[:, t % 4, 0:w], ALU.mult).then_inc(v_s2, 1)
                        if t >= QT + 3 and (t - 3) % QT == 0:
                            c = (t - 3) // QT - 1
                            o, w = CH[c]
                            dve.wait_ge(pe_acc, b * STEPS + (c + 1) * QT)
                            if c == 0:
                                dve.wait_ge(o_x2, b * 32)
                            link(dve.tensor_tensor(half[:, 0:w], acc[c % 2][0:C, 0:w], xb[:, par, o:o + w], ALU.add))
                            dve.tensor_tensor(x2[:, o:o + w], acc[c % 2][C:2 * C, 0:w], half[:, 0:w], ALU.add).then_inc(v_x2, 1)
                    for c, (o, w) in enumerate(CH):
                        dve.wait_ge(a_sd, b * NLN + NCH + c + 1)
                        link(dve.reciprocal(rstd[:, 0:w], sd[:, 0:w]))
                        dve.tensor_tensor(tn[:, o:o + w], cen[:, o:o + w], rstd[:, 0:w], ALU.mult).then_inc(v_ln, 1)
                    dve.wait_ge(o_h, b * 32)
                    for hb in range(NHB):
                        k = min(HPB, QT - hb * HPB)
                        dve.wait_ge(pe_h, b * NHB + hb + 1)
                        dve.tensor_copy(hx[:, hb * HPB:hb * HPB + k, :], lnp[0][:, 0:k * (HE + NH)].rearrange("p (k c) -> p k c", c=HE + NH)).then_inc(v_h, 1)
            dve.wait_ge(kv_out, 28 + 2 if LOG == 18 else len([1 for s in stages if s[1] >= EC]) + 2)
            dve.tensor_reduce(n.single[:, 0:1], n.start[:, 1:EC], AX.X, ALU.min)
            dve.tensor_copy(n.single[:, 1:2], n.start[:, 0:1])
            dve.tensor_reduce(n.single[:, 2:3], DF[:, 1, :], AX.X, ALU.min)


def segments(nc, n, att_s):
    HE, NH, NX, EC, M, ROW, E = n.HE, n.NH, n.NX, n.EC, n.M, n.ROW, n.E
    NC5 = NH * (NX + 1)
    CW = min(64, EC // 2)
    NK = EC // CW
    with ExitStack() as ctx:
        def sb(name, shape, dt=F32):
            return ctx.enter_context(nc.sbuf_tensor(name, shape, dt))

        def sem(name):
            return ctx.enter_context(nc.semaphore(name))
        rows = sb("rows", [P, 2, CW, ROW])
        idx = sb("idx", [P, 2, 2, CW], I32)
        attb = sb("attb", [P, HE])
        stc = sb("stc", [P, CW])
        prod = sb("prod", [P, CW, HE])
        asr = sb("asr", [P, CW, NH])
        ee = sb("ee", [P, CW, NH])
        D0 = sb("D0", [P, NH, CW + 1])
        D1 = sb("D1", [P, NH, CW + 1])
        MF = sb("MF", [P, NH, CW + 1])
        X = sb("X", [P, 2, NH, CW])
        FX = sb("FX", [P, 2, NH, CW])
        G0 = sb("G0", [P, NH, NX + 1, CW + 1])
        G1 = sb("G1", [P, NH, NX + 1, CW + 1])
        S = sb("S", [P, NH, NX + 1, CW + 1])
        empty = sb("empty", [1, ROW])
        tails = sb("tails", [P, 3, NC5])
        rt = sb("rt", [NC5, 3, P])
        Mo = sb("Mo", [NC5, P + 1])
        ex = sb("ex", [NC5, 2, P])
        ea = sb("ea", [NC5, 2, P])
        So = sb("So", [NC5, P + 1])
        carry = sb("carry", [P, 2, NC5])
        fidx = sb("fidx", [P, 2])
        fi = sb("fi", [P, 2], I32)
        fix = sb("fix", [P, ROW])
        fixo = sb("fixo", [P, ROW])
        mm = sb("mm", [P, 3, NH])
        me = sb("me", [P, 2, NH])
        part = sb("part", [P, 2, NC5])
        a_in = sem("a_in")
        slot_free = sem("slot_free")
        ist = sem("ist")
        passed = sem("spassed")
        rows_in = [sem("rows_in0"), sem("rows_in1")]
        vq = sem("vq")
        v_x = sem("v_x")
        a_x = sem("a_x")
        v_rows = sem("v_rows")
        rows_out = sem("rows_out")
        e_out = sem("e_out")
        v_tails = sem("v_tails")
        bounce = sem("bounce")
        v_car = sem("v_car")
        v_fi = sem("v_fi")
        fix_in = sem("fix_in")
        v_fixo = sem("v_fixo")
        fix_out = sem("fix_out")
        block = ctx.enter_context(nc.Block())
        segv = n.seg[1:1 + E, :].rearrange("(p j) c -> p j c", p=P)
        rowt = n.row[:, 0:3 * NC5]
        rowc = n.row[:, 3 * NC5:5 * NC5]

        @block.sync
        def _(sp):
            sp.dma_start(attb[:, :], att_s.rearrange("(a h) e -> a (h e)", a=1).to_broadcast((P, HE))).then_inc(a_in, 16)
            sp.wait_ge(e_out, 1)
            sp.dma_start(n.seg[0:1, :], empty[:, :]).then_inc(e_out, 16)
            with sp.Fori(0, NK // 2) as it:
                for par in range(2):
                    k = it * 2 + par
                    sp.wait_ge(v_rows, k + 1)
                    sp.dma_start(segv[:, bass.ds(k * CW, CW), :].rearrange("p j c -> p (j c)"),
                                 rows[:, par, :, :].rearrange("p j c -> p (j c)")).then_inc(rows_out, 16)
                    sp.wait_ge(rows_out, k * 16 + 16)
                    sp.sem_inc(slot_free, 1)
            sp.wait_ge(e_out, 17)
            sp.wait_ge(v_tails, 1)
            sp.dma_start(rowt, tails[:, :, :].rearrange("p k c -> p (k c)")).then_inc(bounce, 16)
            sp.wait_ge(bounce, 16)
            for k in range(3):
                sp.dma_start(rt[:, k, :], n.row[:, k * NC5:(k + 1) * NC5].rearrange("p c -> c p"), allow_slow_non_contiguous=True).then_inc(bounce, 16)
            sp.wait_ge(v_car, 1)
            sp.dma_start(n.row[:, 3 * NC5:4 * NC5].rearrange("p c -> c p"), So[:, 0:P], allow_slow_non_contiguous=True).then_inc(bounce, 16)
            sp.dma_start(n.row[:, 4 * NC5:5 * NC5].rearrange("p c -> c p"), Mo[:, 0:P], allow_slow_non_contiguous=True).then_inc(bounce, 16)
            sp.wait_ge(bounce, 96)
            sp.dma_start(carry[:, :, :].rearrange("p k c -> p (k c)"), rowc).then_inc(bounce, 16)

        @block.gpsimd
        def _(pool):
            pool.memset(empty[:, 0:NC5], 0.0)
            pool.memset(empty[:, NC5:ROW], NEG).then_inc(e_out, 1)
            pool.memset(fix[:, :], 0.0)
            with pool.Fori(0, NK // 2) as it:
                for par in range(2):
                    k = it * 2 + par
                    pool.wait_ge(slot_free, k + 1)
                    pool.sem_inc(passed, 1)
                    pool.tensor_copy(idx[:, par, 0, :], n.srci[:, bass.ds(k * CW, CW)]).then_inc(ist, 1)
                    pool.tensor_copy(idx[:, par, 1, :], n.dsti[:, bass.ds(k * CW, CW)]).then_inc(ist, 1)
                    pool.wait_ge(ist, k * 2 + 2)
                    pool.sem_inc(passed, 1)
                    for j in range(CW):
                        pool.indirect_dma_start(out=rows[:, par, j, 0:HE], out_offset=None, in_=n.htab,
                                                in_offset=bass.IndirectOffsetOnAxis(ap=idx[:, par, 0, j:j + 1], axis=0)).then_inc(rows_in[par], 16)
                        pool.indirect_dma_start(out=rows[:, par, j, HE:HE + NH], out_offset=None, in_=n.adtab,
                                                in_offset=bass.IndirectOffsetOnAxis(ap=idx[:, par, 1, j:j + 1], axis=0)).then_inc(rows_in[par], 16)
            pool.wait_ge(v_fi, 1)
            pool.wait_ge(rows_out, 16 * NK)
            pool.indirect_dma_start(out=fix[:, :], out_offset=None, in_=n.seg,
                                    in_offset=bass.IndirectOffsetOnAxis(ap=fi[:, 0:1], axis=0),
                                    bounds_check=E, oob_is_err=False).then_inc(fix_in, 16)
            pool.wait_ge(v_fixo, 1)
            pool.indirect_dma_start(out=n.seg, out_offset=bass.IndirectOffsetOnAxis(ap=fi[:, 1:2], axis=0),
                                    in_=fixo[:, :], in_offset=None,
                                    bounds_check=E, oob_is_err=False).then_inc(fix_out, 16)
            pool.wait_ge(fix_out, 16)

        @block.scalar
        def _(act):
            with act.Fori(0, NK) as k:
                act.wait_ge(v_x, k + 1)
                act.activation(FX[:, :, :, :].rearrange("p a h j -> p (a h j)"), X[:, :, :, :].rearrange("p a h j -> p (a h j)"), ACT.Exp).then_inc(a_x, 1)
            act.wait_ge(v_x, NK + 1)
            act.activation(ea[:, :, :].rearrange("c a p -> c (a p)"), ex[:, :, :].rearrange("c a p -> c (a p)"), ACT.Exp).then_inc(a_x, 1)
            act.wait_ge(v_x, NK + 2)
            act.activation(me[:, :, :].rearrange("p a h -> p (a h)"), mm[:, 1:3, :].rearrange("p a h -> p (a h)"), ACT.Exp).then_inc(a_x, 1)

        @block.vector
        def _(dve):
            dve.memset(D0[:, :, 0:1], NEG)
            dve.memset(MF[:, :, CW:CW + 1], NEG)
            dve.memset(G0[:, :, :, 0:1], 0.0)
            dve.memset(Mo[:, 0:1], NEG)
            dve.memset(So[:, 0:1], 0.0)
            dve.memset(S[:, :, :, CW:CW + 1], 0.0).then_inc(slot_free, 2)
            dve.wait_ge(slot_free, 2)
            dve.wait_ge(a_in, 16)
            NL = 10
            with dve.Fori(0, NK // 2) as it:
                for par in range(2):
                    k = it * 2 + par
                    cnt = [0]

                    def link(ins):
                        cnt[0] += 1
                        ins.then_inc(vq, 1)
                        dve.wait_ge(vq, k * NL + cnt[0])
                    dve.tensor_copy(D1[:, :, 0:1], MF[:, :, CW:CW + 1])
                    dve.tensor_copy(G1[:, :, :, 0:1], S[:, :, :, CW:CW + 1])
                    link(dve.tensor_copy(stc[:, :], n.start[:, bass.ds(k * CW, CW)]))
                    dve.tensor_copy(D0[:, :, 1:CW + 1], stc[:, :].unsqueeze(1).to_broadcast([P, NH, CW]))
                    dve.wait_ge(rows_in[par], (it + 1) * 32 * CW)
                    r = rows[:, par, :, :]
                    link(dve.tensor_tensor(prod[:, :, :], r[:, :, 0:HE], attb[:, :].unsqueeze(1).to_broadcast([P, CW, HE]), ALU.mult))
                    link(dve.tensor_reduce(asr[:, :, :], prod[:, :, :].rearrange("p j (h e) -> p j h e", e=NX), AX.X, ALU.add))
                    link(dve.tensor_tensor(ee[:, :, :], asr[:, :, :], r[:, :, HE:HE + NH], ALU.add))
                    link(dve.scalar_tensor_tensor(D1[:, :, 1:CW + 1].rearrange("p h j -> p j h"), ee[:, :, :], 0.2, ee[:, :, :], ALU.mult, ALU.max))
                    link(dve.tensor_tensor_scan(MF[:, :, :].rearrange("p h j -> p (h j)"), D0[:, :, :].rearrange("p h j -> p (h j)"),
                                                D1[:, :, :].rearrange("p h j -> p (h j)"), NEG, ALU.add, ALU.max))
                    link(dve.tensor_tensor(X[:, 0, :, :], MF[:, :, 0:CW], D0[:, :, 1:CW + 1], ALU.add))
                    link(dve.tensor_tensor(X[:, 0, :, :], X[:, 0, :, :], MF[:, :, 1:CW + 1], ALU.subtract))
                    dve.tensor_tensor(X[:, 1, :, :], D1[:, :, 1:CW + 1], MF[:, :, 1:CW + 1], ALU.subtract).then_inc(v_x, 1)
                    dve.wait_ge(a_x, k + 1)
                    dve.tensor_copy(G0[:, :, :, 1:CW + 1], FX[:, 0, :, :].unsqueeze(2).to_broadcast([P, NH, NX + 1, CW]))
                    dve.tensor_copy(G1[:, :, NX, 1:CW + 1], FX[:, 1, :, :])
                    for h in range(NH):
                        last = dve.tensor_tensor(G1[:, h, 0:NX, 1:CW + 1], r[:, :, h * NX:(h + 1) * NX].rearrange("p j e -> p e j"),
                                                 FX[:, 1, h, :].unsqueeze(1).to_broadcast([P, NX, CW]), ALU.mult)
                    link(last)
                    link(dve.tensor_tensor_scan(S[:, :, :, :].rearrange("p h e j -> p (h e j)"), G0[:, :, :, :].rearrange("p h e j -> p (h e j)"),
                                                G1[:, :, :, :].rearrange("p h e j -> p (h e j)"), 0.0, ALU.mult, ALU.add))
                    dve.tensor_copy(r[:, :, 0:NC5], S[:, :, :, :].rearrange("p h e j -> p (h e) j")[:, :, 1:CW + 1].rearrange("p c j -> p j c"))
                    dve.tensor_copy(r[:, :, NC5:ROW], MF[:, :, 1:CW + 1].rearrange("p h j -> p j h")).then_inc(v_rows, 1)
                    dve.wait_ge(v_rows, k + 1)
                    assert cnt[0] == NL, cnt
            done = [NK * NL]

            def step(ins):
                done[0] += 1
                ins.then_inc(vq, 1)
                dve.wait_ge(vq, done[0])
            dve.tensor_copy(tails[:, 0, :], S[:, :, :, CW:CW + 1].rearrange("p h e a -> p (h e a)"))
            for e in range(NX + 1):
                dve.tensor_copy(tails[:, 1, e::NX + 1], MF[:, :, CW:CW + 1].rearrange("p h a -> p (h a)"))
            step(dve.tensor_tensor(fidx[:, 0:1], n.single[:, 0:1], n.single[:, 1:2], ALU.min))
            dve.tensor_copy(tails[:, 2, :], fidx[:, 0:1].to_broadcast([P, NC5])).then_inc(v_tails, 1)
            step(dve.tensor_scalar(fidx[:, 1:2], n.single[:, 1:2], FAR / NEG, None, ALU.mult))
            step(dve.tensor_tensor(fidx[:, 1:2], fidx[:, 1:2], n.single[:, 2:3], ALU.add))
            dve.tensor_copy(fi[:, 0:1], n.single[:, 2:3])
            dve.tensor_copy(fi[:, 1:2], fidx[:, 1:2]).then_inc(v_fi, 1)
            dve.wait_ge(bounce, 64)
            step(dve.tensor_tensor_scan(Mo[:, 1:P + 1], rt[:, 2, :], rt[:, 1, :], NEG, ALU.add, ALU.max))
            step(dve.tensor_tensor(ex[:, 0, :], Mo[:, 0:P], rt[:, 2, :], ALU.add))
            step(dve.tensor_tensor(ex[:, 0, :], ex[:, 0, :], Mo[:, 1:P + 1], ALU.subtract))
            dve.tensor_tensor(ex[:, 1, :], rt[:, 1, :], Mo[:, 1:P + 1], ALU.subtract).then_inc(v_x, 1)
            dve.wait_ge(a_x, NK + 1)
            step(dve.tensor_tensor(ea[:, 1, :], ea[:, 1, :], rt[:, 0, :], ALU.mult))
            dve.tensor_tensor_scan(So[:, 1:P + 1], ea[:, 0, :], ea[:, 1, :], 0.0, ALU.mult, ALU.add).then_inc(v_car, 1)
            dve.wait_ge(bounce, 112)
            dve.wait_ge(fix_in, 16)
            step(dve.tensor_tensor(mm[:, 0, :], fix[:, NC5:ROW], carry[:, 1, ::NX + 1], ALU.max))
            dve.tensor_tensor(mm[:, 1, :], fix[:, NC5:ROW], mm[:, 0, :], ALU.subtract)
            dve.tensor_tensor(mm[:, 2, :], carry[:, 1, ::NX + 1], mm[:, 0, :], ALU.subtract).then_inc(v_x, 1)
            dve.tensor_copy(fixo[:, NC5:ROW], mm[:, 0, :])
            dve.wait_ge(a_x, NK + 2)
            v5 = "p (h e) -> p h e"
            dve.tensor_tensor(part[:, 0, :].rearrange(v5, h=NH), fix[:, 0:NC5].rearrange(v5, h=NH),
                              me[:, 0, :].unsqueeze(2).to_broadcast([P, NH, NX + 1]), ALU.mult)
            step(dve.tensor_tensor(part[:, 1, :].rearrange(v5, h=NH), carry[:, 0, :].rearrange(v5, h=NH),
                                   me[:, 1, :].unsqueeze(2).to_broadcast([P, NH, NX + 1]), ALU.mult))
            dve.tensor_tensor(fixo[:, 0:NC5], part[:, 0, :], part[:, 1, :], ALU.add).then_inc(v_fixo, 1)


def gates(nc, n, att_s, att_d, b_gat, gamma, beta):
    HE, NH, NX, M, ROW, NT = n.HE, n.NH, n.NX, n.M, n.ROW, n.NT
    NC5 = NH * (NX + 1)
    TW = 48 if NT % 96 == 0 else NT // 2
    NK = NT // TW
    with ExitStack() as ctx:
        def sb(name, shape, dt=F32):
            return ctx.enter_context(nc.sbuf_tensor(name, shape, dt))

        def sem(name):
            return ctx.enter_context(nc.semaphore(name))
        pos = sb("pos", [P, NT], I32)
        idx = sb("nidx", [P, 2, TW], I32)
        R = sb("R", [P, 2, TW, ROW])
        Hn = sb("Hn", [P, 2, TW, HE])
        AD = sb("AD", [P, 2, TW, NH])
        cst = sb("cst", [P, 4, HE])
        low = sb("low", [P, NX, NX])
        high = sb("high", [P, NX, NX])
        T0 = sb("T0", [P, TW, HE])
        T1 = sb("T1", [P, TW, HE])
        T2 = sb("T2", [P, TW, HE])
        U0 = sb("U0", [P, TW, NH])
        U1 = sb("U1", [P, TW, NH])
        MX = sb("MX", [P, TW, NH])
        X = sb("Xg", [P, 2, TW, NH])
        FX = sb("FXg", [P, 2, TW, NH])
        dn = sb("dn", [P, TW, NH])
        s1 = sb("s1", [P, TW])
        s3 = sb("s3", [P, TW])
        s4 = sb("s4", [P, TW])
        sc = sb("sc", [P, TW, NX])
        es = sb("es", [P, TW, NX])
        xs = sb("xs", [P, TW, NX])
        G = sb("G", [P, 2, NX, TW])
        eps = sb("epsg", [P, 1])
        c_in = sem("gc_in")
        ist = sem("gist")
        passed = sem("gpassed")
        slot_free = sem("gslot_free")
        r_in = [sem("r_in0"), sem("r_in1")]
        h_in = [sem("h_in0"), sem("h_in1")]
        vq = sem("gvq")
        v_x = sem("gv_x")
        a_x = sem("ga_x")
        v_g = sem("v_g")
        g_out = sem("g_out")
        m_rdy = sem("m_rdy")
        block = ctx.enter_context(nc.Block())
        hv = n.htab.rearrange("(p t) c -> p t c", p=P)
        av = n.adtab.rearrange("(p t) c -> p t c", p=P)
        gv = n.gates.rearrange("e (p t) -> p e t", p=P)

        @block.sync
        def _(sp):
            sp.dma_start(pos[:, :], n.pos.rearrange("(p t) a -> p (t a)", p=P)).then_inc(c_in, 16)
            sp.dma_start(cst[:, 0, :], att_s.rearrange("(a h) e -> a (h e)", a=1).to_broadcast((P, HE))).then_inc(c_in, 16)
            for k, v in ((1, b_gat), (2, gamma), (3, beta)):
                sp.dma_start(cst[:, k, :], v.rearrange("(a c) -> a c", a=1).to_broadcast((P, HE))).then_inc(c_in, 16)
            with sp.Fori(0, NK // 2) as it:
                for par in range(2):
                    k = it * 2 + par
                    sp.wait_ge(slot_free, k + 1)
                    sp.dma_start(Hn[:, par, :, :], hv[:, bass.ds(k * TW, TW), :]).then_inc(h_in[par], 16)
                    sp.dma_start(AD[:, par, :, :], av[:, bass.ds(k * TW, TW), :]).then_inc(h_in[par], 16)

        @block.gpsimd
        def _(pool):
            pool.memset(low[:, :, :], 0.0)
            pool.memset(high[:, :, :], 0.0).then_inc(m_rdy, 1)
            pool.memset(eps[:, :], 1e-5)
            pool.wait_ge(m_rdy, 1)
            for i in range(NX - 1):
                pool.memset(low[:, i + 1, 0:i + 1], 1.0)
                pool.memset(high[:, i, i + 1:NX], 1.0).then_inc(m_rdy, 1)
            pool.wait_ge(c_in, 80)
            with pool.Fori(0, NK // 2) as it:
                for par in range(2):
                    k = it * 2 + par
                    pool.wait_ge(slot_free, k + 1)
                    pool.sem_inc(passed, 1)
                    pool.tensor_copy(idx[:, par, :], pos[:, bass.ds(k * TW, TW)]).then_inc(ist, 1)
                    pool.wait_ge(ist, k + 1)
                    pool.sem_inc(passed, 1)
                    for j in range(TW):
                        pool.indirect_dma_start(out=R[:, par, j, :], out_offset=None, in_=n.seg,
                                                in_offset=bass.IndirectOffsetOnAxis(ap=idx[:, par, j:j + 1], axis=0)).then_inc(r_in[par], 16)

        @block.scalar
        def _(act):
            act.wait_ge(m_rdy, NX)
            with act.Fori(0, NK // 2) as it:
                for par in range(2):
                    k = it * 2 + par
                    act.wait_ge(v_x, k * 3 + 1)
                    act.activation(FX[:, :, :, :].rearrange("p a t h -> p (a t h)"), X[:, :, :, :].rearrange("p a t h -> p (a t h)"), ACT.Exp).then_inc(a_x, 1)
                    act.wait_ge(v_x, k * 3 + 2)
                    act.activation(s3[:, :], s1[:, :], ACT.Sqrt, bias=eps[:, 0:1], scale=1.0 / HE).then_inc(a_x, 1)
                    act.wait_ge(v_x, k * 3 + 3)
                    act.activation(es[:, :, :], xs[:, :, :], ACT.Exp).then_inc(a_x, 1)
                    act.wait_ge(v_g, k + 1)
                    act.dma_start(gv[:, :, bass.ds(k * TW, TW)], G[:, par, :, :]).then_inc(g_out, 16)
            act.wait_ge(g_out, 16 * NK)

        @block.vector
        def _(dve):
            dve.wait_ge(m_rdy, NX)
            dve.wait_ge(c_in, 80)
            dve.memset(s1[:, :], 0.0).then_inc(slot_free, 2)
            bc = lambda k: cst[:, k, :].unsqueeze(1).to_broadcast([P, TW, HE])
            hx = lambda ap: ap.unsqueeze(3).to_broadcast([P, TW, NH, NX])
            v4 = lambda ap: ap.rearrange("p t (h e) -> p t h e", e=NX)
            bt = lambda ap: ap.unsqueeze(2).to_broadcast([P, TW, HE])
            b4 = lambda ap: ap.unsqueeze(2).to_broadcast([P, TW, NX])
            NL = 29
            with dve.Fori(0, NK // 2) as it:
                for par in range(2):
                    k = it * 2 + par
                    cnt = [0]

                    def link(ins):
                        cnt[0] += 1
                        ins.then_inc(vq, 1)
                        dve.wait_ge(vq, k * NL + cnt[0])
                    dve.wait_ge(h_in[par], (it + 1) * 32)
                    dve.wait_ge(r_in[par], (it + 1) * 16 * TW)
                    dve.wait_ge(g_out, it * 32)
                    r = R[:, par, :, :]
                    r5 = r[:, :, 0:NC5].rearrange("p t (h e) -> p t h e", h=NH)
                    link(dve.tensor_tensor(T0[:, :, :], Hn[:, par, :, :], bc(0), ALU.mult))
                    link(dve.tensor_reduce(U0[:, :, :], v4(T0[:, :, :]), AX.X, ALU.add))
                    link(dve.tensor_tensor(U0[:, :, :], U0[:, :, :], AD[:, par, :, :], ALU.add))
                    link(dve.scalar_tensor_tensor(U1[:, :, :], U0[:, :, :], 0.2, U0[:, :, :], ALU.mult, ALU.max))
                    link(dve.tensor_tensor(MX[:, :, :], r[:, :, NC5:ROW], U1[:, :, :], ALU.max))
                    dve.tensor_tensor(X[:, 0, :, :], r[:, :, NC5:ROW], MX[:, :, :], ALU.subtract)
                    dve.tensor_tensor(X[:, 1, :, :], U1[:, :, :], MX[:, :, :], ALU.subtract).then_inc(v_x, 1)
                    dve.wait_ge(a_x, k * 3 + 1)
                    link(dve.tensor_tensor(dn[:, :, :], r5[:, :, :, NX], FX[:, 0, :, :], ALU.mult))
                    link(dve.scalar_tensor_tensor(dn[:, :, :], FX[:, 1, :, :], 1e-16, dn[:, :, :], ALU.add, ALU.add))
                    dve.tensor_tensor(v4(T0[:, :, :]), r5[:, :, :, 0:NX], hx(FX[:, 0, :, :]), ALU.mult)
                    dve.tensor_tensor(v4(T1[:, :, :]), v4(Hn[:, par, :, :]), hx(FX[:, 1, :, :]), ALU.mult)
                    link(dve.reciprocal(U0[:, :, :], dn[:, :, :]))
                    link(dve.tensor_tensor(T0[:, :, :], T0[:, :, :], T1[:, :, :], ALU.add))
                    link(dve.tensor_tensor(v4(T0[:, :, :]), v4(T0[:, :, :]), hx(U0[:, :, :]), ALU.mult))
                    link(dve.tensor_tensor(T0[:, :, :], T0[:, :, :], bc(1), ALU.add))
                    link(dve.tensor_reduce(s1[:, :], T0[:, :, :], AX.X, ALU.add))
                    link(dve.tensor_scalar(s4[:, :], s1[:, :], 1.0 / HE, None, ALU.mult))
                    link(dve.tensor_tensor(T1[:, :, :], T0[:, :, :], bt(s4[:, :]), ALU.subtract))
                    link(dve.tensor_tensor(T2[:, :, :], T1[:, :, :], T1[:, :, :], ALU.mult))
                    dve.tensor_reduce(s1[:, :], T2[:, :, :], AX.X, ALU.add).then_inc(v_x, 1)
                    dve.wait_ge(a_x, k * 3 + 2)
                    link(dve.reciprocal(s4[:, :], s3[:, :]))
                    link(dve.tensor_tensor(T1[:, :, :], T1[:, :, :], bt(s4[:, :]), ALU.mult))
                    link(dve.tensor_tensor(T1[:, :, :], T1[:, :, :], bc(2), ALU.mult))
                    link(dve.tensor_tensor(T1[:, :, :], T1[:, :, :], bc(3), ALU.add))
                    link(dve.tensor_reduce(xs[:, :, :], T1[:, :, :].rearrange("p t (h e) -> p t e h", e=NX), AX.X, ALU.add))
                    link(dve.tensor_scalar(sc[:, :, :], xs[:, :, :], 1.0 / NH, None, ALU.mult))
                    si = sc[:, :, :].unsqueeze(3).to_broadcast([P, TW, NX, NX])
                    sj = sc[:, :, :].unsqueeze(2).to_broadcast([P, TW, NX, NX])
                    dve.tensor_tensor(v4(T0[:, :, :]), sj, si, ALU.is_ge)
                    link(dve.tensor_tensor(v4(T1[:, :, :]), sj, si, ALU.is_gt))
                    dve.tensor_tensor(v4(T0[:, :, :]), v4(T0[:, :, :]), low[:, :, :].unsqueeze(1).to_broadcast([P, TW, NX, NX]), ALU.mult)
                    link(dve.tensor_tensor(v4(T1[:, :, :]), v4(T1[:, :, :]), high[:, :, :].unsqueeze(1).to_broadcast([P, TW, NX, NX]), ALU.mult))
                    link(dve.tensor_tensor(T2[:, :, :], T0[:, :, :], T1[:, :, :], ALU.add))
                    dve.tensor_reduce(U0[:, :, :], v4(T2[:, :, :]), AX.X, ALU.add)
                    link(dve.tensor_reduce(s4[:, :], sc[:, :, :], AX.X, ALU.max))
                    dve.tensor_tensor(xs[:, :, :], sc[:, :, :], b4(s4[:, :]), ALU.subtract).then_inc(v_x, 1)
                    link(dve.tensor_scalar(U0[:, :, :], U0[:, :, :], 1.5, None, ALU.is_lt))
                    dve.wait_ge(a_x, k * 3 + 3)
                    link(dve.tensor_tensor(U1[:, :, :], es[:, :, :], U0[:, :, :], ALU.mult))
                    link(dve.tensor_reduce(s4[:, :], U1[:, :, :], AX.X, ALU.add))
                    link(dve.reciprocal(s4[:, :], s4[:, :]))
                    dve.tensor_tensor(G[:, par, :, :].rearrange("p e t -> p t e"), U1[:, :, :], b4(s4[:, :]), ALU.mult).then_inc(v_g, 1)
                    assert cnt[0] == NL, cnt
                    dve.wait_ge(v_g, k + 1)
                    dve.sem_inc(slot_free, 1)


def experts(nc, n, W1, b1, W2, b2):
    B, C, NP, NX, HID = n.B, n.C, n.NP, n.NX, n.HID
    CW = 384
    NCH = NP // CW
    with ExitStack() as ctx:
        def sb(name, shape, dt=F32):
            return ctx.enter_context(nc.sbuf_tensor(name, shape, dt))

        def pb(name):
            return ctx.enter_context(nc.psum_tensor(name, [P, 512], F32))

        def sem(name):
            return ctx.enter_context(nc.semaphore(name))
        w1 = sb("w1", [C, NX, HID])
        w2 = sb("w2", [HID, NX, C])
        b1r = sb("b1r", [NX, HID])
        b1t = sb("b1t", [HID, NX])
        b2r = sb("b2r", [NX, C])
        pick = sb("pick", [NX, NX, HID])
        tn = sb("tne", [C, 2, NP])
        x2 = sb("x2e", [C, 2, NP])
        g = sb("ge", [NX, 2, NP])
        hid = sb("hid", [HID, 3, CW])
        hg = sb("hg", [HID, 3, CW])
        res = sb("res", [C, 2, NP])
        up = [pb(f"up{i}") for i in range(3)]
        gb = [pb(f"gb{i}") for i in range(3)]
        acc = [pb("eacc0"), pb("eacc1")]
        w_in = sem("ew_in")
        pk = sem("pk")
        pe_b = sem("pe_b")
        v_b = sem("v_b")
        in_ = [sem("e_in0"), sem("e_in1")]
        pe_up = sem("pe_up")
        a_hid = sem("a_hid")
        v_hg = sem("v_hg")
        pe_dn = sem("pe_dn")
        v_res = sem("v_res")
        free = sem("efree")
        passed = sem("epassed")
        r_out = [sem("r_out0"), sem("r_out1")]
        block = ctx.enter_context(nc.Block())
        STEPS = NCH * NX

        @block.sync
        def _(sp):
            sp.dma_start(w1[:, :, :], W1.rearrange("e c h -> c e h")).then_inc(w_in, 16)
            sp.dma_start(w2[:, :, :], W2.rearrange("e h c -> h e c")).then_inc(w_in, 16)
            sp.dma_start(b1r[:, :], b1).then_inc(w_in, 16)
            sp.dma_start(b2r[:, :], b2).then_inc(w_in, 16)
            with sp.Fori(0, B // 2) as ii:
                for par in range(2):
                    b = ii * 2 + par
                    sp.wait_ge(free, b + 1)
                    one = lambda t: t[bass.ds(b, 1), :, :].rearrange("a c p -> (a c) p")
                    sp.dma_start(tn[:, par, :], one(n.tn)).then_inc(in_[par], 16)
                    sp.dma_start(x2[:, par, :], one(n.x2)).then_inc(in_[par], 16)
                    sp.dma_start(g[:, par, :], n.gates[:, bass.ds(b * NP, NP)]).then_inc(in_[par], 16)

        @block.gpsimd
        def _(pool):
            pool.memset(pick[:, :, :], 0.0).then_inc(pk, 1)
            pool.wait_ge(pk, 1)
            pool.affine_select(out=pick[:, :, :], in_=pick[:, :, :], compare_op=ALU.not_equal, fill=1.0, base=0,
                               pattern=[[-1, NX], [0, HID]], channel_multiplier=1).then_inc(pk, 1)
            with pool.Fori(0, B // 2) as ii:
                for par in range(2):
                    pool.wait_ge(v_res, (ii * 2 + par + 1) * NCH)
                    pool.sem_inc(passed, 1)
                    pool.dma_start(n.of[bass.ds(ii * 2 + par, 1), :, :].rearrange("a c p -> (a c) p"), res[:, par, :]).then_inc(r_out[par], 16)
            for par in range(2):
                pool.wait_ge(r_out[par], 16 * (B // 2))

        @block.tensor
        def _(pe):
            pe.wait_ge(w_in, 64)
            pe.wait_ge(pk, 2)
            pe.transpose(up[0][0:HID, 0:NX], b1r[:, :], n.ident[0:NX, 0:NX]).then_inc(pe_b, 1)
            pe.wait_ge(v_b, 1)
            LAG = 2
            with pe.Fori(0, B // 2) as ii:
                for par in range(2):
                    b = ii * 2 + par
                    pe.wait_ge(in_[par], (ii + 1) * 48)
                    for t in range(STEPS + LAG):
                        if t < STEPS:
                            c, e = divmod(t, NX)
                            if t >= 3:
                                pe.wait_ge(v_hg, b * STEPS + t - 2)
                            elif t < 3:
                                pe.wait_ge(v_hg, b * STEPS)
                            pe.matmul(up[t % 3][:, 0:CW], w1[:, e, :], tn[:, par, c * CW:(c + 1) * CW], start=True, stop=True)
                            pe.matmul(gb[t % 3][:, 0:CW], pick[:, e, :], g[:, par, c * CW:(c + 1) * CW], start=True, stop=True).then_inc(pe_up, 1)
                        u = t - LAG
                        if u >= 0:
                            c, e = divmod(u, NX)
                            if e == 0 and c >= 2:
                                pe.wait_ge(v_res, b * NCH + c - 1)
                            elif e == 0:
                                pe.wait_ge(v_res, b * NCH)
                            if e == 0:
                                pe.matmul(acc[c % 2][0:C, 0:CW], b2r[:, :], g[:, par, c * CW:(c + 1) * CW], start=True, stop=False)
                            pe.wait_ge(v_hg, b * STEPS + u + 1)
                            pe.matmul(acc[c % 2][0:C, 0:CW], w2[:, e, :], hg[:, u % 3, :], start=False, stop=e == NX - 1).then_inc(pe_dn, 1)

        @block.scalar
        def _(act):
            act.wait_ge(v_b, 1)
            with act.Fori(0, B // 2) as ii:
                for par in range(2):
                    b = ii * 2 + par
                    for t in range(STEPS):
                        act.wait_ge(pe_up, b * STEPS + t + 1)
                        if t >= 3:
                            act.wait_ge(v_hg, b * STEPS + t - 2)
                        act.activation(hid[:, t % 3, :], up[t % 3][:, 0:CW], ACT.Gelu, bias=b1t[:, t % NX:t % NX + 1]).then_inc(a_hid, 1)

        @block.vector
        def _(dve):
            dve.wait_ge(pe_b, 1)
            dve.tensor_copy(b1t[:, :], up[0][0:HID, 0:NX]).then_inc(v_b, 1)
            dve.sem_inc(free, 2)
            with dve.Fori(0, B // 2) as ii:
                for par in range(2):
                    b = ii * 2 + par
                    dve.wait_ge(r_out[par], ii * 16)
                    for t in range(STEPS):
                        c, e = divmod(t, NX)
                        dve.wait_ge(a_hid, b * STEPS + t + 1)
                        if t >= 3:
                            dve.wait_ge(pe_dn, b * STEPS + t - 2)
                        else:
                            dve.wait_ge(pe_dn, b * STEPS)
                        dve.tensor_tensor(hg[:, t % 3, :], gb[t % 3][:, 0:CW], hid[:, t % 3, :], ALU.mult).then_inc(v_hg, 1)
                        if e == 1 and c or t == STEPS - 1:
                            for cc in ([c - 1] if e == 1 else []) + ([c] if t == STEPS - 1 else []):
                                dve.wait_ge(pe_dn, b * STEPS + (cc + 1) * NX)
                                last = dve.tensor_tensor(res[:, par, cc * CW:(cc + 1) * CW], acc[cc % 2][0:C, 0:CW],
                                                         x2[:, par, cc * CW:(cc + 1) * CW], ALU.add)
                                last.then_inc(v_res, 1)
                    dve.wait_ge(v_res, (b + 1) * NCH)
                    dve.sem_inc(free, 1)


_INS = ["x", "L0_conv_Wc", "L0_conv_bc", "L0_ffn_W_gat", "L0_ffn_att_src", "L0_ffn_att_dst", "L0_ffn_b_gat", "L0_ffn_ln_gamma",
        "L0_ffn_ln_beta", "L0_ffn_W1", "L0_ffn_b1", "L0_ffn_W2", "L0_ffn_b2", "L0_ffn_edge_index"]


def kernel(**inputs):
    import concourse.bacc as bacc
    from concourse.bass_utils import run_bass_kernel_spmd

    nc = bacc.Bacc("TRN2", target_bir_lowering=False, num_devices=1)
    arrays = {f"in_{name}": np.ascontiguousarray(inputs[name]) for name in _INS}
    args = [nc.dram_tensor(k, a.shape, mybir.dt.from_np(a.dtype), kind="ExternalInput").ap() for k, a in arrays.items()]
    out = nc.dram_tensor("out_0", inputs["x"].shape, F32, kind="ExternalOutput").ap()
    kernel_program(nc, *args, out)
    return run_bass_kernel_spmd(nc, [arrays], core_ids=[0]).results[0]["out_0"]
```

```python
from contextlib import ExitStack
import numpy as np
import concourse.bass as bass
import concourse.mybir as mybir

F32 = mybir.dt.float32
F16 = mybir.dt.float16
BF16 = mybir.dt.bfloat16
I32 = mybir.dt.int32
ALU = mybir.AluOpType
ACT = mybir.ActivationFunctionType
AX = mybir.AxisListType

P = 128
NEG = -1.0e30
SPLIT = 64.0
GSPLIT = 4096.0
FAR = 1.0e6


def chunks(n, size=512):
    return [(o, min(size, n - o)) for o in range(0, n, size)]


class Net:
    pass


def kernel_program(nc, x, Wc, bc, Wg, att_s, att_d, b_gat, gamma, beta, W1, b1, W2, b2, edges, out):
    B, C, H, W = x.shape
    NP = H * W
    M = B * NP
    E = edges.shape[1]
    HE = Wg.shape[1]
    NH, NX = att_s.shape
    HID = W1.shape[2]
    EC = E // P
    NT = M // P
    n = Net()
    n.B, n.C, n.NP, n.M, n.E, n.HE, n.NH, n.NX, n.HID, n.EC, n.NT = B, C, NP, M, E, HE, NH, NX, HID, EC, NT
    n.ROW = HE + 2 * NH
    n.x2 = nc.dram_tensor("x2_d", (B, C, NP), F32).ap()
    n.tn = nc.dram_tensor("tn_d", (B, 2 * C, NP), F16).ap()
    n.htab = nc.dram_tensor("htab_d", (M, HE), F32).ap()
    n.adtab = nc.dram_tensor("adtab_d", (M, NH), F32).ap()
    n.pos = nc.dram_tensor("pos_d", (M, 1), I32).ap()
    n.seg = nc.dram_tensor("seg_d", (E + 1, n.ROW), F32).ap()
    n.row = nc.dram_tensor("row_d", (P, 5 * (HE + NH)), F32).ap()
    n.gates = nc.dram_tensor("gates_d", (2 * NX, M), F16).ap()
    n.xf = x.rearrange("b c h w -> b c (h w)")
    n.of = out.rearrange("b c h w -> b c (h w)")
    with ExitStack() as ctx:
        def sb(name, shape, dt=F32):
            return ctx.enter_context(nc.sbuf_tensor(name, shape, dt))
        n.dsti = sb("dsti", [P, EC], I32)
        n.srci = sb("srci", [P, EC], I32)
        n.start = sb("start", [P, EC])
        n.single = sb("single", [P, 4])
        n.ident = sb("ident", [P, P])
        images_and_sort(nc, n, Wc, bc, Wg, att_s, att_d, edges)
        segments(nc, n, att_s)
        gates(nc, n, att_s, att_d, b_gat, gamma, beta)
        experts(nc, n, W1, b1, W2, b2)


def images_and_sort(nc, n, Wc, bc, Wg, att_s, att_d, edges):
    B, C, NP, HE, NH, NX, EC, M = n.B, n.C, n.NP, n.HE, n.NH, n.NX, n.EC, n.M
    QT = NP // P
    CH = chunks(NP)
    NCH = len(CH)
    STEPS = NCH * QT
    LOG = int(np.log2(n.E))
    LC = int(np.log2(EC))
    with ExitStack() as ctx:
        def sb(name, shape, dt=F32):
            return ctx.enter_context(nc.sbuf_tensor(name, shape, dt))

        def pb(name):
            return ctx.enter_context(nc.psum_tensor(name, [P, 512], F32))

        def sem(name):
            return ctx.enter_context(nc.semaphore(name))
        xb = sb("xb", [P, 2, NP])
        cen = sb("cen", [P, 512])
        sq = sb("sq", [P, 512])
        sd = sb("sd", [P, 512])
        rstd = sb("rstd", [P, 512])
        r2 = sb("r2", [P, 512])
        n2 = sb("n2", [P, 512])
        nrm = sb("nrm", [P, 512])
        xn = sb("xn", [P, 512])
        xl = sb("xl", [P, NP])
        hl = sb("hl", [P, 2, NP], F16)
        lh = sb("lh", [P, 2, NP], F16)
        gT = sb("gT", [P, QT, C])
        rel = sb("rel", [P, 4, 512])
        s2 = sb("s2", [P, 4, 512])
        half = sb("half", [C, 512])
        x2 = sb("x2", [P, NP])
        tf = sb("tf", [P, NP])
        th = sb("th", [P, NP], F16)
        hx = sb("hx", [P, QT, HE + NH])
        centre = sb("centre", [P, 2, C])
        mean = sb("mean", [P, 2, C])
        wcl = sb("wcl", [C, C])
        wcT = sb("wcT", [P, C])
        bcb = sb("bcb", [P, C])
        wgx = sb("wgx", [P, HE + NH])
        adb = sb("adb", [C, HE])
        wad = sb("wad", [C, HE])
        epsc = sb("epsc", [P, 2])
        KV = sb("KV", [P, 2, EC])
        PV = sb("PV", [P, 2, EC])
        DF = sb("DF", [P, 2, EC])
        MK = sb("MK", [P, EC])
        KK = sb("KK", [P, EC + 2])
        bits = sb("bits", [P, 8])
        sx = sb("sx", [P, 64])
        ei = PV[:, :, :].bitcast(I32)
        endi = ei[:, 0, :]
        posv = ei[:, 1, :]
        zero = KK[:, 0:M // P].bitcast(I32)
        gram = [pb(f"gram{i}") for i in range(4)]
        acc = [pb("acc0"), pb("acc1")]
        lnp = [pb("lnp0"), pb("lnp1")]
        w_in = sem("w_in")
        x_in = [sem("x_in0"), sem("x_in1")]
        xb_free = sem("xb_free")
        const_ready = sem("const_ready")
        wct_ps = sem("wct_ps")
        w_ready = sem("w_ready")
        pe_cen = sem("pe_cen")
        a_sq = sem("a_sq")
        pe_var = sem("pe_var")
        a_sd = sem("a_sd")
        v_n2 = sem("v_n2")
        a_nrm = sem("a_nrm")
        v_ln = sem("v_ln")
        v_r = sem("v_r")
        pe_gt = sem("pe_gt")
        v_gt = sem("v_gt")
        pe_gram = sem("pe_gram")
        a_rel = sem("a_rel")
        v_s2 = sem("v_s2")
        pe_acc = sem("pe_acc")
        v_x2 = sem("v_x2")
        pe_h = sem("pe_h")
        v_h = sem("v_h")
        o_x2 = sem("o_x2")
        left = sem("left")
        v_hi = sem("v_hi")
        v_th = sem("v_th")
        vc = sem("vc")
        e_in = sem("e_in")
        pc = sem("pc")
        kv_out = sem("kv_out")
        pv_in = sem("pv_in")
        z_out = sem("z_out")
        sc_out = [sem("sc_out0"), sem("sc_out1")]
        st = sem("st")
        passed = sem("passed")
        SW = min(64, EC // 2)
        stage = sb("stage", [P, 2, 2, SW], I32)
        block = ctx.enter_context(nc.Block())
        GB = (QT * C + 511) // 512
        GPB = 512 // C
        HPB = 512 // (HE + NH)
        NHB = -(-QT // HPB)
        NLN = 2 * NCH
        stages = [(L, d) for L in range(1, LOG + 1) for d in [1 << t for t in range(L - 1, -1, -1)]]

        def swaps(pd):
            if 2 * pd <= P // pd:
                got = []
                for r in range(pd):
                    a, b = slice(r, P, 2 * pd), slice(r + pd, P, 2 * pd)
                    got += [(a, b), (b, a)]
                return got
            got = []
            for g in range(0, P, 2 * pd):
                a, b = slice(g, g + pd), slice(g + pd, g + 2 * pd)
                got += [(a, b), (b, a)]
            return got

        @block.sync
        def _(sp):
            sp.dma_start(ei, edges.rearrange("a (p j) -> p a j", p=P)).then_inc(e_in, 16)
            sp.dma_start(wcl[:, :], Wc).then_inc(w_in, 16)
            sp.dma_start(bcb[:, :], bc.rearrange("(a c) -> a c", a=1).to_broadcast((P, C))).then_inc(w_in, 16)
            sp.dma_start(wgx[0:C, 0:HE], Wg).then_inc(w_in, 16)
            sp.dma_start(adb[:, :], att_d.rearrange("(a h) e -> a (h e)", a=1).to_broadcast((C, HE))).then_inc(w_in, 16)
            sp.wait_ge(z_out, 1)
            sp.dma_start(n.pos.rearrange("(p t) a -> p (t a)", p=P), zero).then_inc(z_out, 16)
            served = 0
            for L, d in stages:
                if d >= EC:
                    served += 1
                    sp.wait_ge(kv_out, served)
                    for a, b in swaps(d // EC):
                        sp.dma_start(PV[b, :, :], KV[a, :, :]).then_inc(pv_in, 16)
            sp.wait_ge(kv_out, served + 1)
            sp.dma_start(KK[1:P, 0:1], KV[0:P - 1, 0, EC - 1:EC]).then_inc(pv_in, 16)
            sp.dma_start(KK[0:P - 1, EC + 1:EC + 2], KV[1:P, 0, 0:1]).then_inc(pv_in, 16)

        @block.gpsimd
        def _(pool):
            done = [0]

            def step(ins):
                done[0] += 1
                ins.then_inc(pc, 1)
                pool.wait_ge(pc, done[0])
            step(pool.memset(n.ident[:, :], 0.0))
            step(pool.affine_select(out=n.ident[:, :], in_=n.ident[:, :], compare_op=ALU.not_equal, fill=1.0, base=0,
                                    pattern=[[-1, P]], channel_multiplier=1))
            step(pool.memset(mean[0:C, :, :], 1.0 / C))
            step(pool.memset(mean[C:P, :, :], 0.0))
            step(pool.memset(centre[C:P, :, :], 0.0))
            step(pool.memset(wcT[C:P, :], 0.0))
            step(pool.memset(wgx[C:P, :], 0.0))
            step(pool.memset(x2[C:P, :], 0.0))
            pool.tensor_tensor(centre[0:C, :, :], n.ident[0:C, 0:C].unsqueeze(1).to_broadcast([C, 2, C]), mean[0:C, :, :],
                               ALU.subtract).then_inc(const_ready, 1)
            pool.memset(epsc[:, 0:1], 1e-6).then_inc(const_ready, 1)
            pool.memset(epsc[:, 1:2], 1e-5).then_inc(const_ready, 1)
            pool.memset(zero, 0).then_inc(z_out, 1)
            for b in range(8):
                w = 1 << b
                v = MK[:, 0:P].rearrange("p (g two run) -> p g two run", two=2, run=w) if w < P else None
                step(pool.memset(MK[:, 0:P], 1.0))
                if v is not None:
                    step(pool.memset(v[:, :, 1, :], -1.0))
                step(pool.tensor_tensor(DF[:, 0, 0:P], MK[:, 0:P], n.ident[:, :], ALU.mult))
                step(pool.tensor_tensor(DF[:, 1, 0:64], DF[:, 0, 0:64], DF[:, 0, 64:128], ALU.add))
                w2 = 32
                while w2:
                    step(pool.tensor_tensor(DF[:, 1, 0:w2], DF[:, 1, 0:w2], DF[:, 1, w2:2 * w2], ALU.add))
                    w2 //= 2
                step(pool.tensor_copy(bits[:, b:b + 1], DF[:, 1, 0:1]))
            for b in range(8):
                step(pool.tensor_scalar(sx[:, 8 * b:8 * b + 8], bits[:, :], bits[:, b:b + 1], None, ALU.mult))
            pool.wait_ge(e_in, 16)
            step(pool.tensor_copy(KV[:, 0, :], ei[:, 1, :]))
            step(pool.tensor_copy(KV[:, 1, :], ei[:, 0, :]))
            served = arrived = 0
            for L, d in stages:
                if d >= EC:
                    served += 1
                    pool.sem_inc(kv_out, 1)
                    arrived += 16 * len(swaps(d // EC))
                    pool.wait_ge(pv_in, arrived)
                    col = 8 * (L - LC) + int(np.log2(d // EC))
                    step(pool.tensor_tensor(DF[:, :, :], PV[:, :, :], KV[:, :, :], ALU.subtract))
                    step(pool.tensor_scalar(MK[:, :], DF[:, 0, :], sx[:, col:col + 1], 0.0, ALU.mult, ALU.is_lt))
                    step(pool.tensor_tensor(DF[:, :, :], DF[:, :, :], MK[:, :].unsqueeze(1).to_broadcast([P, 2, EC]), ALU.mult))
                    step(pool.tensor_tensor(KV[:, :, :], KV[:, :, :], DF[:, :, :], ALU.add))
                    continue
                pair = KV[:, :, :].rearrange("p a (g two run) -> p a g two run", two=2, run=d)
                lo, hi = pair[:, :, :, 0, :], pair[:, :, :, 1, :]
                HC = EC // 2
                df = DF[:, :, 0:HC]
                dv = df.rearrange("p a (g run) -> p a g run", run=d)
                step(pool.tensor_tensor(dv, hi, lo, ALU.subtract))
                if L < LC:
                    t = DF[:, 0, 0:HC].rearrange("p (g two run) -> p g two run", two=2, run=1 << (L - 1))
                    u = MK[:, 0:HC].rearrange("p (g two run) -> p g two run", two=2, run=1 << (L - 1))
                    pool.tensor_scalar(u[:, :, 0, :], t[:, :, 0, :], 0.0, None, ALU.is_lt)
                    step(pool.tensor_scalar(u[:, :, 1, :], t[:, :, 1, :], 0.0, None, ALU.is_gt))
                else:
                    b = L - LC
                    step(pool.tensor_scalar(MK[:, 0:HC], DF[:, 0, 0:HC], bits[:, b:b + 1], 0.0, ALU.mult, ALU.is_lt))
                step(pool.tensor_tensor(df, df, MK[:, 0:HC].unsqueeze(1).to_broadcast([P, 2, HC]), ALU.mult))
                pool.tensor_tensor(lo, lo, dv, ALU.add)
                step(pool.tensor_tensor(hi, hi, dv, ALU.subtract))
            pool.wait_ge(z_out, 17)
            step(pool.memset(KK[:, :], -1.0))
            step(pool.tensor_copy(KK[:, 1:EC + 1], KV[:, 0, :]))
            pool.sem_inc(kv_out, 1)
            step(pool.tensor_copy(n.dsti[:, :], KV[:, 0, :]))
            step(pool.tensor_copy(n.srci[:, :], KV[:, 1, :]))
            pool.wait_ge(pv_in, arrived + 32)
            step(pool.tensor_tensor(n.start[:, :], KK[:, 0:EC], KK[:, 1:EC + 1], ALU.subtract))
            step(pool.tensor_scalar(n.start[:, :], n.start[:, :], 0.0, None, ALU.is_equal))
            step(pool.tensor_scalar(n.start[:, :], n.start[:, :], -1.0, -NEG, ALU.add, ALU.mult))
            step(pool.tensor_tensor(DF[:, 0, :], KK[:, 1:EC + 1], KK[:, 2:EC + 2], ALU.subtract))
            step(pool.tensor_scalar(DF[:, 0, :], DF[:, 0, :], 0.0, None, ALU.is_equal))
            step(pool.tensor_scalar(DF[:, 1, :], DF[:, 0, :], FAR, None, ALU.mult))
            step(pool.tensor_tensor(DF[:, 1, :], DF[:, 1, :], KK[:, 1:EC + 1], ALU.add))
            step(pool.tensor_copy(endi, DF[:, 1, :]))
            step(pool.iota(posv, pattern=[[1, EC]], base=1, channel_multiplier=EC))
            step(pool.tensor_copy(DF[:, 1, :], posv))
            step(pool.tensor_scalar(DF[:, 0, :], DF[:, 0, :], FAR, None, ALU.mult))
            step(pool.tensor_tensor(DF[:, 1, :], DF[:, 1, :], DF[:, 0, :], ALU.add))
            pool.sem_inc(kv_out, 1)
            with pool.Fori(0, EC // (2 * SW)) as it:
                for par in range(2):
                    k = it * 2 + par
                    pool.wait_ge(sc_out[par], it * 16 * SW)
                    pool.sem_inc(passed, 1)
                    pool.tensor_copy(stage[:, par, 0, :], endi[:, bass.ds(k * SW, SW)]).then_inc(st, 1)
                    pool.tensor_copy(stage[:, par, 1, :], posv[:, bass.ds(k * SW, SW)]).then_inc(st, 1)
                    pool.wait_ge(st, k * 2 + 2)
                    pool.sem_inc(passed, 1)
                    for j in range(SW):
                        pool.indirect_dma_start(out=n.pos, out_offset=bass.IndirectOffsetOnAxis(ap=stage[:, par, 0, j:j + 1], axis=0),
                                                in_=stage[:, par, 1, j:j + 1], in_offset=None, bounds_check=M - 1,
                                                oob_is_err=False).then_inc(sc_out[par], 16)
            for par in range(2):
                pool.wait_ge(sc_out[par], 16 * EC // 2)

        PRE = NCH
        ATQ = QT // 6

        def ln_at(b, c, post):
            return PRE + b * NLN + 2 * c + post

        def sums(dve, b, ii, par, c, link):
            o, w = CH[c]
            if c == 0:
                if par:
                    dve.wait_ge(o_x2, ii * 128 + 64)
                else:
                    dve.wait_ge(left, ii + 1)
            dve.wait_ge(pe_acc, b * STEPS + (c + 1) * QT)
            link(dve.tensor_tensor(half[:, 0:w], acc[c % 2][0:C, 0:w], xb[0:C, par, o:o + w], ALU.add))
            dve.tensor_tensor(x2[0:C, o:o + w], acc[c % 2][C:2 * C, 0:w], half[:, 0:w], ALU.add).then_inc(v_x2, 1)

        @block.tensor
        def _(pe):
            pe.wait_ge(const_ready, 3)
            pe.wait_ge(w_in, 64)
            pe.transpose(lnp[0][0:C, 0:C], wcl[:, :], n.ident[0:C, 0:C]).then_inc(wct_ps, 1)
            pe.wait_ge(w_ready, 2)

            def centring(k, src, c):
                o, w = CH[c]
                if not isinstance(k, int) or k:
                    pe.wait_ge(v_ln, k)
                pe.matmul(lnp[0][:, 0:w], centre[:, :, :].rearrange("p a c -> p (a c)"), src[:, o:o + w],
                          start=True, stop=True).then_inc(pe_cen, 1)

            def variance(k, c):
                w = CH[c][1]
                pe.wait_ge(a_sq, k + 1)
                pe.matmul(lnp[1][:, 0:w], mean[:, :, :].rearrange("p a c -> p (a c)"), sq[:, 0:w],
                          start=True, stop=True).then_inc(pe_var, 1)

            def values(b):
                for gb in range(GB):
                    if gb:
                        pe.wait_ge(v_gt, b * GB + gb)
                    for k in range(min(GPB, QT - gb * GPB)):
                        q = gb * GPB + k
                        last = pe.matmul(lnp[0][:, k * C:(k + 1) * C], xl[:, q * P:(q + 1) * P], wcT[:, :], start=True, stop=True)
                    last.then_inc(pe_gt, 1)
            pe.wait_ge(x_in[0], 32)
            for c in range(NCH):
                centring(c, xb[:, 0, :], c)
                variance(c, c)
            pe.wait_ge(v_ln, NCH)
            values(0)
            with pe.Fori(0, B // 2) as ii:
                for par in range(2):
                    b = ii * 2 + par
                    pe.wait_ge(x_in[1 - par], (ii + 1 + par) * 32)
                    pe.wait_ge(v_gt, (b + 1) * GB)
                    for c in range(NCH):
                        o, w = CH[c]
                        for q in range(0, QT + 2, 2):
                            if q < QT:
                                for k in (q, q + 1):
                                    t = c * QT + k
                                    if t >= 4:
                                        pe.wait_ge(a_rel, b * STEPS + t - 3)
                                    pe.matmul(gram[t % 4][:, 0:w], hl[:, par, k * P:(k + 1) * P], hl[:, par, o:o + w], start=True, stop=False)
                                    pe.matmul(gram[t % 4][:, 0:w], lh[:, par, k * P:(k + 1) * P], hl[:, par, o:o + w],
                                              start=False, stop=True).then_inc(pe_gram, 1)
                            if q >= 2:
                                u = c * QT + q - 2
                                pe.wait_ge(v_s2, b * STEPS + u + 2)
                                if c >= 2 and q == 2:
                                    pe.wait_ge(v_x2, b * NCH + c - 1)
                                for k in (q - 2, q - 1):
                                    h = C * (k % 2)
                                    pe.matmul(acc[c % 2][h:h + C, 0:w], gT[:, k, :], s2[:, (c * QT + k) % 4, 0:w], start=k < 2,
                                              stop=k >= QT - 2).then_inc(pe_acc, 1)
                            if q == 4 and c:
                                pe.wait_ge(v_x2, b * NCH + c)
                                centring(ln_at(b, c - 1, 1), x2, c - 1)
                            if q == 6 and c:
                                variance(ln_at(b, c - 1, 1), c - 1)
                            if q == 12:
                                centring(ln_at(b, c, 0), xb[:, 1 - par, :], c)
                            if q == 14:
                                variance(ln_at(b, c, 0), c)
                    k = ln_at(b, NCH - 1, 1)
                    pe.wait_ge(v_x2, (b + 1) * NCH)
                    centring(k, x2, NCH - 1)
                    variance(k, NCH - 1)
                    pe.wait_ge(v_ln, k + 1)
                    values(b + 1)
                    for hb in range(NHB):
                        if hb:
                            pe.wait_ge(v_h, b * NHB + hb)
                        for j in range(min(HPB, QT - hb * HPB)):
                            q = hb * HPB + j
                            last = pe.matmul(lnp[1][:, j * (HE + NH):(j + 1) * (HE + NH)], tf[:, q * P:(q + 1) * P],
                                             wgx[:, :], start=True, stop=True)
                        last.then_inc(pe_h, 1)

        @block.scalar
        def _(act):
            def load(img, par):
                for h in (0, C):
                    act.dma_start(xb[h:h + C, par, :], img).then_inc(x_in[par], 16)
            load(n.xf[0], 0)
            load(n.xf[1], 1)
            act.wait_ge(const_ready, 3)

            def centred(k, c):
                w = CH[c][1]
                act.wait_ge(pe_cen, k + 1)
                act.activation(cen[:, 0:w], lnp[0][:, 0:w], ACT.Copy)
                act.activation(sq[:, 0:w], lnp[0][:, 0:w], ACT.Square).then_inc(a_sq, 1)

            def deviation(k, c, eps):
                w = CH[c][1]
                act.wait_ge(pe_var, k + 1)
                act.activation(sd[:, 0:w], lnp[1][:, 0:w], ACT.Sqrt, bias=epsc[:, eps:eps + 1]).then_inc(a_sd, 1)

            def norm(k, c):
                w = CH[c][1]
                act.wait_ge(v_n2, k + 1)
                act.activation(nrm[:, 0:w], n2[:, 0:w], ACT.Sqrt).then_inc(a_nrm, 1)
            for c in range(NCH):
                centred(c, c)
                deviation(c, c, 0)
                norm(c, c)
            with act.Fori(0, B // 2) as ii:
                for par in range(2):
                    b = ii * 2 + par
                    for c in range(NCH):
                        w = CH[c][1]
                        for q in range(QT):
                            t = c * QT + q
                            act.wait_ge(pe_gram, b * STEPS + t + 1)
                            if t >= 4:
                                act.wait_ge(v_s2, b * STEPS + t - 3)
                            act.activation(rel[:, t % 4, 0:w], gram[t % 4][:, 0:w], ACT.Relu, scale=1.0 / SPLIT ** 2).then_inc(a_rel, 1)
                            if q == 4 and c:
                                centred(ln_at(b, c - 1, 1), c - 1)
                            if q == 7 and c:
                                deviation(ln_at(b, c - 1, 1), c - 1, 1)
                            if q == 12:
                                centred(ln_at(b, c, 0), c)
                            if q == 15:
                                deviation(ln_at(b, c, 0), c, 0)
                            if q == 17:
                                norm(PRE + b * NCH + c, c)
                    centred(ln_at(b, NCH - 1, 1), NCH - 1)
                    deviation(ln_at(b, NCH - 1, 1), NCH - 1, 1)
                    act.wait_ge(v_ln, PRE + (b + 1) * NLN)
                    act.dma_start(n.x2[bass.ds(b, 1), :, :].rearrange("a c p -> (a c) p"), x2[0:C, :]).then_inc(o_x2, 16)
                    act.dma_start(n.tn[bass.ds(b, 1), :, :].rearrange("a c p -> (a c) p"), th[:, :]).then_inc(o_x2, 16)
                    act.wait_ge(v_h, (b + 1) * NHB)
                    act.dma_start(n.htab[bass.ds(b * NP, NP), :].rearrange("(q p) c -> p q c", p=P), hx[:, :, 0:HE]).then_inc(o_x2, 16)
                    act.dma_start(n.adtab[bass.ds(b * NP, NP), :].rearrange("(q p) c -> p q c", p=P), hx[:, :, HE:HE + NH]).then_inc(o_x2, 16)
                    nb = ii * 2 + par + 2
                    load(n.xf[bass.ds(nb % B, 1), :, :].rearrange("a c p -> (a c) p"), par)
                act.wait_ge(o_x2, 128 * (ii + 1))
                act.sem_inc(left, 1)
            act.wait_ge(x_in[0], 32 * (B // 2 + 1))
            act.wait_ge(x_in[1], 32 * (B // 2 + 1))

        @block.vector
        def _(dve):
            dve.sem_inc(left, 1)
            dve.wait_ge(w_in, 64)
            dve.wait_ge(wct_ps, 1)
            dve.wait_ge(const_ready, 3)
            dve.tensor_copy(wcT[0:C, :], lnp[0][0:C, 0:C]).then_inc(w_ready, 1)
            dve.tensor_tensor(wad[:, :], wgx[0:C, 0:HE], adb[:, :], ALU.mult).then_inc(vc, 1)
            dve.wait_ge(vc, 1)
            dve.tensor_reduce(wgx[0:C, HE:HE + NH], wad[:, :].rearrange("p (h e) -> p h e", e=NX), AX.X, ALU.add).then_inc(w_ready, 1)
            PRE_LINKS, POST_LINKS = 4, 2
            IMAGE_LINKS = NCH * (PRE_LINKS + POST_LINKS + 1)
            base = [1, 0]

            def link(ins):
                base[1] += 1
                ins.then_inc(vc, 1)
                dve.wait_ge(vc, base[0] + base[1])

            def pre_norm(k, c, slot):
                o, w = CH[c]
                dve.wait_ge(a_sd, k + 1)
                link(dve.reciprocal(rstd[:, 0:w], sd[:, 0:w]))
                dve.tensor_tensor(xl[:, o:o + w], cen[:, 0:w], rstd[:, 0:w], ALU.mult)
                link(dve.tensor_tensor(r2[:, 0:w], rstd[:, 0:w], rstd[:, 0:w], ALU.mult))
                link(dve.scalar_tensor_tensor(n2[:, 0:w], lnp[1][:, 0:w], float(C), r2[:, 0:w], ALU.mult, ALU.mult))
                dve.tensor_scalar(n2[:, 0:w], n2[:, 0:w], 1e-16, None, ALU.max).then_inc(v_n2, 1)

            def pre_unit(kn, c, slot):
                o, w = CH[c]
                dve.wait_ge(a_nrm, kn + 1)
                dve.reciprocal(r2[:, 0:w], nrm[:, 0:w]).then_inc(v_r, 1)
                dve.wait_ge(v_r, kn + 1)
                link(dve.tensor_tensor(xn[:, 0:w], xl[:, o:o + w], r2[:, 0:w], ALU.mult))
                dve.tensor_scalar(hl[0:C, slot, o:o + w], xn[0:C, 0:w], SPLIT, None, ALU.mult)
                dve.tensor_scalar(lh[C:P, slot, o:o + w], xn[C:P, 0:w], SPLIT, None, ALU.mult).then_inc(v_hi, 1)
                dve.wait_ge(v_hi, kn + 1)
                dve.scalar_tensor_tensor(lh[0:C, slot, o:o + w], xn[0:C, 0:w], SPLIT, hl[0:C, slot, o:o + w], ALU.mult, ALU.subtract)
                dve.scalar_tensor_tensor(hl[C:P, slot, o:o + w], xn[C:P, 0:w], SPLIT, lh[C:P, slot, o:o + w], ALU.mult,
                                         ALU.subtract).then_inc(v_ln, 1)

            def post(k, b, c):
                o, w = CH[c]
                dve.wait_ge(a_sd, k + 1)
                link(dve.reciprocal(rstd[:, 0:w], sd[:, 0:w]))
                link(dve.tensor_tensor(tf[:, o:o + w], cen[:, 0:w], rstd[:, 0:w], ALU.mult))
                dve.tensor_scalar(th[:, o:o + w], tf[:, o:o + w], SPLIT, None, ALU.mult).then_inc(v_th, 1)
                dve.wait_ge(v_th, b * NCH + c + 1)
                dve.scalar_tensor_tensor(th[C:P, o:o + w], tf[C:P, o:o + w], SPLIT, th[C:P, o:o + w], ALU.mult,
                                         ALU.subtract).then_inc(v_ln, 1)

            def values(b):
                for gb in range(GB):
                    k = min(GPB, QT - gb * GPB)
                    dve.wait_ge(pe_gt, b * GB + gb + 1)
                    dve.tensor_tensor(gT[:, gb * GPB:gb * GPB + k, :], lnp[0][:, 0:k * C].rearrange("p (k c) -> p k c", c=C),
                                      bcb[:, :].unsqueeze(1).to_broadcast([P, k, C]), ALU.add).then_inc(v_gt, 1)
            for c in range(NCH):
                pre_norm(c, c, 0)
                pre_unit(c, c, 0)
            values(0)
            base[0] += base[1]
            first = base[0]
            with dve.Fori(0, B // 2) as ii:
                for par in range(2):
                    b = ii * 2 + par
                    base[0], base[1] = b * IMAGE_LINKS + first, 0
                    for c in range(NCH):
                        w = CH[c][1]
                        for q in range(QT):
                            t = c * QT + q
                            dve.wait_ge(a_rel, b * STEPS + t + 1)
                            if t >= 4:
                                dve.wait_ge(pe_acc, b * STEPS + t - 3)
                            dve.tensor_tensor(s2[:, t % 4, 0:w], rel[:, t % 4, 0:w], rel[:, t % 4, 0:w], ALU.mult).then_inc(v_s2, 1)
                            if q == 3 and c:
                                sums(dve, b, ii, par, c - 1, link)
                            if q == 9 and c:
                                post(ln_at(b, c - 1, 1), b, c - 1)
                            if q == 16:
                                pre_norm(ln_at(b, c, 0), c, 1 - par)
                            if q == 17:
                                pre_unit(PRE + b * NCH + c, c, 1 - par)
                    sums(dve, b, ii, par, NCH - 1, link)
                    post(ln_at(b, NCH - 1, 1), b, NCH - 1)
                    values(b + 1)
                    for hb in range(NHB):
                        k = min(HPB, QT - hb * HPB)
                        dve.wait_ge(pe_h, b * NHB + hb + 1)
                        dve.tensor_copy(hx[:, hb * HPB:hb * HPB + k, :], lnp[1][:, 0:k * (HE + NH)].rearrange("p (k c) -> p k c", c=HE + NH)).then_inc(v_h, 1)
                    assert base[1] == IMAGE_LINKS, base
            dve.wait_ge(kv_out, 28 + 2 if LOG == 18 else len([1 for s in stages if s[1] >= EC]) + 2)
            dve.tensor_reduce(n.single[:, 0:1], n.start[:, 1:EC], AX.X, ALU.min)
            dve.tensor_copy(n.single[:, 1:2], n.start[:, 0:1])
            dve.tensor_reduce(n.single[:, 2:3], DF[:, 1, :], AX.X, ALU.min)


def segments(nc, n, att_s):
    HE, NH, NX, EC, M, ROW, E = n.HE, n.NH, n.NX, n.EC, n.M, n.ROW, n.E
    NC5 = NH * (NX + 1)
    CW = min(64, EC // 2)
    NK = EC // CW
    with ExitStack() as ctx:
        def sb(name, shape, dt=F32):
            return ctx.enter_context(nc.sbuf_tensor(name, shape, dt))

        def sem(name):
            return ctx.enter_context(nc.semaphore(name))
        rows = sb("rows", [P, 2, CW, ROW])
        idx = sb("idx", [P, 2, 2, CW], I32)
        attb = sb("attb", [P, HE])
        stc = sb("stc", [P, CW])
        prod = sb("prod", [P, CW, HE])
        asr = sb("asr", [P, CW, NH])
        ee = sb("ee", [P, CW, NH])
        D0 = sb("D0", [P, NH, CW + 1])
        D1 = sb("D1", [P, NH, CW + 1])
        MF = sb("MF", [P, NH, CW + 1])
        X = sb("X", [P, 2, NH, CW])
        FX = sb("FX", [P, 2, NH, CW])
        G0 = sb("G0", [P, NH, NX + 1, CW + 1])
        G1 = sb("G1", [P, NH, NX + 1, CW + 1])
        S = sb("S", [P, NH, NX + 1, CW + 1])
        empty = sb("empty", [1, ROW])
        tails = sb("tails", [P, 3, NC5])
        rt = sb("rt", [NC5, 3, P])
        Mo = sb("Mo", [NC5, P + 1])
        ex = sb("ex", [NC5, 2, P])
        ea = sb("ea", [NC5, 2, P])
        So = sb("So", [NC5, P + 1])
        carry = sb("carry", [P, 2, NC5])
        fidx = sb("fidx", [P, 2])
        fi = sb("fi", [P, 2], I32)
        fix = sb("fix", [P, ROW])
        fixo = sb("fixo", [P, ROW])
        mm = sb("mm", [P, 3, NH])
        me = sb("me", [P, 2, NH])
        part = sb("part", [P, 2, NC5])
        a_in = sem("a_in")
        slot_free = sem("slot_free")
        ist = sem("ist")
        passed = sem("spassed")
        rows_in = [sem("rows_in0"), sem("rows_in1")]
        vq = sem("vq")
        v_x = sem("v_x")
        a_x = sem("a_x")
        v_rows = sem("v_rows")
        rows_out = sem("rows_out")
        e_out = sem("e_out")
        v_tails = sem("v_tails")
        bounce = sem("bounce")
        v_car = sem("v_car")
        v_fi = sem("v_fi")
        fix_in = sem("fix_in")
        v_fixo = sem("v_fixo")
        fix_out = sem("fix_out")
        block = ctx.enter_context(nc.Block())
        segv = n.seg[1:1 + E, :].rearrange("(p j) c -> p j c", p=P)
        rowt = n.row[:, 0:3 * NC5]
        rowc = n.row[:, 3 * NC5:5 * NC5]

        @block.sync
        def _(sp):
            sp.dma_start(attb[:, :], att_s.rearrange("(a h) e -> a (h e)", a=1).to_broadcast((P, HE))).then_inc(a_in, 16)
            sp.wait_ge(e_out, 1)
            sp.dma_start(n.seg[0:1, :], empty[:, :]).then_inc(e_out, 16)
            with sp.Fori(0, NK // 2) as it:
                for par in range(2):
                    k = it * 2 + par
                    sp.wait_ge(v_rows, k + 1)
                    sp.dma_start(segv[:, bass.ds(k * CW, CW), :].rearrange("p j c -> p (j c)"),
                                 rows[:, par, :, :].rearrange("p j c -> p (j c)")).then_inc(rows_out, 16)
                    sp.wait_ge(rows_out, k * 16 + 16)
                    sp.sem_inc(slot_free, 1)
            sp.wait_ge(e_out, 17)
            sp.wait_ge(v_tails, 1)
            sp.dma_start(rowt, tails[:, :, :].rearrange("p k c -> p (k c)")).then_inc(bounce, 16)
            sp.wait_ge(bounce, 16)
            for k in range(3):
                sp.dma_start(rt[:, k, :], n.row[:, k * NC5:(k + 1) * NC5].rearrange("p c -> c p"), allow_slow_non_contiguous=True).then_inc(bounce, 16)
            sp.wait_ge(v_car, 1)
            sp.dma_start(n.row[:, 3 * NC5:4 * NC5].rearrange("p c -> c p"), So[:, 0:P], allow_slow_non_contiguous=True).then_inc(bounce, 16)
            sp.dma_start(n.row[:, 4 * NC5:5 * NC5].rearrange("p c -> c p"), Mo[:, 0:P], allow_slow_non_contiguous=True).then_inc(bounce, 16)
            sp.wait_ge(bounce, 96)
            sp.dma_start(carry[:, :, :].rearrange("p k c -> p (k c)"), rowc).then_inc(bounce, 16)

        @block.gpsimd
        def _(pool):
            pool.memset(empty[:, 0:NC5], 0.0)
            pool.memset(empty[:, NC5:ROW], NEG).then_inc(e_out, 1)
            pool.memset(fix[:, :], 0.0)
            with pool.Fori(0, NK // 2) as it:
                for par in range(2):
                    k = it * 2 + par
                    pool.wait_ge(slot_free, k + 1)
                    pool.sem_inc(passed, 1)
                    pool.tensor_copy(idx[:, par, 0, :], n.srci[:, bass.ds(k * CW, CW)]).then_inc(ist, 1)
                    pool.tensor_copy(idx[:, par, 1, :], n.dsti[:, bass.ds(k * CW, CW)]).then_inc(ist, 1)
                    pool.wait_ge(ist, k * 2 + 2)
                    pool.sem_inc(passed, 1)
                    for j in range(CW):
                        pool.indirect_dma_start(out=rows[:, par, j, 0:HE], out_offset=None, in_=n.htab,
                                                in_offset=bass.IndirectOffsetOnAxis(ap=idx[:, par, 0, j:j + 1], axis=0)).then_inc(rows_in[par], 16)
                        pool.indirect_dma_start(out=rows[:, par, j, HE:HE + NH], out_offset=None, in_=n.adtab,
                                                in_offset=bass.IndirectOffsetOnAxis(ap=idx[:, par, 1, j:j + 1], axis=0)).then_inc(rows_in[par], 16)
            pool.wait_ge(v_fi, 1)
            pool.wait_ge(rows_out, 16 * NK)
            pool.indirect_dma_start(out=fix[:, :], out_offset=None, in_=n.seg,
                                    in_offset=bass.IndirectOffsetOnAxis(ap=fi[:, 0:1], axis=0),
                                    bounds_check=E, oob_is_err=False).then_inc(fix_in, 16)
            pool.wait_ge(v_fixo, 1)
            pool.indirect_dma_start(out=n.seg, out_offset=bass.IndirectOffsetOnAxis(ap=fi[:, 1:2], axis=0),
                                    in_=fixo[:, :], in_offset=None,
                                    bounds_check=E, oob_is_err=False).then_inc(fix_out, 16)
            pool.wait_ge(fix_out, 16)

        @block.scalar
        def _(act):
            with act.Fori(0, NK) as k:
                act.wait_ge(v_x, k + 1)
                act.activation(FX[:, :, :, :].rearrange("p a h j -> p (a h j)"), X[:, :, :, :].rearrange("p a h j -> p (a h j)"), ACT.Exp).then_inc(a_x, 1)
            act.wait_ge(v_x, NK + 1)
            act.activation(ea[:, :, :].rearrange("c a p -> c (a p)"), ex[:, :, :].rearrange("c a p -> c (a p)"), ACT.Exp).then_inc(a_x, 1)
            act.wait_ge(v_x, NK + 2)
            act.activation(me[:, :, :].rearrange("p a h -> p (a h)"), mm[:, 1:3, :].rearrange("p a h -> p (a h)"), ACT.Exp).then_inc(a_x, 1)

        @block.vector
        def _(dve):
            dve.memset(D0[:, :, 0:1], NEG)
            dve.memset(MF[:, :, CW:CW + 1], NEG)
            dve.memset(G0[:, :, :, 0:1], 0.0)
            dve.memset(Mo[:, 0:1], NEG)
            dve.memset(So[:, 0:1], 0.0)
            dve.memset(S[:, :, :, CW:CW + 1], 0.0).then_inc(slot_free, 2)
            dve.wait_ge(slot_free, 2)
            dve.wait_ge(a_in, 16)
            NL = 10
            with dve.Fori(0, NK // 2) as it:
                for par in range(2):
                    k = it * 2 + par
                    cnt = [0]

                    def link(ins):
                        cnt[0] += 1
                        ins.then_inc(vq, 1)
                        dve.wait_ge(vq, k * NL + cnt[0])
                    dve.tensor_copy(D1[:, :, 0:1], MF[:, :, CW:CW + 1])
                    dve.tensor_copy(G1[:, :, :, 0:1], S[:, :, :, CW:CW + 1])
                    link(dve.tensor_copy(stc[:, :], n.start[:, bass.ds(k * CW, CW)]))
                    dve.tensor_copy(D0[:, :, 1:CW + 1], stc[:, :].unsqueeze(1).to_broadcast([P, NH, CW]))
                    dve.wait_ge(rows_in[par], (it + 1) * 32 * CW)
                    r = rows[:, par, :, :]
                    link(dve.tensor_tensor(prod[:, :, :], r[:, :, 0:HE], attb[:, :].unsqueeze(1).to_broadcast([P, CW, HE]), ALU.mult))
                    link(dve.tensor_reduce(asr[:, :, :], prod[:, :, :].rearrange("p j (h e) -> p j h e", e=NX), AX.X, ALU.add))
                    link(dve.tensor_tensor(ee[:, :, :], asr[:, :, :], r[:, :, HE:HE + NH], ALU.add))
                    link(dve.scalar_tensor_tensor(D1[:, :, 1:CW + 1].rearrange("p h j -> p j h"), ee[:, :, :], 0.2, ee[:, :, :], ALU.mult, ALU.max))
                    link(dve.tensor_tensor_scan(MF[:, :, :].rearrange("p h j -> p (h j)"), D0[:, :, :].rearrange("p h j -> p (h j)"),
                                                D1[:, :, :].rearrange("p h j -> p (h j)"), NEG, ALU.add, ALU.max))
                    link(dve.tensor_tensor(X[:, 0, :, :], MF[:, :, 0:CW], D0[:, :, 1:CW + 1], ALU.add))
                    link(dve.tensor_tensor(X[:, 0, :, :], X[:, 0, :, :], MF[:, :, 1:CW + 1], ALU.subtract))
                    dve.tensor_tensor(X[:, 1, :, :], D1[:, :, 1:CW + 1], MF[:, :, 1:CW + 1], ALU.subtract).then_inc(v_x, 1)
                    dve.wait_ge(a_x, k + 1)
                    dve.tensor_copy(G0[:, :, :, 1:CW + 1], FX[:, 0, :, :].unsqueeze(2).to_broadcast([P, NH, NX + 1, CW]))
                    dve.tensor_copy(G1[:, :, NX, 1:CW + 1], FX[:, 1, :, :])
                    for h in range(NH):
                        last = dve.tensor_tensor(G1[:, h, 0:NX, 1:CW + 1], r[:, :, h * NX:(h + 1) * NX].rearrange("p j e -> p e j"),
                                                 FX[:, 1, h, :].unsqueeze(1).to_broadcast([P, NX, CW]), ALU.mult)
                    link(last)
                    link(dve.tensor_tensor_scan(S[:, :, :, :].rearrange("p h e j -> p (h e j)"), G0[:, :, :, :].rearrange("p h e j -> p (h e j)"),
                                                G1[:, :, :, :].rearrange("p h e j -> p (h e j)"), 0.0, ALU.mult, ALU.add))
                    dve.tensor_copy(r[:, :, 0:NC5], S[:, :, :, :].rearrange("p h e j -> p (h e) j")[:, :, 1:CW + 1].rearrange("p c j -> p j c"))
                    dve.tensor_copy(r[:, :, NC5:ROW], MF[:, :, 1:CW + 1].rearrange("p h j -> p j h")).then_inc(v_rows, 1)
                    dve.wait_ge(v_rows, k + 1)
                    assert cnt[0] == NL, cnt
            done = [NK * NL]

            def step(ins):
                done[0] += 1
                ins.then_inc(vq, 1)
                dve.wait_ge(vq, done[0])
            dve.tensor_copy(tails[:, 0, :], S[:, :, :, CW:CW + 1].rearrange("p h e a -> p (h e a)"))
            for e in range(NX + 1):
                dve.tensor_copy(tails[:, 1, e::NX + 1], MF[:, :, CW:CW + 1].rearrange("p h a -> p (h a)"))
            step(dve.tensor_tensor(fidx[:, 0:1], n.single[:, 0:1], n.single[:, 1:2], ALU.min))
            dve.tensor_copy(tails[:, 2, :], fidx[:, 0:1].to_broadcast([P, NC5])).then_inc(v_tails, 1)
            step(dve.tensor_scalar(fidx[:, 1:2], n.single[:, 1:2], FAR / NEG, None, ALU.mult))
            step(dve.tensor_tensor(fidx[:, 1:2], fidx[:, 1:2], n.single[:, 2:3], ALU.add))
            dve.tensor_copy(fi[:, 0:1], n.single[:, 2:3])
            dve.tensor_copy(fi[:, 1:2], fidx[:, 1:2]).then_inc(v_fi, 1)
            dve.wait_ge(bounce, 64)
            step(dve.tensor_tensor_scan(Mo[:, 1:P + 1], rt[:, 2, :], rt[:, 1, :], NEG, ALU.add, ALU.max))
            step(dve.tensor_tensor(ex[:, 0, :], Mo[:, 0:P], rt[:, 2, :], ALU.add))
            step(dve.tensor_tensor(ex[:, 0, :], ex[:, 0, :], Mo[:, 1:P + 1], ALU.subtract))
            dve.tensor_tensor(ex[:, 1, :], rt[:, 1, :], Mo[:, 1:P + 1], ALU.subtract).then_inc(v_x, 1)
            dve.wait_ge(a_x, NK + 1)
            step(dve.tensor_tensor(ea[:, 1, :], ea[:, 1, :], rt[:, 0, :], ALU.mult))
            dve.tensor_tensor_scan(So[:, 1:P + 1], ea[:, 0, :], ea[:, 1, :], 0.0, ALU.mult, ALU.add).then_inc(v_car, 1)
            dve.wait_ge(bounce, 112)
            dve.wait_ge(fix_in, 16)
            step(dve.tensor_tensor(mm[:, 0, :], fix[:, NC5:ROW], carry[:, 1, ::NX + 1], ALU.max))
            dve.tensor_tensor(mm[:, 1, :], fix[:, NC5:ROW], mm[:, 0, :], ALU.subtract)
            dve.tensor_tensor(mm[:, 2, :], carry[:, 1, ::NX + 1], mm[:, 0, :], ALU.subtract).then_inc(v_x, 1)
            dve.tensor_copy(fixo[:, NC5:ROW], mm[:, 0, :])
            dve.wait_ge(a_x, NK + 2)
            v5 = "p (h e) -> p h e"
            dve.tensor_tensor(part[:, 0, :].rearrange(v5, h=NH), fix[:, 0:NC5].rearrange(v5, h=NH),
                              me[:, 0, :].unsqueeze(2).to_broadcast([P, NH, NX + 1]), ALU.mult)
            step(dve.tensor_tensor(part[:, 1, :].rearrange(v5, h=NH), carry[:, 0, :].rearrange(v5, h=NH),
                                   me[:, 1, :].unsqueeze(2).to_broadcast([P, NH, NX + 1]), ALU.mult))
            dve.tensor_tensor(fixo[:, 0:NC5], part[:, 0, :], part[:, 1, :], ALU.add).then_inc(v_fixo, 1)


def gates(nc, n, att_s, att_d, b_gat, gamma, beta):
    HE, NH, NX, M, ROW, NT = n.HE, n.NH, n.NX, n.M, n.ROW, n.NT
    NC5 = NH * (NX + 1)
    TW = 48 if NT % 96 == 0 else NT // 2
    NK = NT // TW
    with ExitStack() as ctx:
        def sb(name, shape, dt=F32):
            return ctx.enter_context(nc.sbuf_tensor(name, shape, dt))

        def sem(name):
            return ctx.enter_context(nc.semaphore(name))
        pos = sb("pos", [P, NT], I32)
        idx = sb("nidx", [P, 2, TW], I32)
        R = sb("R", [P, 2, TW, ROW])
        Hn = sb("Hn", [P, 2, TW, HE])
        AD = sb("AD", [P, 2, TW, NH])
        cst = sb("cst", [P, 4, HE])
        low = sb("low", [P, NX, NX])
        high = sb("high", [P, NX, NX])
        T0 = sb("T0", [P, TW, HE])
        T1 = sb("T1", [P, TW, HE])
        T2 = sb("T2", [P, TW, HE])
        U0 = sb("U0", [P, TW, NH])
        U1 = sb("U1", [P, TW, NH])
        MX = sb("MX", [P, TW, NH])
        X = sb("Xg", [P, 2, TW, NH])
        FX = sb("FXg", [P, 2, TW, NH])
        dn = sb("dn", [P, TW, NH])
        s1 = sb("s1", [P, TW])
        s3 = sb("s3", [P, TW])
        s4 = sb("s4", [P, TW])
        sc = sb("sc", [P, TW, NX])
        es = sb("es", [P, TW, NX])
        xs = sb("xs", [P, TW, NX])
        G = sb("G", [P, NX, TW])
        GH = sb("GH", [P, 2, 2 * NX, TW], F16)
        eps = sb("epsg", [P, 1])
        c_in = sem("gc_in")
        ist = sem("gist")
        passed = sem("gpassed")
        slot_free = sem("gslot_free")
        r_in = [sem("r_in0"), sem("r_in1")]
        h_in = [sem("h_in0"), sem("h_in1")]
        vq = sem("gvq")
        v_x = sem("gv_x")
        a_x = sem("ga_x")
        v_g = sem("v_g")
        g_out = sem("g_out")
        m_rdy = sem("m_rdy")
        block = ctx.enter_context(nc.Block())
        hv = n.htab.rearrange("(p t) c -> p t c", p=P)
        av = n.adtab.rearrange("(p t) c -> p t c", p=P)
        gv = n.gates.rearrange("e (p t) -> p e t", p=P)

        @block.sync
        def _(sp):
            sp.dma_start(pos[:, :], n.pos.rearrange("(p t) a -> p (t a)", p=P)).then_inc(c_in, 16)
            sp.dma_start(cst[:, 0, :], att_s.rearrange("(a h) e -> a (h e)", a=1).to_broadcast((P, HE))).then_inc(c_in, 16)
            for k, v in ((1, b_gat), (2, gamma), (3, beta)):
                sp.dma_start(cst[:, k, :], v.rearrange("(a c) -> a c", a=1).to_broadcast((P, HE))).then_inc(c_in, 16)
            with sp.Fori(0, NK // 2) as it:
                for par in range(2):
                    k = it * 2 + par
                    sp.wait_ge(slot_free, k + 1)
                    sp.dma_start(Hn[:, par, :, :], hv[:, bass.ds(k * TW, TW), :]).then_inc(h_in[par], 16)
                    sp.dma_start(AD[:, par, :, :], av[:, bass.ds(k * TW, TW), :]).then_inc(h_in[par], 16)

        @block.gpsimd
        def _(pool):
            pool.memset(low[:, :, :], 0.0)
            pool.memset(high[:, :, :], 0.0).then_inc(m_rdy, 1)
            pool.memset(eps[:, :], 1e-5)
            pool.wait_ge(m_rdy, 1)
            for i in range(NX - 1):
                pool.memset(low[:, i + 1, 0:i + 1], 1.0)
                pool.memset(high[:, i, i + 1:NX], 1.0).then_inc(m_rdy, 1)
            pool.wait_ge(c_in, 80)
            with pool.Fori(0, NK // 2) as it:
                for par in range(2):
                    k = it * 2 + par
                    pool.wait_ge(slot_free, k + 1)
                    pool.sem_inc(passed, 1)
                    pool.tensor_copy(idx[:, par, :], pos[:, bass.ds(k * TW, TW)]).then_inc(ist, 1)
                    pool.wait_ge(ist, k + 1)
                    pool.sem_inc(passed, 1)
                    for j in range(TW):
                        pool.indirect_dma_start(out=R[:, par, j, :], out_offset=None, in_=n.seg,
                                                in_offset=bass.IndirectOffsetOnAxis(ap=idx[:, par, j:j + 1], axis=0)).then_inc(r_in[par], 16)

        @block.scalar
        def _(act):
            act.wait_ge(m_rdy, NX)
            with act.Fori(0, NK // 2) as it:
                for par in range(2):
                    k = it * 2 + par
                    act.wait_ge(v_x, k * 3 + 1)
                    act.activation(FX[:, :, :, :].rearrange("p a t h -> p (a t h)"), X[:, :, :, :].rearrange("p a t h -> p (a t h)"), ACT.Exp).then_inc(a_x, 1)
                    act.wait_ge(v_x, k * 3 + 2)
                    act.activation(s3[:, :], s1[:, :], ACT.Sqrt, bias=eps[:, 0:1], scale=1.0 / HE).then_inc(a_x, 1)
                    act.wait_ge(v_x, k * 3 + 3)
                    act.activation(es[:, :, :], xs[:, :, :], ACT.Exp).then_inc(a_x, 1)
                    act.wait_ge(v_g, k + 1)
                    act.dma_start(gv[:, :, bass.ds(k * TW, TW)], GH[:, par, :, :]).then_inc(g_out, 16)
            act.wait_ge(g_out, 16 * NK)

        @block.vector
        def _(dve):
            dve.wait_ge(m_rdy, NX)
            dve.wait_ge(c_in, 80)
            dve.memset(s1[:, :], 0.0).then_inc(slot_free, 2)
            bc = lambda k: cst[:, k, :].unsqueeze(1).to_broadcast([P, TW, HE])
            hx = lambda ap: ap.unsqueeze(3).to_broadcast([P, TW, NH, NX])
            v4 = lambda ap: ap.rearrange("p t (h e) -> p t h e", e=NX)
            bt = lambda ap: ap.unsqueeze(2).to_broadcast([P, TW, HE])
            b4 = lambda ap: ap.unsqueeze(2).to_broadcast([P, TW, NX])
            NL = 31
            with dve.Fori(0, NK // 2) as it:
                for par in range(2):
                    k = it * 2 + par
                    cnt = [0]

                    def link(ins):
                        cnt[0] += 1
                        ins.then_inc(vq, 1)
                        dve.wait_ge(vq, k * NL + cnt[0])
                    dve.wait_ge(h_in[par], (it + 1) * 32)
                    dve.wait_ge(r_in[par], (it + 1) * 16 * TW)
                    dve.wait_ge(g_out, it * 32)
                    r = R[:, par, :, :]
                    r5 = r[:, :, 0:NC5].rearrange("p t (h e) -> p t h e", h=NH)
                    link(dve.tensor_tensor(T0[:, :, :], Hn[:, par, :, :], bc(0), ALU.mult))
                    link(dve.tensor_reduce(U0[:, :, :], v4(T0[:, :, :]), AX.X, ALU.add))
                    link(dve.tensor_tensor(U0[:, :, :], U0[:, :, :], AD[:, par, :, :], ALU.add))
                    link(dve.scalar_tensor_tensor(U1[:, :, :], U0[:, :, :], 0.2, U0[:, :, :], ALU.mult, ALU.max))
                    link(dve.tensor_tensor(MX[:, :, :], r[:, :, NC5:ROW], U1[:, :, :], ALU.max))
                    dve.tensor_tensor(X[:, 0, :, :], r[:, :, NC5:ROW], MX[:, :, :], ALU.subtract)
                    dve.tensor_tensor(X[:, 1, :, :], U1[:, :, :], MX[:, :, :], ALU.subtract).then_inc(v_x, 1)
                    dve.wait_ge(a_x, k * 3 + 1)
                    link(dve.tensor_tensor(dn[:, :, :], r5[:, :, :, NX], FX[:, 0, :, :], ALU.mult))
                    link(dve.scalar_tensor_tensor(dn[:, :, :], FX[:, 1, :, :], 1e-16, dn[:, :, :], ALU.add, ALU.add))
                    dve.tensor_tensor(v4(T0[:, :, :]), r5[:, :, :, 0:NX], hx(FX[:, 0, :, :]), ALU.mult)
                    dve.tensor_tensor(v4(T1[:, :, :]), v4(Hn[:, par, :, :]), hx(FX[:, 1, :, :]), ALU.mult)
                    link(dve.reciprocal(U0[:, :, :], dn[:, :, :]))
                    link(dve.tensor_tensor(T0[:, :, :], T0[:, :, :], T1[:, :, :], ALU.add))
                    link(dve.tensor_tensor(v4(T0[:, :, :]), v4(T0[:, :, :]), hx(U0[:, :, :]), ALU.mult))
                    link(dve.tensor_tensor(T0[:, :, :], T0[:, :, :], bc(1), ALU.add))
                    link(dve.tensor_reduce(s1[:, :], T0[:, :, :], AX.X, ALU.add))
                    link(dve.tensor_scalar(s4[:, :], s1[:, :], 1.0 / HE, None, ALU.mult))
                    link(dve.tensor_tensor(T1[:, :, :], T0[:, :, :], bt(s4[:, :]), ALU.subtract))
                    link(dve.tensor_tensor(T2[:, :, :], T1[:, :, :], T1[:, :, :], ALU.mult))
                    dve.tensor_reduce(s1[:, :], T2[:, :, :], AX.X, ALU.add).then_inc(v_x, 1)
                    dve.wait_ge(a_x, k * 3 + 2)
                    link(dve.reciprocal(s4[:, :], s3[:, :]))
                    link(dve.tensor_tensor(T1[:, :, :], T1[:, :, :], bt(s4[:, :]), ALU.mult))
                    link(dve.tensor_tensor(T1[:, :, :], T1[:, :, :], bc(2), ALU.mult))
                    link(dve.tensor_tensor(T1[:, :, :], T1[:, :, :], bc(3), ALU.add))
                    link(dve.tensor_reduce(xs[:, :, :], T1[:, :, :].rearrange("p t (h e) -> p t e h", e=NX), AX.X, ALU.add))
                    link(dve.tensor_scalar(sc[:, :, :], xs[:, :, :], 1.0 / NH, None, ALU.mult))
                    si = sc[:, :, :].unsqueeze(3).to_broadcast([P, TW, NX, NX])
                    sj = sc[:, :, :].unsqueeze(2).to_broadcast([P, TW, NX, NX])
                    dve.tensor_tensor(v4(T0[:, :, :]), sj, si, ALU.is_ge)
                    link(dve.tensor_tensor(v4(T1[:, :, :]), sj, si, ALU.is_gt))
                    dve.tensor_tensor(v4(T0[:, :, :]), v4(T0[:, :, :]), low[:, :, :].unsqueeze(1).to_broadcast([P, TW, NX, NX]), ALU.mult)
                    link(dve.tensor_tensor(v4(T1[:, :, :]), v4(T1[:, :, :]), high[:, :, :].unsqueeze(1).to_broadcast([P, TW, NX, NX]), ALU.mult))
                    link(dve.tensor_tensor(T2[:, :, :], T0[:, :, :], T1[:, :, :], ALU.add))
                    dve.tensor_reduce(U0[:, :, :], v4(T2[:, :, :]), AX.X, ALU.add)
                    link(dve.tensor_reduce(s4[:, :], sc[:, :, :], AX.X, ALU.max))
                    dve.tensor_tensor(xs[:, :, :], sc[:, :, :], b4(s4[:, :]), ALU.subtract).then_inc(v_x, 1)
                    link(dve.tensor_scalar(U0[:, :, :], U0[:, :, :], 1.5, None, ALU.is_lt))
                    dve.wait_ge(a_x, k * 3 + 3)
                    link(dve.tensor_tensor(U1[:, :, :], es[:, :, :], U0[:, :, :], ALU.mult))
                    link(dve.tensor_reduce(s4[:, :], U1[:, :, :], AX.X, ALU.add))
                    link(dve.reciprocal(s4[:, :], s4[:, :]))
                    link(dve.tensor_tensor(G[:, :, :].rearrange("p e t -> p t e"), U1[:, :, :], b4(s4[:, :]), ALU.mult))
                    link(dve.tensor_scalar(GH[:, par, 0:NX, :], G[:, :, :], GSPLIT, None, ALU.mult))
                    dve.scalar_tensor_tensor(GH[:, par, NX:2 * NX, :], G[:, :, :], GSPLIT, GH[:, par, 0:NX, :], ALU.mult,
                                             ALU.subtract).then_inc(v_g, 1)
                    assert cnt[0] == NL, cnt
                    dve.wait_ge(v_g, k + 1)
                    dve.sem_inc(slot_free, 1)


def experts(nc, n, W1, b1, W2, b2):
    B, C, NP, NX, HID = n.B, n.C, n.NP, n.NX, n.HID
    CW = 384
    NCH = NP // CW
    PARTS = 3
    with ExitStack() as ctx:
        def sb(name, shape, dt=F32):
            return ctx.enter_context(nc.sbuf_tensor(name, shape, dt))

        def pb(name):
            return ctx.enter_context(nc.psum_tensor(name, [P, 512], F32))

        def sem(name):
            return ctx.enter_context(nc.semaphore(name))
        w1 = sb("w1", [2 * C, NX, HID])
        w1p = sb("w1p", [2 * C, PARTS, NX, HID], BF16)
        w2 = sb("w2", [HID, NX, C])
        b1r = sb("b1r", [NX, HID])
        b1t = sb("b1t", [HID, NX])
        b2r = sb("b2r", [2 * NX, C])
        b2p = sb("b2p", [2 * NX, PARTS, C], BF16)
        pickf = sb("pickf", [2 * NX, NX, HID])
        pick = sb("pick", [2 * NX, NX, HID], BF16)
        tn = sb("tne", [2 * C, 2, NP], F16)
        x2 = sb("x2e", [C, 2, NP])
        g = sb("ge", [2 * NX, 2, NP], F16)
        hid = sb("hid", [HID, 4, CW])
        hg = sb("hg", [HID, 4, CW])
        half = sb("ehalf", [C, CW])
        res = sb("res", [C, 2, NP])
        up = [pb(f"up{i}") for i in range(3)]
        gb = [pb(f"gb{i}") for i in range(3)]
        acc = [pb("eacc0"), pb("eacc1")]
        w_in = sem("ew_in")
        pk = sem("pk")
        pe_b = sem("pe_b")
        v_b = sem("v_b")
        v_w = sem("v_w")
        in_ = [sem("e_in0"), sem("e_in1")]
        pe_up = sem("pe_up")
        a_hid = sem("a_hid")
        v_hg = sem("v_hg")
        pe_dn = sem("pe_dn")
        v_half = sem("v_half")
        v_res = sem("v_res")
        free = sem("efree")
        left = sem("eleft")
        passed = sem("epassed")
        r_out = [sem("r_out0"), sem("r_out1")]
        block = ctx.enter_context(nc.Block())
        STEPS = NCH * NX

        @block.sync
        def _(sp):
            for h in (0, C):
                sp.dma_start(w1[h:h + C, :, :], W1.rearrange("e c h -> c e h")).then_inc(w_in, 16)
            sp.dma_start(w2[:, :, :], W2.rearrange("e h c -> h e c")).then_inc(w_in, 16)
            sp.dma_start(b1r[:, :], b1).then_inc(w_in, 16)
            for h in (0, NX):
                sp.dma_start(b2r[h:h + NX, :], b2).then_inc(w_in, 16)
            with sp.Fori(0, B // 2) as ii:
                for par in range(2):
                    b = ii * 2 + par
                    sp.wait_ge(free, b + 1)
                    one = lambda t: t[bass.ds(b, 1), :, :].rearrange("a c p -> (a c) p")
                    sp.dma_start(tn[:, par, :], one(n.tn)).then_inc(in_[par], 16)
                    sp.dma_start(x2[:, par, :], one(n.x2)).then_inc(in_[par], 16)
                    sp.dma_start(g[:, par, :], n.gates[:, bass.ds(b * NP, NP)]).then_inc(in_[par], 16)

        @block.gpsimd
        def _(pool):
            pool.memset(pickf[:, :, :], 0.0).then_inc(pk, 1)
            for k in range(2):
                pool.wait_ge(pk, k + 1)
                pool.affine_select(out=pickf[:, :, :], in_=pickf[:, :, :], compare_op=ALU.not_equal, fill=1.0 / GSPLIT,
                                   base=-k * NX, pattern=[[-1, NX], [0, HID]], channel_multiplier=1).then_inc(pk, 1)
            pool.wait_ge(pk, 3)
            pool.tensor_copy(pick[:, :, :], pickf[:, :, :]).then_inc(pk, 1)
            with pool.Fori(0, B // 2) as ii:
                for par in range(2):
                    pool.wait_ge(v_res, (ii * 2 + par + 1) * NCH)
                    pool.sem_inc(passed, 1)
                    pool.dma_start(n.of[bass.ds(ii * 2 + par, 1), :, :].rearrange("a c p -> (a c) p"), res[:, par, :]).then_inc(r_out[par], 16)
                for par in range(2):
                    pool.wait_ge(r_out[par], (ii + 1) * 16)
                    pool.sem_inc(passed, 1)
                pool.sem_inc(left, 1)

        @block.tensor
        def _(pe):
            pe.wait_ge(w_in, 96)
            pe.wait_ge(pk, 4)
            pe.transpose(up[0][0:HID, 0:NX], b1r[:, :], n.ident[0:NX, 0:NX]).then_inc(pe_b, 1)
            pe.wait_ge(v_b, 1)
            pe.wait_ge(v_w, 2 * (2 * PARTS - 1))
            with pe.Fori(0, B // 2) as ii:
                for par in range(2):
                    b = ii * 2 + par
                    pe.wait_ge(in_[par], (ii + 1) * 48)
                    for t in range(STEPS + 3):
                        if t < STEPS:
                            c, e = divmod(t, NX)
                            rhs = tn[:, par, c * CW:(c + 1) * CW]
                            if t >= 3:
                                pe.wait_ge(v_hg, b * STEPS + t - 2)
                            for k in range(PARTS):
                                pe.matmul(up[t % 3][:, 0:CW], w1p[:, k, e, :], rhs, start=k == 0, stop=k == PARTS - 1)
                            pe.matmul(gb[t % 3][:, 0:CW], pick[:, e, :], g[:, par, c * CW:(c + 1) * CW], start=True, stop=True).then_inc(pe_up, 1)
                        u = t - 3
                        if u >= 0 and u % 2 == 0:
                            c, e = divmod(u, NX)
                            if e == 0:
                                if c >= 2:
                                    pe.wait_ge(v_res, b * NCH + c - 1)
                                for k in range(PARTS):
                                    pe.matmul(acc[c % 2][0:C, 0:CW], b2p[:, k, :], g[:, par, c * CW:(c + 1) * CW], start=k == 0, stop=False)
                            pe.wait_ge(v_hg, b * STEPS + u + 2)
                            for v in (u, u + 1):
                                h = C * (v % 2)
                                pe.matmul(acc[c % 2][h:h + C, 0:CW], w2[:, v % NX, :], hg[:, v % 4, :], start=v % NX == 1,
                                          stop=v % NX >= NX - 2).then_inc(pe_dn, 1)
                    pe.wait_ge(v_res, (b + 1) * NCH)

        @block.scalar
        def _(act):
            act.wait_ge(v_b, 1)
            with act.Fori(0, B // 2) as ii:
                for par in range(2):
                    b = ii * 2 + par
                    for t in range(STEPS):
                        act.wait_ge(pe_up, b * STEPS + t + 1)
                        if t >= 4:
                            act.wait_ge(v_hg, b * STEPS + t - 3)
                        act.activation(hid[:, t % 4, :], up[t % 3][:, 0:CW], ACT.Gelu, bias=b1t[:, t % NX:t % NX + 1],
                                       scale=1.0 / SPLIT).then_inc(a_hid, 1)

        @block.vector
        def _(dve):
            dve.wait_ge(pe_b, 1)
            dve.tensor_copy(b1t[:, :], up[0][0:HID, 0:NX]).then_inc(v_b, 1)
            dve.tensor_scalar(b2r[:, :], b2r[:, :], 1.0 / GSPLIT, None, ALU.mult).then_inc(v_b, 1)
            dve.wait_ge(v_b, 2)
            done = 0
            for full, parts, at in ((w1, w1p, lambda k: w1p[:, k, :, :].rearrange("c e h -> c (e h)")), (b2r, b2p, lambda k: b2p[:, k, :])):
                rest = w1[:, :, :].rearrange("c e h -> c (e h)") if full is w1 else b2r[:, :]
                for k in range(PARTS):
                    dve.tensor_copy(at(k), rest).then_inc(v_w, 1)
                    done += 1
                    dve.wait_ge(v_w, done)
                    if k < PARTS - 1:
                        dve.tensor_tensor(rest, rest, at(k), ALU.subtract).then_inc(v_w, 1)
                        done += 1
                        dve.wait_ge(v_w, done)
            dve.sem_inc(free, 2)
            dve.sem_inc(left, 1)

            def sums(b, par, c):
                cols = slice(c * CW, (c + 1) * CW)
                dve.wait_ge(pe_dn, b * STEPS + (c + 1) * NX)
                dve.tensor_tensor(half[:, :], acc[c % 2][0:C, 0:CW], x2[:, par, cols], ALU.add).then_inc(v_half, 1)
                dve.wait_ge(v_half, b * NCH + c + 1)
                dve.tensor_tensor(res[:, par, cols], acc[c % 2][C:2 * C, 0:CW], half[:, :], ALU.add).then_inc(v_res, 1)
            with dve.Fori(0, B // 2) as ii:
                dve.wait_ge(left, ii + 1)
                for par in range(2):
                    b = ii * 2 + par
                    for t in range(STEPS):
                        c, e = divmod(t, NX)
                        dve.wait_ge(a_hid, b * STEPS + t + 1)
                        if t >= 4:
                            dve.wait_ge(pe_dn, b * STEPS + t - 3)
                        dve.tensor_tensor(hg[:, t % 4, :], gb[t % 3][:, 0:CW], hid[:, t % 4, :], ALU.mult).then_inc(v_hg, 1)
                        if e == 2 and c:
                            sums(b, par, c - 1)
                    sums(b, par, NCH - 1)
                    dve.wait_ge(v_res, (b + 1) * NCH)
                    dve.sem_inc(free, 1)


_INS = ["x", "L0_conv_Wc", "L0_conv_bc", "L0_ffn_W_gat", "L0_ffn_att_src", "L0_ffn_att_dst", "L0_ffn_b_gat", "L0_ffn_ln_gamma",
        "L0_ffn_ln_beta", "L0_ffn_W1", "L0_ffn_b1", "L0_ffn_W2", "L0_ffn_b2", "L0_ffn_edge_index"]


def kernel(**inputs):
    import concourse.bacc as bacc
    from concourse.bass_utils import run_bass_kernel_spmd

    nc = bacc.Bacc("TRN2", target_bir_lowering=False, num_devices=1)
    arrays = {f"in_{name}": np.ascontiguousarray(inputs[name]) for name in _INS}
    args = [nc.dram_tensor(k, a.shape, mybir.dt.from_np(a.dtype), kind="ExternalInput").ap() for k, a in arrays.items()]
    out = nc.dram_tensor("out_0", inputs["x"].shape, F32, kind="ExternalOutput").ap()
    kernel_program(nc, *args, out)
    return run_bass_kernel_spmd(nc, [arrays], core_ids=[0]).results[0]["out_0"]
```

```python
from contextlib import ExitStack
import numpy as np
import concourse.bass as bass
import concourse.mybir as mybir

F32 = mybir.dt.float32
F16 = mybir.dt.float16
BF16 = mybir.dt.bfloat16
I32 = mybir.dt.int32
ALU = mybir.AluOpType
ACT = mybir.ActivationFunctionType
AX = mybir.AxisListType

P = 128
NEG = -1.0e30
SPLIT = 64.0
GSPLIT = 4096.0
FAR = 1.0e6


def chunks(n, size=512):
    return [(o, min(size, n - o)) for o in range(0, n, size)]


class Net:
    pass


def kernel_program(nc, x, Wc, bc, Wg, att_s, att_d, b_gat, gamma, beta, W1, b1, W2, b2, edges, out):
    B, C, H, W = x.shape
    NP = H * W
    M = B * NP
    E = edges.shape[1]
    HE = Wg.shape[1]
    NH, NX = att_s.shape
    HID = W1.shape[2]
    EC = E // P
    NT = M // P
    n = Net()
    n.B, n.C, n.NP, n.M, n.E, n.HE, n.NH, n.NX, n.HID, n.EC, n.NT = B, C, NP, M, E, HE, NH, NX, HID, EC, NT
    n.ROW = HE + 2 * NH
    n.x2 = nc.dram_tensor("x2_d", (B, C, NP), F32).ap()
    n.tn = nc.dram_tensor("tn_d", (B, 2 * C, NP), F16).ap()
    n.htab = nc.dram_tensor("htab_d", (M, HE), F32).ap()
    n.adtab = nc.dram_tensor("adtab_d", (M, NH), F32).ap()
    n.adend = nc.dram_tensor("adend_d", (E + 1, NH), F32).ap()
    n.pos = nc.dram_tensor("pos_d", (M, 1), I32).ap()
    n.seg = nc.dram_tensor("seg_d", (E + 1, n.ROW), F32).ap()
    n.row = nc.dram_tensor("row_d", (P, 5 * (HE + NH)), F32).ap()
    n.gates = nc.dram_tensor("gates_d", (2 * NX, M), F16).ap()
    n.xf = x.rearrange("b c h w -> b c (h w)")
    n.of = out.rearrange("b c h w -> b c (h w)")
    with ExitStack() as ctx:
        def sb(name, shape, dt=F32):
            return ctx.enter_context(nc.sbuf_tensor(name, shape, dt))
        n.dsti = sb("dsti", [P, EC], I32)
        n.srci = sb("srci", [P, EC], I32)
        n.start = sb("start", [P, EC])
        n.single = sb("single", [P, 4])
        n.ident = sb("ident", [P, P])
        with ExitStack() as edge_ctx:
            tiles = [edge_ctx.enter_context(nc.sbuf_tensor(name, [P, 2, EC], F32)) for name in ("edges0", "edges1")]
            KV, PV = sort_edges(nc, n, edges, *tiles)
            images(nc, n, Wc, bc, Wg, att_s, att_d, KV, PV)
        segments(nc, n, att_s)
        gates(nc, n, att_s, att_d, b_gat, gamma, beta)
        experts(nc, n, W1, b1, W2, b2)


def sort_edges(nc, n, edges, first, second):
    EC, E = n.EC, n.E
    LOG = int(np.log2(E))
    LC = int(np.log2(EC))
    stages = [(L, d) for L in range(1, LOG + 1) for d in [1 << t for t in range(L - 1, -1, -1)]]
    with ExitStack() as ctx:
        def sem(name):
            return ctx.enter_context(nc.semaphore(name))
        signs = ctx.enter_context(nc.sbuf_tensor("signs", [P, P], F32))
        work = ctx.enter_context(nc.sbuf_tensor("signwork", [P, P], F32))
        fold = ctx.enter_context(nc.sbuf_tensor("signfold", [P, 64], F32))
        bits = ctx.enter_context(nc.sbuf_tensor("bits", [P, 8], F32))
        sx = ctx.enter_context(nc.sbuf_tensor("sx", [P, 64], F32))
        mask = ctx.enter_context(nc.psum_tensor("swapmask", [P, max(EC, 512)], F32))
        e_in = sem("e_in")
        signs_ready = sem("signs_ready")
        pc = sem("spc")
        vs = sem("vs")
        v_pay = sem("v_pay")
        a_pay = sem("a_pay")
        kv_out = sem("skv_out")
        pv_in = sem("spv_in")
        block = ctx.enter_context(nc.Block())

        def swaps(pd):
            if 2 * pd <= P // pd:
                got = []
                for r in range(pd):
                    a, b = slice(r, P, 2 * pd), slice(r + pd, P, 2 * pd)
                    got += [(a, b), (b, a)]
                return got
            got = []
            for g in range(0, P, 2 * pd):
                a, b = slice(g, g + pd), slice(g + pd, g + 2 * pd)
                got += [(a, b), (b, a)]
            return got

        def other(t):
            return second if t is first else first

        def pair(t, a, d):
            v = t[:, a, :].rearrange("p (g two run) -> p g two run", two=2, run=d)
            return v[:, :, 0, :], v[:, :, 1, :]

        @block.sync
        def _(sp):
            sp.dma_start(second[:, :, :].bitcast(I32), edges.rearrange("a (p j) -> p a j", p=P)).then_inc(e_in, 16)
            served = 0
            cur = first
            for L, d in stages:
                if d >= EC:
                    served += 1
                    sp.wait_ge(kv_out, served)
                    for a, b in swaps(d // EC):
                        sp.dma_start(other(cur)[b, :, :], cur[a, :, :]).then_inc(pv_in, 16)
                else:
                    cur = other(cur)

        @block.gpsimd
        def _(pool):
            done = [0]

            def step(ins):
                done[0] += 1
                ins.then_inc(pc, 1)
                pool.wait_ge(pc, done[0])
            step(pool.memset(n.ident[:, :], 0.0))
            step(pool.affine_select(out=n.ident[:, :], in_=n.ident[:, :], compare_op=ALU.not_equal, fill=1.0, base=0,
                                    pattern=[[-1, P]], channel_multiplier=1))
            for b in range(8):
                w = 1 << b
                step(pool.memset(signs[:, :], 1.0))
                if w < P:
                    step(pool.memset(signs[:, :].rearrange("p (g two run) -> p g two run", two=2, run=w)[:, :, 1, :], -1.0))
                step(pool.tensor_tensor(work[:, :], signs[:, :], n.ident[:, :], ALU.mult))
                step(pool.tensor_tensor(fold[:, :], work[:, 0:64], work[:, 64:128], ALU.add))
                w2 = 32
                while w2:
                    step(pool.tensor_tensor(fold[:, 0:w2], fold[:, 0:w2], fold[:, w2:2 * w2], ALU.add))
                    w2 //= 2
                step(pool.tensor_copy(bits[:, b:b + 1], fold[:, 0:1]))
            for b in range(8):
                step(pool.tensor_scalar(sx[:, 8 * b:8 * b + 8], bits[:, :], bits[:, b:b + 1], None, ALU.mult))
            pool.sem_inc(signs_ready, 1)

        @block.scalar
        def _(act):
            cur = first
            paid = copied = 0
            for L, d in stages:
                if d >= EC:
                    paid += 1
                    continue
                act.wait_ge(v_pay, 1 + paid)
                act.activation(other(cur)[:, 1, :], cur[:, 1, :], ACT.Copy).then_inc(a_pay, 1)
                paid += 1
                cur = other(cur)

        @block.vector
        def _(dve):
            done = [0]

            def step(ins):
                done[0] += 1
                ins.then_inc(vs, 1)
                dve.wait_ge(vs, done[0])

            def flip(t, *which):
                col = bits[:, which[0]:which[0] + 1] if len(which) == 1 else sx[:, 8 * which[0] + which[1]:8 * which[0] + which[1] + 1]
                step(dve.tensor_scalar(t[:, 0, :], t[:, 0, :], col, None, ALU.mult))

            dve.wait_ge(e_in, 16)
            raw = second[:, :, :].bitcast(I32)
            dve.tensor_copy(first[:, 1, :], raw[:, 0, :])
            step(dve.tensor_copy(first[:, 0, :], raw[:, 1, :]))
            dve.sem_inc(v_pay, 1)
            cur = first
            served = arrived = copied = 0
            for L, d in stages:
                nxt = other(cur)
                if d == 1 << (L - 1):
                    if L < LC:
                        run = 1 << (L - 1)
                        v = cur[:, 0, :].rearrange("p (g four run) -> p g four run", four=4, run=run)[:, :, 1:3, :] if L > 1 else \
                            cur[:, 0, :].rearrange("p (g two run) -> p g two run", two=2, run=2)[:, :, 1, :]
                        step(dve.tensor_scalar(v, v, -1.0, None, ALU.mult))
                    elif L == LC:
                        v = cur[:, 0, EC // 2:EC]
                        step(dve.tensor_scalar(v, v, -1.0, None, ALU.mult))
                        dve.wait_ge(signs_ready, 1)
                        flip(cur, 0)
                if d >= EC:
                    t = int(np.log2(d // EC))
                    if t == L - LC - 1:
                        flip(cur, L - LC)
                    else:
                        flip(cur, t + 1, t)
                    served += 1
                    dve.sem_inc(kv_out, 1)
                    arrived += 16 * len(swaps(d // EC))
                    dve.wait_ge(pv_in, arrived)
                    step(dve.scalar_tensor_tensor(mask[:, 0:EC], nxt[:, 0, :], -1.0, cur[:, 0, :], ALU.mult, ALU.is_lt))
                    dve.scalar_tensor_tensor(cur[:, 0, :], nxt[:, 0, :], -1.0, cur[:, 0, :], ALU.mult, ALU.min)
                    step(dve.copy_predicated(cur[:, 1, :], mask[:, 0:EC].bitcast(I32), nxt[:, 1, :]))
                    if t == 0:
                        flip(cur, 0)
                    dve.sem_inc(v_pay, 1)
                    continue
                HC = EC // 2
                (klo, khi), (plo, phi) = pair(cur, 0, d), pair(cur, 1, d)
                (qlo, qhi), (rlo, rhi) = pair(nxt, 0, d), pair(nxt, 1, d)
                m = mask[:, 0:HC].rearrange("p (g run) -> p g run", run=d)
                dve.tensor_tensor(m, klo, khi, ALU.is_gt)
                dve.tensor_tensor(qlo, klo, khi, ALU.min)
                step(dve.tensor_tensor(qhi, klo, khi, ALU.max))
                copied += 1
                dve.wait_ge(a_pay, copied)
                dve.copy_predicated(rlo, m.bitcast(I32), phi)
                step(dve.copy_predicated(rhi, m.bitcast(I32), plo))
                dve.sem_inc(v_pay, 1)
                cur = nxt
    within = len([1 for L, d in stages if d < EC])
    return (first, second) if within % 2 == 0 else (second, first)


def images(nc, n, Wc, bc, Wg, att_s, att_d, KV, PV):
    B, C, NP, HE, NH, NX, EC, M = n.B, n.C, n.NP, n.HE, n.NH, n.NX, n.EC, n.M
    QT = NP // P
    CH = chunks(NP)
    NCH = len(CH)
    STEPS = NCH * QT
    SLOTS = 12
    RELS = 6
    LAG = 8
    LC = int(np.log2(EC))
    with ExitStack() as ctx:
        def sb(name, shape, dt=F32):
            return ctx.enter_context(nc.sbuf_tensor(name, shape, dt))

        def pb(name):
            return ctx.enter_context(nc.psum_tensor(name, [P, 512], F32))

        def sem(name):
            return ctx.enter_context(nc.semaphore(name))
        xb = sb("xb", [P, 2, NP])
        cen = sb("cen", [P, 2, 512])
        sq = sb("sq", [P, 512])
        sd = sb("sd", [P, 2, 512])
        rstd = sb("rstd", [P, 512])
        r2 = sb("r2", [P, 512])
        n2 = sb("n2", [P, 512])
        xn = sb("xn", [P, 512])
        xl = sb("xl", [P, NP])
        hl = sb("hl", [P, 2, NP], F16)
        lh = sb("lh", [P, 2, NP], F16)
        gT = sb("gT", [P, 2, QT, C])
        rel = sb("rel", [P, RELS, 512])
        s2 = sb("s2", [P, SLOTS, 512])
        half = sb("half", [C, 512])
        x2 = sb("x2", [P, NP])
        tf = sb("tf", [P, NP])
        th = sb("th", [P, NP], F16)
        hx = sb("hx", [P, QT, HE + NH])
        centre = sb("centre", [P, 2, C])
        mean = sb("mean", [P, 2, C])
        wcl = sb("wcl", [C, C])
        wcT = sb("wcT", [P, C])
        bcb = sb("bcb", [P, C])
        wgx = sb("wgx", [P, HE + NH])
        adb = sb("adb", [C, HE])
        wad = sb("wad", [C, HE])
        epsc = sb("epsc", [P, 2])
        DF = KV
        KK = sb("KK", [P, EC + 2])
        ei = PV[:, :, :].bitcast(I32)
        endi = ei[:, 0, :]
        posv = ei[:, 1, :]
        zero = KK[:, 0:EC]
        pnode = sb("pnode", [P, QT], I32)
        anode = sb("anode", [P, QT, NH])
        inode = sb("inode", [P, QT], I32)
        fnode = sb("fnode", [P, 2, QT])
        gram = [pb(f"gram{i}") for i in range(4)]
        acc = [pb("acc0"), pb("acc1")]
        lnp = [pb("lnp0"), pb("lnp1")]
        w_in = sem("w_in")
        x_in = [sem("x_in0"), sem("x_in1")]
        xb_free = sem("xb_free")
        const_ready = sem("const_ready")
        wct_ps = sem("wct_ps")
        w_ready = sem("w_ready")
        pe_cen = sem("pe_cen")
        a_sq = sem("a_sq")
        pe_var = sem("pe_var")
        a_sd = sem("a_sd")
        v_n2 = sem("v_n2")
        a_nrm = sem("a_nrm")
        a_s2 = sem("a_s2")
        v_ln = sem("v_ln")
        pe_gt = sem("pe_gt")
        v_gt = sem("v_gt")
        pe_gram = sem("pe_gram")
        a_rel = sem("a_rel")
        v_s2 = sem("v_s2")
        pe_acc = sem("pe_acc")
        v_x2 = sem("v_x2")
        pe_h = sem("pe_h")
        v_h = sem("v_h")
        o_x2 = sem("o_x2")
        left = sem("left")
        v_hi = sem("v_hi")
        v_th = sem("v_th")
        vc = sem("vc")
        pc = sem("pc")
        kv_out = sem("kv_out")
        pv_in = sem("pv_in")
        z_out = sem("z_out")
        sc_out = [sem("sc_out0"), sem("sc_out1")]
        n_in = sem("n_in")
        nq = sem("nq")
        ad_out = sem("ad_out")
        st = sem("st")
        passed = sem("passed")
        SW = min(64, EC // 2)
        stage = sb("stage", [P, 2, 2, SW], I32)
        block = ctx.enter_context(nc.Block())
        GB = (QT * C + 511) // 512
        GPB = 512 // C
        HPB = 512 // (HE + NH)
        NHB = -(-QT // HPB)
        NLN = 2 * NCH

        PRE = NCH
        VALUES_AT = (16,)

        @block.sync
        def _(sp):
            def load(img, par):
                for h in (0, C):
                    sp.dma_start(xb[h:h + C, par, :], img).then_inc(x_in[par], 16)
            load(n.xf[0], 0)
            load(n.xf[1], 1)
            sp.dma_start(wcl[:, :], Wc).then_inc(w_in, 16)
            sp.dma_start(bcb[:, :], bc.rearrange("(a c) -> a c", a=1).to_broadcast((P, C))).then_inc(w_in, 16)
            sp.dma_start(wgx[0:C, 0:HE], Wg).then_inc(w_in, 16)
            sp.dma_start(adb[:, :], att_d.rearrange("(a h) e -> a (h e)", a=1).to_broadcast((C, HE))).then_inc(w_in, 16)
            sp.wait_ge(z_out, 1)
            done = 0
            while done < M // P:
                cols = min(EC, M // P - done)
                sp.dma_start(n.pos.rearrange("(p t) a -> p (t a)", p=P)[:, done:done + cols], zero[:, 0:cols].bitcast(I32)).then_inc(z_out, 16)
                done += cols
            for k in range(NH):
                sp.dma_start(n.adend[1:1 + n.E, :].rearrange("(p j) c -> p (j c)", p=P)[:, k * EC:(k + 1) * EC], zero).then_inc(z_out, 16)
            sp.wait_ge(kv_out, 1)
            sp.dma_start(KK[1:P, 0:1], KV[0:P - 1, 0, EC - 1:EC]).then_inc(pv_in, 16)
            sp.dma_start(KK[0:P - 1, EC + 1:EC + 2], KV[1:P, 0, 0:1]).then_inc(pv_in, 16)
            with sp.Fori(0, B // 2) as ii:
                for par in range(2):
                    b = ii * 2 + par
                    one = lambda t: t[bass.ds(b, 1), :, :].rearrange("a c p -> (a c) p")
                    sp.wait_ge(v_x2, (b + 1) * NCH)
                    nb = b + 2
                    load(n.xf[bass.ds(nb % B, 1), :, :].rearrange("a c p -> (a c) p"), par)
                    sp.dma_start(one(n.x2), x2[0:C, :]).then_inc(o_x2, 16)
                    sp.wait_ge(v_ln, PRE + (b + 1) * NLN)
                    sp.dma_start(one(n.tn), th[:, :]).then_inc(o_x2, 16)
                    sp.wait_ge(v_h, (b + 1) * NHB + 1)
                    sp.dma_start(n.htab[bass.ds(b * NP, NP), :].rearrange("(q p) c -> p q c", p=P), hx[:, :, 0:HE]).then_inc(o_x2, 16)
                    sp.dma_start(n.adtab[bass.ds(b * NP, NP), :].rearrange("(q p) c -> p q c", p=P), hx[:, :, HE:HE + NH]).then_inc(o_x2, 16)
                    sp.wait_ge(o_x2, 64 * (b + 1))
                    sp.sem_inc(left, 1)
            for par in range(2):
                sp.wait_ge(x_in[par], 32 * (B // 2 + 1))

        @block.gpsimd
        def _(pool):
            done = [0]

            def step(ins):
                done[0] += 1
                ins.then_inc(pc, 1)
                pool.wait_ge(pc, done[0])
            step(pool.memset(mean[0:C, :, :], 1.0 / C))
            step(pool.memset(mean[C:P, :, :], 0.0))
            step(pool.memset(centre[C:P, :, :], 0.0))
            step(pool.memset(wcT[C:P, :], 0.0))
            step(pool.memset(wgx[C:P, :], 0.0))
            step(pool.memset(x2[C:P, :], 0.0))
            pool.tensor_tensor(centre[0:C, :, :], n.ident[0:C, 0:C].unsqueeze(1).to_broadcast([C, 2, C]), mean[0:C, :, :],
                               ALU.subtract).then_inc(const_ready, 1)
            pool.memset(epsc[:, 0:1], 1e-6).then_inc(const_ready, 1)
            pool.memset(epsc[:, 1:2], 1e-5).then_inc(const_ready, 1)
            pool.memset(zero, 0.0).then_inc(z_out, 1)
            pool.wait_ge(z_out, 1 + 16 * (NH + -(-(M // P) // EC)))
            step(pool.memset(KK[:, :], -1.0))
            step(pool.tensor_copy(KK[:, 1:EC + 1], KV[:, 0, :]))
            pool.sem_inc(kv_out, 1)
            step(pool.tensor_copy(n.dsti[:, :], KV[:, 0, :]))
            step(pool.tensor_copy(n.srci[:, :], KV[:, 1, :]))
            pool.wait_ge(pv_in, 32)
            step(pool.tensor_tensor(n.start[:, :], KK[:, 0:EC], KK[:, 1:EC + 1], ALU.subtract))
            step(pool.tensor_scalar(n.start[:, :], n.start[:, :], 0.0, None, ALU.is_equal))
            step(pool.tensor_scalar(n.start[:, :], n.start[:, :], -1.0, -NEG, ALU.add, ALU.mult))
            step(pool.tensor_tensor(DF[:, 0, :], KK[:, 1:EC + 1], KK[:, 2:EC + 2], ALU.subtract))
            step(pool.tensor_scalar(DF[:, 0, :], DF[:, 0, :], 0.0, None, ALU.is_equal))
            step(pool.tensor_scalar(DF[:, 1, :], DF[:, 0, :], FAR, None, ALU.mult))
            step(pool.tensor_tensor(DF[:, 1, :], DF[:, 1, :], KK[:, 1:EC + 1], ALU.add))
            step(pool.tensor_copy(endi, DF[:, 1, :]))
            step(pool.iota(posv, pattern=[[1, EC]], base=1, channel_multiplier=EC))
            step(pool.tensor_copy(DF[:, 1, :], posv))
            step(pool.tensor_scalar(DF[:, 0, :], DF[:, 0, :], FAR, None, ALU.mult))
            step(pool.tensor_tensor(DF[:, 1, :], DF[:, 1, :], DF[:, 0, :], ALU.add))
            pool.sem_inc(kv_out, 1)
            with pool.Fori(0, EC // (2 * SW)) as it:
                for par in range(2):
                    k = it * 2 + par
                    pool.tensor_copy(stage[:, par, 0, :], endi[:, bass.ds(k * SW, SW)]).then_inc(st, 1)
                    pool.tensor_copy(stage[:, par, 1, :], posv[:, bass.ds(k * SW, SW)]).then_inc(st, 1)
                    pool.wait_ge(st, k * 2 + 2)
                    pool.sem_inc(passed, 1)
                    for j in range(SW):
                        pool.indirect_dma_start(out=n.pos, out_offset=bass.IndirectOffsetOnAxis(ap=stage[:, par, 0, j:j + 1], axis=0),
                                                in_=stage[:, par, 1, j:j + 1], in_offset=None, bounds_check=M - 1,
                                                oob_is_err=False).then_inc(sc_out[par], 16)
                for par in range(2):
                    pool.wait_ge(sc_out[par], (it + 1) * 16 * SW)
                    pool.sem_inc(passed, 1)
            for par in range(2):
                pool.wait_ge(sc_out[par], 16 * EC // 2)
            with pool.Fori(0, B) as b:
                pool.wait_ge(o_x2, (b + 1) * 64)
                pool.sem_inc(passed, 1)
                pool.dma_start(pnode[:, :], n.pos[bass.ds(b * NP, NP), :].rearrange("(p t) a -> p (t a)", p=P)).then_inc(n_in, 16)
                pool.dma_start(anode[:, :, :], n.adtab[bass.ds(b * NP, NP), :].rearrange("(p t) c -> p t c", p=P)).then_inc(n_in, 16)
                pool.wait_ge(n_in, (b + 1) * 32)
                pool.sem_inc(passed, 1)
                for k, make in enumerate((
                        lambda: pool.tensor_copy(fnode[:, 0, :], pnode[:, :]),
                        lambda: pool.tensor_scalar(fnode[:, 1, :], fnode[:, 0, :], 0.0, FAR, ALU.is_equal, ALU.mult),
                        lambda: pool.tensor_tensor(fnode[:, 0, :], fnode[:, 0, :], fnode[:, 1, :], ALU.add),
                        lambda: pool.tensor_copy(inode[:, :], fnode[:, 0, :]))):
                    make().then_inc(nq, 1)
                    pool.wait_ge(nq, b * 4 + k + 1)
                    pool.sem_inc(passed, 1)
                for t in range(QT):
                    pool.indirect_dma_start(out=n.adend, out_offset=bass.IndirectOffsetOnAxis(ap=inode[:, t:t + 1], axis=0),
                                            in_=anode[:, t, :], in_offset=None, bounds_check=n.E, oob_is_err=False).then_inc(ad_out, 16)
                pool.wait_ge(ad_out, (b + 1) * 16 * QT)
                pool.sem_inc(passed, 1)

        def ln_at(b, c, post):
            if post:
                return PRE + b * NLN + min(2 * c + 2, NLN - 1)
            return PRE + b * NLN + max(2 * c - 1, 0)

        def by_act(t):
            return t - (t + 2) // 3 if isinstance(t, int) else t // 3 * 2

        def by_dve(t):
            return (t + 2) // 3 if isinstance(t, int) else t // 3

        def sums(dve, b, ii, par, c, link):
            o, w = CH[c]
            if c == 0:
                dve.wait_ge(left, b + 1)
            dve.wait_ge(pe_acc, b * STEPS + (c + 1) * QT)
            link(dve.tensor_tensor(half[:, 0:w], acc[c % 2][0:C, 0:w], xb[0:C, par, o:o + w], ALU.add))
            dve.tensor_tensor(x2[0:C, o:o + w], acc[c % 2][C:2 * C, 0:w], half[:, 0:w], ALU.add).then_inc(v_x2, 1)

        @block.tensor
        def _(pe):
            pe.wait_ge(const_ready, 3)
            pe.wait_ge(w_in, 64)
            pe.transpose(lnp[0][0:C, 0:C], wcl[:, :], n.ident[0:C, 0:C]).then_inc(wct_ps, 1)
            pe.wait_ge(w_ready, 2)

            def centring(k, src, c):
                o, w = CH[c]
                if not isinstance(k, int) or k:
                    pe.wait_ge(a_sq, k)
                pe.matmul(lnp[0][:, 0:w], centre[:, :, :].rearrange("p a c -> p (a c)"), src[:, o:o + w],
                          start=True, stop=True).then_inc(pe_cen, 1)

            def variance(k, c, pres):
                w = CH[c][1]
                pe.wait_ge(a_sq, k + 1)
                if not isinstance(k, int) or k:
                    pe.wait_ge(a_sd, k)
                    pe.wait_ge(v_n2, pres)
                pe.matmul(lnp[1][:, 0:w], mean[:, :, :].rearrange("p a c -> p (a c)"), sq[:, 0:w],
                          start=True, stop=True).then_inc(pe_var, 1)

            def values(b, gb):
                if gb:
                    pe.wait_ge(v_gt, b * GB + gb)
                for k in range(min(GPB, QT - gb * GPB)):
                    q = gb * GPB + k
                    last = pe.matmul(lnp[0][:, k * C:(k + 1) * C], xl[:, q * P:(q + 1) * P], wcT[:, :], start=True, stop=True)
                last.then_inc(pe_gt, 1)
            pe.wait_ge(x_in[0], 32)
            for c in range(NCH):
                centring(c, xb[:, 0, :], c)
                variance(c, c, c)
            pe.wait_ge(v_ln, NCH)
            for gb in range(GB):
                values(0, gb)
            with pe.Fori(0, B // 2) as ii:
                for par in range(2):
                    b = ii * 2 + par
                    pe.wait_ge(x_in[1 - par], (ii + 1 + par) * 32)
                    pe.wait_ge(v_gt, (b + 1) * GB)
                    for t in range(0, STEPS + LAG, 2):
                        c, q = divmod(t, QT)
                        if t < STEPS:
                            o, w = CH[c]
                            for k in (0, 1):
                                if t + k >= 4:
                                    pe.wait_ge(a_rel, b * STEPS + t + k - 3)
                                bank, pixels = gram[(t + k) % 4], slice((q + k) * P, (q + k + 1) * P)
                                pe.matmul(bank[:, 0:w], hl[:, par, pixels], hl[:, par, o:o + w], start=True, stop=False)
                                pe.matmul(bank[:, 0:w], lh[:, par, pixels], hl[:, par, o:o + w], start=False, stop=True).then_inc(pe_gram, 1)
                        u = t - LAG
                        if u >= 0:
                            cu, qu = divmod(u, QT)
                            w = CH[cu][1]
                            pe.wait_ge(v_s2, by_dve(b * STEPS) + by_dve(u + 2))
                            pe.wait_ge(a_s2, by_act(b * STEPS) + by_act(u + 2))
                            if cu >= 2 and qu == 0:
                                pe.wait_ge(v_x2, b * NCH + cu - 1)
                            for k in (0, 1):
                                h = C * k
                                pe.matmul(acc[cu % 2][h:h + C, 0:w], gT[:, par, qu + k, :], s2[:, (u + k) % SLOTS, 0:w], start=qu == 0,
                                          stop=qu == QT - 2).then_inc(pe_acc, 1)
                        if t < STEPS:
                            if q == 2:
                                centring(ln_at(b, c, 0), xb[:, 1 - par, :], c)
                            if q == 4:
                                if c == 0:
                                    pe.wait_ge(v_h, b * NHB + 1)
                                variance(ln_at(b, c, 0), c, PRE + b * NCH + c)
                            if q == 12 and c:
                                pe.wait_ge(v_x2, b * NCH + c)
                                centring(ln_at(b, c - 1, 1), x2, c - 1)
                            if q == 14 and c:
                                variance(ln_at(b, c - 1, 1), c - 1, PRE + b * NCH + c + 1)
                            if c == NCH - 1 and q in VALUES_AT:
                                if q == VALUES_AT[0]:
                                    pe.wait_ge(v_ln, ln_at(b, c, 0) + 1)
                                    pe.wait_ge(a_sq, ln_at(b, c - 1, 1) + 1)
                                values(b + 1, VALUES_AT.index(q))
                    for gb in range(len(VALUES_AT), GB):
                        values(b + 1, gb)
                    k = ln_at(b, NCH - 1, 1)
                    pe.wait_ge(v_gt, (b + 2) * GB)
                    pe.wait_ge(v_x2, (b + 1) * NCH)
                    centring(k, x2, NCH - 1)
                    variance(k, NCH - 1, PRE + (b + 1) * NCH)
                    pe.wait_ge(v_ln, k + 1)
                    for hb in range(NHB):
                        if hb:
                            pe.wait_ge(v_h, b * NHB + hb + 1)
                        for j in range(min(HPB, QT - hb * HPB)):
                            q = hb * HPB + j
                            last = pe.matmul(lnp[1][:, j * (HE + NH):(j + 1) * (HE + NH)], tf[:, q * P:(q + 1) * P],
                                             wgx[:, :], start=True, stop=True)
                        last.then_inc(pe_h, 1)

        @block.scalar
        def _(act):
            act.wait_ge(const_ready, 3)

            def centred(k, c, post, done=None):
                w = CH[c][1]
                act.wait_ge(pe_cen, k + 1)
                if done is not None:
                    act.wait_ge(v_ln, done)
                act.activation(cen[:, post, 0:w], lnp[0][:, 0:w], ACT.Copy)
                if not isinstance(k, int) or k:
                    act.wait_ge(pe_var, k)
                act.activation(sq[:, 0:w], lnp[0][:, 0:w], ACT.Square).then_inc(a_sq, 1)

            def deviation(k, c, post):
                w = CH[c][1]
                act.wait_ge(pe_var, k + 1)
                act.activation(sd[:, post, 0:w], lnp[1][:, 0:w], ACT.Sqrt, bias=epsc[:, post:post + 1]).then_inc(a_sd, 1)

            def norm(k, c):
                w = CH[c][1]
                act.wait_ge(v_n2, k + 1)
                act.activation(n2[:, 0:w], n2[:, 0:w], ACT.Sqrt).then_inc(a_nrm, 1)
            for c in range(NCH):
                centred(c, c, 0, c or None)
                deviation(c, c, 0)
                norm(c, c)

            def square(b, t):
                w = CH[t // QT][1]
                act.wait_ge(a_rel, b * STEPS + t + 1)
                if t >= SLOTS:
                    act.wait_ge(pe_acc, b * STEPS + t - SLOTS + 1)
                act.activation(s2[:, t % SLOTS, 0:w], rel[:, t % RELS, 0:w], ACT.Square).then_inc(a_s2, 1)
            with act.Fori(0, B // 2) as ii:
                for par in range(2):
                    b = ii * 2 + par
                    for t in range(STEPS):
                        c, q = divmod(t, QT)
                        w = CH[c][1]
                        act.wait_ge(pe_gram, b * STEPS + t + 1)
                        if t >= RELS and t % 3:
                            act.wait_ge(a_s2, by_act(b * STEPS) + by_act(t - RELS + 1))
                        elif t >= RELS:
                            act.wait_ge(v_s2, by_dve(b * STEPS) + by_dve(t - RELS + 1))
                        act.activation(rel[:, t % RELS, 0:w], gram[t % 4][:, 0:w], ACT.Relu, scale=1.0 / SPLIT ** 2).then_inc(a_rel, 1)
                        if t and (t - 1) % 3:
                            square(b, t - 1)
                        if q == 3:
                            k = ln_at(b, c, 0)
                            centred(k, c, 0, None if c == 0 else k - (c > 1))
                        if q == 5:
                            deviation(ln_at(b, c, 0), c, 0)
                        if q == 12:
                            norm(PRE + b * NCH + c, c)
                            if c:
                                k = ln_at(b, c - 1, 1)
                                centred(k, c - 1, 1, k - 1)
                        if q == 15 and c:
                            deviation(ln_at(b, c - 1, 1), c - 1, 1)
                    square(b, STEPS - 1)
                    centred(ln_at(b, NCH - 1, 1), NCH - 1, 1, ln_at(b, NCH - 1, 1))
                    deviation(ln_at(b, NCH - 1, 1), NCH - 1, 1)

        @block.vector
        def _(dve):
            dve.sem_inc(left, 1)
            dve.sem_inc(v_h, 1)
            dve.wait_ge(w_in, 64)
            dve.wait_ge(wct_ps, 1)
            dve.wait_ge(const_ready, 3)
            dve.tensor_copy(wcT[0:C, :], lnp[0][0:C, 0:C]).then_inc(w_ready, 1)
            dve.tensor_tensor(wad[:, :], wgx[0:C, 0:HE], adb[:, :], ALU.mult).then_inc(vc, 1)
            dve.wait_ge(vc, 1)
            dve.tensor_reduce(wgx[0:C, HE:HE + NH], wad[:, :].rearrange("p (h e) -> p h e", e=NX), AX.X, ALU.add).then_inc(w_ready, 1)
            PRE_LINKS, POST_LINKS = 6, 2
            IMAGE_LINKS = NCH * (PRE_LINKS + POST_LINKS + 1)
            base = [1, 0]

            def link(ins):
                base[1] += 1
                ins.then_inc(vc, 1)
                dve.wait_ge(vc, base[0] + base[1])

            def pre_norm(k, kn, c):
                o, w = CH[c]
                dve.wait_ge(a_sd, k + 1)
                link(dve.reciprocal(rstd[:, 0:w], sd[:, 0, 0:w]))
                link(dve.tensor_tensor(r2[:, 0:w], rstd[:, 0:w], rstd[:, 0:w], ALU.mult))
                link(dve.scalar_tensor_tensor(n2[:, 0:w], lnp[1][:, 0:w], float(C), r2[:, 0:w], ALU.mult, ALU.mult))
                dve.tensor_scalar(n2[:, 0:w], n2[:, 0:w], 1e-16, None, ALU.max).then_inc(v_n2, 1)
                link(dve.tensor_tensor(xl[:, o:o + w], cen[:, 0, 0:w], rstd[:, 0:w], ALU.mult))

            def pre_unit(kn, c, slot):
                o, w = CH[c]
                dve.wait_ge(a_nrm, kn + 1)
                link(dve.reciprocal(r2[:, 0:w], n2[:, 0:w]))
                link(dve.tensor_tensor(xn[:, 0:w], xl[:, o:o + w], r2[:, 0:w], ALU.mult))
                dve.tensor_scalar(hl[0:C, slot, o:o + w], xn[0:C, 0:w], SPLIT, None, ALU.mult)
                dve.tensor_scalar(lh[C:P, slot, o:o + w], xn[C:P, 0:w], SPLIT, None, ALU.mult).then_inc(v_hi, 1)
                dve.wait_ge(v_hi, kn + 1)
                dve.scalar_tensor_tensor(lh[0:C, slot, o:o + w], xn[0:C, 0:w], SPLIT, hl[0:C, slot, o:o + w], ALU.mult, ALU.subtract)
                dve.scalar_tensor_tensor(hl[C:P, slot, o:o + w], xn[C:P, 0:w], SPLIT, lh[C:P, slot, o:o + w], ALU.mult,
                                         ALU.subtract).then_inc(v_ln, 1)

            def post(k, b, c):
                o, w = CH[c]
                dve.wait_ge(a_sd, k + 1)
                link(dve.reciprocal(rstd[:, 0:w], sd[:, 1, 0:w]))
                link(dve.tensor_tensor(tf[:, o:o + w], cen[:, 1, 0:w], rstd[:, 0:w], ALU.mult))
                dve.tensor_scalar(th[:, o:o + w], tf[:, o:o + w], SPLIT, None, ALU.mult).then_inc(v_th, 1)
                dve.wait_ge(v_th, b * NCH + c + 1)
                dve.scalar_tensor_tensor(th[C:P, o:o + w], tf[C:P, o:o + w], SPLIT, th[C:P, o:o + w], ALU.mult,
                                         ALU.subtract).then_inc(v_ln, 1)

            def values(b, gb, slot):
                k = min(GPB, QT - gb * GPB)
                dve.wait_ge(pe_gt, b * GB + gb + 1)
                dve.tensor_tensor(gT[:, slot, gb * GPB:gb * GPB + k, :], lnp[0][:, 0:k * C].rearrange("p (k c) -> p k c", c=C),
                                  bcb[:, :].unsqueeze(1).to_broadcast([P, k, C]), ALU.add).then_inc(v_gt, 1)
            for c in range(NCH):
                pre_norm(c, c, c)
                pre_unit(c, c, 0)
            for gb in range(GB):
                values(0, gb, 0)
            base[0] += base[1]
            first = base[0]
            with dve.Fori(0, B // 2) as ii:
                for par in range(2):
                    b = ii * 2 + par
                    base[0], base[1] = b * IMAGE_LINKS + first, 0
                    for t in range(STEPS):
                        c, q = divmod(t, QT)
                        w = CH[c][1]
                        if t % 3 == 0:
                            dve.wait_ge(a_rel, b * STEPS + t + 1)
                            if t >= SLOTS:
                                dve.wait_ge(pe_acc, b * STEPS + t - SLOTS + 1)
                            dve.tensor_tensor(s2[:, t % SLOTS, 0:w], rel[:, t % RELS, 0:w], rel[:, t % RELS, 0:w], ALU.mult).then_inc(v_s2, 1)
                        if q == 6 and c:
                            sums(dve, b, ii, par, c - 1, link)
                        if q == 8:
                            pre_norm(ln_at(b, c, 0), PRE + b * NCH + c, c)
                        if q == 13:
                            pre_unit(PRE + b * NCH + c, c, 1 - par)
                        if q == 16 and c:
                            post(ln_at(b, c - 1, 1), b, c - 1)
                        if c == NCH - 1 and q - 1 in VALUES_AT:
                            values(b + 1, VALUES_AT.index(q - 1), 1 - par)
                        if t == STEPS - 1:
                            for gb in range(len(VALUES_AT), GB):
                                values(b + 1, gb, 1 - par)
                    sums(dve, b, ii, par, NCH - 1, link)
                    post(ln_at(b, NCH - 1, 1), b, NCH - 1)
                    for hb in range(NHB):
                        k = min(HPB, QT - hb * HPB)
                        dve.wait_ge(pe_h, b * NHB + hb + 1)
                        dve.tensor_copy(hx[:, hb * HPB:hb * HPB + k, :], lnp[1][:, 0:k * (HE + NH)].rearrange("p (k c) -> p k c", c=HE + NH)).then_inc(v_h, 1)
                    assert base[1] == IMAGE_LINKS, base
            dve.wait_ge(kv_out, 2)
            dve.tensor_reduce(n.single[:, 0:1], n.start[:, 1:EC], AX.X, ALU.min)
            dve.tensor_copy(n.single[:, 1:2], n.start[:, 0:1])
            dve.tensor_reduce(n.single[:, 2:3], DF[:, 1, :], AX.X, ALU.min)


def segments(nc, n, att_s):
    HE, NH, NX, EC, M, ROW, E = n.HE, n.NH, n.NX, n.EC, n.M, n.ROW, n.E
    NC5 = NH * (NX + 1)
    CW = min(64, EC // 2)
    NK = EC // CW
    with ExitStack() as ctx:
        def sb(name, shape, dt=F32):
            return ctx.enter_context(nc.sbuf_tensor(name, shape, dt))

        def sem(name):
            return ctx.enter_context(nc.semaphore(name))
        rows = sb("rows", [P, 2, CW, ROW])
        idx = sb("idx", [P, 2, CW], I32)
        adend = sb("adend", [P, EC, NH])
        keep = sb("keep", [P, EC])
        ad = sb("ad", [P, NH, EC])
        attb = sb("attb", [P, HE])
        stc = sb("stc", [P, CW])
        prod = sb("prod", [P, CW, HE])
        asr = sb("asr", [P, CW, NH])
        ee = sb("ee", [P, CW, NH])
        D0 = sb("D0", [P, NH, CW + 1])
        D1 = sb("D1", [P, NH, CW + 1])
        MF = sb("MF", [P, NH, CW + 1])
        X = sb("X", [P, 2, NH, CW])
        FX = sb("FX", [P, 2, NH, CW])
        G0 = sb("G0", [P, NH, NX + 1, CW + 1])
        G1 = sb("G1", [P, NH, NX + 1, CW + 1])
        S = sb("S", [P, NH, NX + 1, CW + 1])
        empty = sb("empty", [1, ROW])
        tails = sb("tails", [P, 3, NC5])
        rt = sb("rt", [NC5, 3, P])
        Mo = sb("Mo", [NC5, P + 1])
        ex = sb("ex", [NC5, 2, P])
        ea = sb("ea", [NC5, 2, P])
        So = sb("So", [NC5, P + 1])
        carry = sb("carry", [P, 2, NC5])
        fidx = sb("fidx", [P, 2])
        fi = sb("fi", [P, 2], I32)
        fix = sb("fix", [P, ROW])
        fixo = sb("fixo", [P, ROW])
        mm = sb("mm", [P, 3, NH])
        me = sb("me", [P, 2, NH])
        part = sb("part", [P, 2, NC5])
        a_in = sem("a_in")
        ends_in = sem("ends_in")
        last_in = sem("last_in")
        ad_ready = sem("ad_ready")
        slot_free = sem("slot_free")
        ist = sem("ist")
        passed = sem("spassed")
        rows_in = [sem("rows_in0"), sem("rows_in1")]
        vq = sem("vq")
        v_x = sem("v_x")
        a_x = sem("a_x")
        v_rows = sem("v_rows")
        rows_out = sem("rows_out")
        e_out = sem("e_out")
        v_tails = sem("v_tails")
        bounce = sem("bounce")
        v_car = sem("v_car")
        v_fi = sem("v_fi")
        fix_in = sem("fix_in")
        v_fixo = sem("v_fixo")
        fix_out = sem("fix_out")
        block = ctx.enter_context(nc.Block())
        segv = n.seg[1:1 + E, :].rearrange("(p j) c -> p j c", p=P)
        rowt = n.row[:, 0:3 * NC5]
        rowc = n.row[:, 3 * NC5:5 * NC5]

        @block.sync
        def _(sp):
            sp.dma_start(attb[:, :], att_s.rearrange("(a h) e -> a (h e)", a=1).to_broadcast((P, HE))).then_inc(a_in, 16)
            sp.dma_start(adend[:, :, :], n.adend[1:1 + E, :].rearrange("(p j) c -> p j c", p=P)).then_inc(ends_in, 16)
            sp.wait_ge(e_out, 1)
            sp.dma_start(n.seg[0:1, :], empty[:, :]).then_inc(e_out, 16)
            with sp.Fori(0, NK // 2) as it:
                for par in range(2):
                    k = it * 2 + par
                    sp.wait_ge(v_rows, k + 1)
                    sp.dma_start(segv[:, bass.ds(k * CW, CW), :].rearrange("p j c -> p (j c)"),
                                 rows[:, par, :, :].rearrange("p j c -> p (j c)")).then_inc(rows_out, 16)
                    sp.wait_ge(rows_out, k * 16 + 16)
                    sp.sem_inc(slot_free, 1)
            sp.wait_ge(e_out, 17)
            sp.wait_ge(v_tails, 1)
            sp.dma_start(rowt, tails[:, :, :].rearrange("p k c -> p (k c)")).then_inc(bounce, 16)
            sp.wait_ge(bounce, 16)
            for k in range(3):
                sp.dma_start(rt[:, k, :], n.row[:, k * NC5:(k + 1) * NC5].rearrange("p c -> c p"), allow_slow_non_contiguous=True).then_inc(bounce, 16)
            sp.wait_ge(v_car, 1)
            sp.dma_start(n.row[:, 3 * NC5:4 * NC5].rearrange("p c -> c p"), So[:, 0:P], allow_slow_non_contiguous=True).then_inc(bounce, 16)
            sp.dma_start(n.row[:, 4 * NC5:5 * NC5].rearrange("p c -> c p"), Mo[:, 0:P], allow_slow_non_contiguous=True).then_inc(bounce, 16)
            sp.wait_ge(bounce, 96)
            sp.dma_start(carry[:, :, :].rearrange("p k c -> p (k c)"), rowc).then_inc(bounce, 16)

        @block.gpsimd
        def _(pool):
            pool.memset(empty[:, 0:NC5], 0.0)
            pool.memset(empty[:, NC5:ROW], NEG).then_inc(e_out, 1)
            pool.memset(fix[:, :], 0.0)
            pool.wait_ge(ends_in, 16)
            pool.indirect_dma_start(out=adend[:, EC - 1, :], out_offset=None, in_=n.adtab,
                                    in_offset=bass.IndirectOffsetOnAxis(ap=n.dsti[:, EC - 1:EC], axis=0)).then_inc(last_in, 16)
            with pool.Fori(0, NK // 2) as it:
                for par in range(2):
                    k = it * 2 + par
                    pool.wait_ge(slot_free, k + 1)
                    pool.sem_inc(passed, 1)
                    pool.tensor_copy(idx[:, par, :], n.srci[:, bass.ds(k * CW, CW)]).then_inc(ist, 1)
                    pool.wait_ge(ist, k + 1)
                    pool.sem_inc(passed, 1)
                    for j in range(CW):
                        pool.indirect_dma_start(out=rows[:, par, j, 0:HE], out_offset=None, in_=n.htab,
                                                in_offset=bass.IndirectOffsetOnAxis(ap=idx[:, par, j:j + 1], axis=0)).then_inc(rows_in[par], 16)
            pool.wait_ge(v_fi, 1)
            pool.wait_ge(rows_out, 16 * NK)
            pool.indirect_dma_start(out=fix[:, :], out_offset=None, in_=n.seg,
                                    in_offset=bass.IndirectOffsetOnAxis(ap=fi[:, 0:1], axis=0),
                                    bounds_check=E, oob_is_err=False).then_inc(fix_in, 16)
            pool.wait_ge(v_fixo, 1)
            pool.indirect_dma_start(out=n.seg, out_offset=bass.IndirectOffsetOnAxis(ap=fi[:, 1:2], axis=0),
                                    in_=fixo[:, :], in_offset=None,
                                    bounds_check=E, oob_is_err=False).then_inc(fix_out, 16)
            pool.wait_ge(fix_out, 16)

        @block.scalar
        def _(act):
            with act.Fori(0, NK) as k:
                act.wait_ge(v_x, k + 1)
                act.activation(FX[:, :, :, :].rearrange("p a h j -> p (a h j)"), X[:, :, :, :].rearrange("p a h j -> p (a h j)"), ACT.Exp).then_inc(a_x, 1)
            act.wait_ge(v_x, NK + 1)
            act.activation(ea[:, :, :].rearrange("c a p -> c (a p)"), ex[:, :, :].rearrange("c a p -> c (a p)"), ACT.Exp).then_inc(a_x, 1)
            act.wait_ge(v_x, NK + 2)
            act.activation(me[:, :, :].rearrange("p a h -> p (a h)"), mm[:, 1:3, :].rearrange("p a h -> p (a h)"), ACT.Exp).then_inc(a_x, 1)

        @block.vector
        def _(dve):
            dve.memset(D0[:, :, 0:1], NEG)
            dve.memset(MF[:, :, CW:CW + 1], NEG)
            dve.memset(G0[:, :, :, 0:1], 0.0)
            dve.memset(Mo[:, 0:1], NEG)
            dve.memset(So[:, 0:1], 0.0)
            dve.memset(S[:, :, :, CW:CW + 1], 0.0).then_inc(slot_free, 2)
            dve.wait_ge(slot_free, 2)
            dve.wait_ge(a_in, 16)
            dve.memset(keep[:, EC - 1:EC], 0.0)
            dve.tensor_scalar(keep[:, 0:EC - 1], n.start[:, 1:EC], 0.5 * NEG, None, ALU.is_gt).then_inc(ad_ready, 1)
            dve.wait_ge(ad_ready, 1)
            dve.wait_ge(ends_in, 16)
            dve.wait_ge(last_in, 16)
            for h in range(NH):
                dve.tensor_tensor_scan(ad[:, h, ::-1], keep[:, ::-1], adend[:, ::-1, h], 0.0, ALU.mult, ALU.add).then_inc(ad_ready, 1)
            dve.wait_ge(ad_ready, 1 + NH)
            NL = 10
            with dve.Fori(0, NK // 2) as it:
                for par in range(2):
                    k = it * 2 + par
                    cnt = [0]

                    def link(ins):
                        cnt[0] += 1
                        ins.then_inc(vq, 1)
                        dve.wait_ge(vq, k * NL + cnt[0])
                    dve.tensor_copy(D1[:, :, 0:1], MF[:, :, CW:CW + 1])
                    dve.tensor_copy(G1[:, :, :, 0:1], S[:, :, :, CW:CW + 1])
                    link(dve.tensor_copy(stc[:, :], n.start[:, bass.ds(k * CW, CW)]))
                    dve.tensor_copy(D0[:, :, 1:CW + 1], stc[:, :].unsqueeze(1).to_broadcast([P, NH, CW]))
                    dve.wait_ge(rows_in[par], (it + 1) * 16 * CW)
                    r = rows[:, par, :, :]
                    link(dve.tensor_tensor(prod[:, :, :], r[:, :, 0:HE], attb[:, :].unsqueeze(1).to_broadcast([P, CW, HE]), ALU.mult))
                    link(dve.tensor_reduce(asr[:, :, :], prod[:, :, :].rearrange("p j (h e) -> p j h e", e=NX), AX.X, ALU.add))
                    link(dve.tensor_tensor(ee[:, :, :], asr[:, :, :], ad[:, :, bass.ds(k * CW, CW)].rearrange("p h j -> p j h"), ALU.add))
                    link(dve.scalar_tensor_tensor(D1[:, :, 1:CW + 1].rearrange("p h j -> p j h"), ee[:, :, :], 0.2, ee[:, :, :], ALU.mult, ALU.max))
                    link(dve.tensor_tensor_scan(MF[:, :, :].rearrange("p h j -> p (h j)"), D0[:, :, :].rearrange("p h j -> p (h j)"),
                                                D1[:, :, :].rearrange("p h j -> p (h j)"), NEG, ALU.add, ALU.max))
                    link(dve.tensor_tensor(X[:, 0, :, :], MF[:, :, 0:CW], D0[:, :, 1:CW + 1], ALU.add))
                    link(dve.tensor_tensor(X[:, 0, :, :], X[:, 0, :, :], MF[:, :, 1:CW + 1], ALU.subtract))
                    dve.tensor_tensor(X[:, 1, :, :], D1[:, :, 1:CW + 1], MF[:, :, 1:CW + 1], ALU.subtract).then_inc(v_x, 1)
                    dve.wait_ge(a_x, k + 1)
                    dve.tensor_copy(G0[:, :, :, 1:CW + 1], FX[:, 0, :, :].unsqueeze(2).to_broadcast([P, NH, NX + 1, CW]))
                    dve.tensor_copy(G1[:, :, NX, 1:CW + 1], FX[:, 1, :, :])
                    for h in range(NH):
                        last = dve.tensor_tensor(G1[:, h, 0:NX, 1:CW + 1], r[:, :, h * NX:(h + 1) * NX].rearrange("p j e -> p e j"),
                                                 FX[:, 1, h, :].unsqueeze(1).to_broadcast([P, NX, CW]), ALU.mult)
                    link(last)
                    link(dve.tensor_tensor_scan(S[:, :, :, :].rearrange("p h e j -> p (h e j)"), G0[:, :, :, :].rearrange("p h e j -> p (h e j)"),
                                                G1[:, :, :, :].rearrange("p h e j -> p (h e j)"), 0.0, ALU.mult, ALU.add))
                    dve.tensor_copy(r[:, :, 0:NC5], S[:, :, :, :].rearrange("p h e j -> p (h e) j")[:, :, 1:CW + 1].rearrange("p c j -> p j c"))
                    dve.tensor_copy(r[:, :, NC5:ROW], MF[:, :, 1:CW + 1].rearrange("p h j -> p j h")).then_inc(v_rows, 1)
                    dve.wait_ge(v_rows, k + 1)
                    assert cnt[0] == NL, cnt
            done = [NK * NL]

            def step(ins):
                done[0] += 1
                ins.then_inc(vq, 1)
                dve.wait_ge(vq, done[0])
            dve.tensor_copy(tails[:, 0, :], S[:, :, :, CW:CW + 1].rearrange("p h e a -> p (h e a)"))
            for e in range(NX + 1):
                dve.tensor_copy(tails[:, 1, e::NX + 1], MF[:, :, CW:CW + 1].rearrange("p h a -> p (h a)"))
            step(dve.tensor_tensor(fidx[:, 0:1], n.single[:, 0:1], n.single[:, 1:2], ALU.min))
            dve.tensor_copy(tails[:, 2, :], fidx[:, 0:1].to_broadcast([P, NC5])).then_inc(v_tails, 1)
            step(dve.tensor_scalar(fidx[:, 1:2], n.single[:, 1:2], FAR / NEG, None, ALU.mult))
            step(dve.tensor_tensor(fidx[:, 1:2], fidx[:, 1:2], n.single[:, 2:3], ALU.add))
            dve.tensor_copy(fi[:, 0:1], n.single[:, 2:3])
            dve.tensor_copy(fi[:, 1:2], fidx[:, 1:2]).then_inc(v_fi, 1)
            dve.wait_ge(bounce, 64)
            step(dve.tensor_tensor_scan(Mo[:, 1:P + 1], rt[:, 2, :], rt[:, 1, :], NEG, ALU.add, ALU.max))
            step(dve.tensor_tensor(ex[:, 0, :], Mo[:, 0:P], rt[:, 2, :], ALU.add))
            step(dve.tensor_tensor(ex[:, 0, :], ex[:, 0, :], Mo[:, 1:P + 1], ALU.subtract))
            dve.tensor_tensor(ex[:, 1, :], rt[:, 1, :], Mo[:, 1:P + 1], ALU.subtract).then_inc(v_x, 1)
            dve.wait_ge(a_x, NK + 1)
            step(dve.tensor_tensor(ea[:, 1, :], ea[:, 1, :], rt[:, 0, :], ALU.mult))
            dve.tensor_tensor_scan(So[:, 1:P + 1], ea[:, 0, :], ea[:, 1, :], 0.0, ALU.mult, ALU.add).then_inc(v_car, 1)
            dve.wait_ge(bounce, 112)
            dve.wait_ge(fix_in, 16)
            step(dve.tensor_tensor(mm[:, 0, :], fix[:, NC5:ROW], carry[:, 1, ::NX + 1], ALU.max))
            dve.tensor_tensor(mm[:, 1, :], fix[:, NC5:ROW], mm[:, 0, :], ALU.subtract)
            dve.tensor_tensor(mm[:, 2, :], carry[:, 1, ::NX + 1], mm[:, 0, :], ALU.subtract).then_inc(v_x, 1)
            dve.tensor_copy(fixo[:, NC5:ROW], mm[:, 0, :])
            dve.wait_ge(a_x, NK + 2)
            v5 = "p (h e) -> p h e"
            dve.tensor_tensor(part[:, 0, :].rearrange(v5, h=NH), fix[:, 0:NC5].rearrange(v5, h=NH),
                              me[:, 0, :].unsqueeze(2).to_broadcast([P, NH, NX + 1]), ALU.mult)
            step(dve.tensor_tensor(part[:, 1, :].rearrange(v5, h=NH), carry[:, 0, :].rearrange(v5, h=NH),
                                   me[:, 1, :].unsqueeze(2).to_broadcast([P, NH, NX + 1]), ALU.mult))
            dve.tensor_tensor(fixo[:, 0:NC5], part[:, 0, :], part[:, 1, :], ALU.add).then_inc(v_fixo, 1)


def gates(nc, n, att_s, att_d, b_gat, gamma, beta):
    HE, NH, NX, M, ROW, NT = n.HE, n.NH, n.NX, n.M, n.ROW, n.NT
    NC5 = NH * (NX + 1)
    TW = 48 if NT % 96 == 0 else NT // 2
    NK = NT // TW
    with ExitStack() as ctx:
        def sb(name, shape, dt=F32):
            return ctx.enter_context(nc.sbuf_tensor(name, shape, dt))

        def sem(name):
            return ctx.enter_context(nc.semaphore(name))
        pos = sb("pos", [P, NT], I32)
        idx = sb("nidx", [P, 2, TW], I32)
        R = sb("R", [P, 2, TW, ROW])
        Hn = sb("Hn", [P, 2, TW, HE])
        AD = sb("AD", [P, 2, TW, NH])
        cst = sb("cst", [P, 4, HE])
        low = sb("low", [P, NX, NX])
        high = sb("high", [P, NX, NX])
        T0 = sb("T0", [P, TW, HE])
        T1 = sb("T1", [P, TW, HE])
        T2 = sb("T2", [P, TW, HE])
        U0 = sb("U0", [P, TW, NH])
        U1 = sb("U1", [P, TW, NH])
        MX = sb("MX", [P, TW, NH])
        X = sb("Xg", [P, 2, TW, NH])
        FX = sb("FXg", [P, 2, TW, NH])
        dn = sb("dn", [P, TW, NH])
        s1 = sb("s1", [P, TW])
        s3 = sb("s3", [P, TW])
        s4 = sb("s4", [P, TW])
        sc = sb("sc", [P, TW, NX])
        es = sb("es", [P, TW, NX])
        xs = sb("xs", [P, TW, NX])
        G = sb("G", [P, NX, TW])
        GH = sb("GH", [P, 2, 2 * NX, TW], F16)
        eps = sb("epsg", [P, 1])
        c_in = sem("gc_in")
        ist = sem("gist")
        passed = sem("gpassed")
        slot_free = sem("gslot_free")
        r_in = [sem("r_in0"), sem("r_in1")]
        h_in = [sem("h_in0"), sem("h_in1")]
        vq = sem("gvq")
        v_x = sem("gv_x")
        a_x = sem("ga_x")
        v_g = sem("v_g")
        g_out = sem("g_out")
        g_left = sem("g_left")
        m_rdy = sem("m_rdy")
        block = ctx.enter_context(nc.Block())
        hv = n.htab.rearrange("(p t) c -> p t c", p=P)
        av = n.adtab.rearrange("(p t) c -> p t c", p=P)
        gv = n.gates.rearrange("e (p t) -> p e t", p=P)

        @block.sync
        def _(sp):
            sp.dma_start(pos[:, :], n.pos.rearrange("(p t) a -> p (t a)", p=P)).then_inc(c_in, 16)
            sp.dma_start(cst[:, 0, :], att_s.rearrange("(a h) e -> a (h e)", a=1).to_broadcast((P, HE))).then_inc(c_in, 16)
            for k, v in ((1, b_gat), (2, gamma), (3, beta)):
                sp.dma_start(cst[:, k, :], v.rearrange("(a c) -> a c", a=1).to_broadcast((P, HE))).then_inc(c_in, 16)
            with sp.Fori(0, NK // 2) as it:
                for par in range(2):
                    k = it * 2 + par
                    sp.wait_ge(slot_free, k + 1)
                    sp.dma_start(Hn[:, par, :, :], hv[:, bass.ds(k * TW, TW), :]).then_inc(h_in[par], 16)
                    sp.dma_start(AD[:, par, :, :], av[:, bass.ds(k * TW, TW), :]).then_inc(h_in[par], 16)

        @block.gpsimd
        def _(pool):
            pool.memset(low[:, :, :], 0.0)
            pool.memset(high[:, :, :], 0.0).then_inc(m_rdy, 1)
            pool.memset(eps[:, :], 1e-5)
            pool.wait_ge(m_rdy, 1)
            for i in range(NX - 1):
                pool.memset(low[:, i + 1, 0:i + 1], 1.0)
                pool.memset(high[:, i, i + 1:NX], 1.0).then_inc(m_rdy, 1)
            pool.wait_ge(c_in, 80)
            with pool.Fori(0, NK // 2) as it:
                for par in range(2):
                    k = it * 2 + par
                    pool.wait_ge(slot_free, k + 1)
                    pool.sem_inc(passed, 1)
                    pool.tensor_copy(idx[:, par, :], pos[:, bass.ds(k * TW, TW)]).then_inc(ist, 1)
                    pool.wait_ge(ist, k + 1)
                    pool.sem_inc(passed, 1)
                    for j in range(TW):
                        pool.indirect_dma_start(out=R[:, par, j, :], out_offset=None, in_=n.seg,
                                                in_offset=bass.IndirectOffsetOnAxis(ap=idx[:, par, j:j + 1], axis=0)).then_inc(r_in[par], 16)

        @block.scalar
        def _(act):
            act.wait_ge(m_rdy, NX)
            with act.Fori(0, NK // 2) as it:
                for par in range(2):
                    k = it * 2 + par
                    act.wait_ge(v_x, k * 3 + 1)
                    act.activation(FX[:, :, :, :].rearrange("p a t h -> p (a t h)"), X[:, :, :, :].rearrange("p a t h -> p (a t h)"), ACT.Exp).then_inc(a_x, 1)
                    act.wait_ge(v_x, k * 3 + 2)
                    act.activation(s3[:, :], s1[:, :], ACT.Sqrt, bias=eps[:, 0:1], scale=1.0 / HE).then_inc(a_x, 1)
                    act.wait_ge(v_x, k * 3 + 3)
                    act.activation(es[:, :, :], xs[:, :, :], ACT.Exp).then_inc(a_x, 1)
                    act.wait_ge(v_g, k + 1)
                    act.dma_start(gv[:, :, bass.ds(k * TW, TW)], GH[:, par, :, :]).then_inc(g_out, 16)
                act.wait_ge(g_out, (it + 1) * 32)
                act.sem_inc(g_left, 1)

        @block.vector
        def _(dve):
            dve.wait_ge(m_rdy, NX)
            dve.wait_ge(c_in, 80)
            dve.memset(s1[:, :], 0.0).then_inc(slot_free, 2)
            dve.sem_inc(g_left, 1)
            bc = lambda k: cst[:, k, :].unsqueeze(1).to_broadcast([P, TW, HE])
            hx = lambda ap: ap.unsqueeze(3).to_broadcast([P, TW, NH, NX])
            v4 = lambda ap: ap.rearrange("p t (h e) -> p t h e", e=NX)
            bt = lambda ap: ap.unsqueeze(2).to_broadcast([P, TW, HE])
            b4 = lambda ap: ap.unsqueeze(2).to_broadcast([P, TW, NX])
            NL = 31
            with dve.Fori(0, NK // 2) as it:
                for par in range(2):
                    k = it * 2 + par
                    cnt = [0]

                    def link(ins):
                        cnt[0] += 1
                        ins.then_inc(vq, 1)
                        dve.wait_ge(vq, k * NL + cnt[0])
                    dve.wait_ge(h_in[par], (it + 1) * 32)
                    dve.wait_ge(r_in[par], (it + 1) * 16 * TW)
                    dve.wait_ge(g_left, it + 1)
                    r = R[:, par, :, :]
                    r5 = r[:, :, 0:NC5].rearrange("p t (h e) -> p t h e", h=NH)
                    link(dve.tensor_tensor(T0[:, :, :], Hn[:, par, :, :], bc(0), ALU.mult))
                    link(dve.tensor_reduce(U0[:, :, :], v4(T0[:, :, :]), AX.X, ALU.add))
                    link(dve.tensor_tensor(U0[:, :, :], U0[:, :, :], AD[:, par, :, :], ALU.add))
                    link(dve.scalar_tensor_tensor(U1[:, :, :], U0[:, :, :], 0.2, U0[:, :, :], ALU.mult, ALU.max))
                    link(dve.tensor_tensor(MX[:, :, :], r[:, :, NC5:ROW], U1[:, :, :], ALU.max))
                    dve.tensor_tensor(X[:, 0, :, :], r[:, :, NC5:ROW], MX[:, :, :], ALU.subtract)
                    dve.tensor_tensor(X[:, 1, :, :], U1[:, :, :], MX[:, :, :], ALU.subtract).then_inc(v_x, 1)
                    dve.wait_ge(a_x, k * 3 + 1)
                    link(dve.tensor_tensor(dn[:, :, :], r5[:, :, :, NX], FX[:, 0, :, :], ALU.mult))
                    link(dve.scalar_tensor_tensor(dn[:, :, :], FX[:, 1, :, :], 1e-16, dn[:, :, :], ALU.add, ALU.add))
                    dve.tensor_tensor(v4(T0[:, :, :]), r5[:, :, :, 0:NX], hx(FX[:, 0, :, :]), ALU.mult)
                    dve.tensor_tensor(v4(T1[:, :, :]), v4(Hn[:, par, :, :]), hx(FX[:, 1, :, :]), ALU.mult)
                    link(dve.reciprocal(U0[:, :, :], dn[:, :, :]))
                    link(dve.tensor_tensor(T0[:, :, :], T0[:, :, :], T1[:, :, :], ALU.add))
                    link(dve.tensor_tensor(v4(T0[:, :, :]), v4(T0[:, :, :]), hx(U0[:, :, :]), ALU.mult))
                    link(dve.tensor_tensor(T0[:, :, :], T0[:, :, :], bc(1), ALU.add))
                    link(dve.tensor_reduce(s1[:, :], T0[:, :, :], AX.X, ALU.add))
                    link(dve.tensor_scalar(s4[:, :], s1[:, :], 1.0 / HE, None, ALU.mult))
                    link(dve.tensor_tensor(T1[:, :, :], T0[:, :, :], bt(s4[:, :]), ALU.subtract))
                    link(dve.tensor_tensor(T2[:, :, :], T1[:, :, :], T1[:, :, :], ALU.mult))
                    dve.tensor_reduce(s1[:, :], T2[:, :, :], AX.X, ALU.add).then_inc(v_x, 1)
                    dve.wait_ge(a_x, k * 3 + 2)
                    link(dve.reciprocal(s4[:, :], s3[:, :]))
                    link(dve.tensor_tensor(T1[:, :, :], T1[:, :, :], bt(s4[:, :]), ALU.mult))
                    link(dve.tensor_tensor(T1[:, :, :], T1[:, :, :], bc(2), ALU.mult))
                    link(dve.tensor_tensor(T1[:, :, :], T1[:, :, :], bc(3), ALU.add))
                    link(dve.tensor_reduce(xs[:, :, :], T1[:, :, :].rearrange("p t (h e) -> p t e h", e=NX), AX.X, ALU.add))
                    link(dve.tensor_scalar(sc[:, :, :], xs[:, :, :], 1.0 / NH, None, ALU.mult))
                    si = sc[:, :, :].unsqueeze(3).to_broadcast([P, TW, NX, NX])
                    sj = sc[:, :, :].unsqueeze(2).to_broadcast([P, TW, NX, NX])
                    dve.tensor_tensor(v4(T0[:, :, :]), sj, si, ALU.is_ge)
                    link(dve.tensor_tensor(v4(T1[:, :, :]), sj, si, ALU.is_gt))
                    dve.tensor_tensor(v4(T0[:, :, :]), v4(T0[:, :, :]), low[:, :, :].unsqueeze(1).to_broadcast([P, TW, NX, NX]), ALU.mult)
                    link(dve.tensor_tensor(v4(T1[:, :, :]), v4(T1[:, :, :]), high[:, :, :].unsqueeze(1).to_broadcast([P, TW, NX, NX]), ALU.mult))
                    link(dve.tensor_tensor(T2[:, :, :], T0[:, :, :], T1[:, :, :], ALU.add))
                    dve.tensor_reduce(U0[:, :, :], v4(T2[:, :, :]), AX.X, ALU.add)
                    link(dve.tensor_reduce(s4[:, :], sc[:, :, :], AX.X, ALU.max))
                    dve.tensor_tensor(xs[:, :, :], sc[:, :, :], b4(s4[:, :]), ALU.subtract).then_inc(v_x, 1)
                    link(dve.tensor_scalar(U0[:, :, :], U0[:, :, :], 1.5, None, ALU.is_lt))
                    dve.wait_ge(a_x, k * 3 + 3)
                    link(dve.tensor_tensor(U1[:, :, :], es[:, :, :], U0[:, :, :], ALU.mult))
                    link(dve.tensor_reduce(s4[:, :], U1[:, :, :], AX.X, ALU.add))
                    link(dve.reciprocal(s4[:, :], s4[:, :]))
                    link(dve.tensor_tensor(G[:, :, :].rearrange("p e t -> p t e"), U1[:, :, :], b4(s4[:, :]), ALU.mult))
                    link(dve.tensor_scalar(GH[:, par, 0:NX, :], G[:, :, :], GSPLIT, None, ALU.mult))
                    dve.scalar_tensor_tensor(GH[:, par, NX:2 * NX, :], G[:, :, :], GSPLIT, GH[:, par, 0:NX, :], ALU.mult,
                                             ALU.subtract).then_inc(v_g, 1)
                    assert cnt[0] == NL, cnt
                    dve.wait_ge(v_g, k + 1)
                    dve.sem_inc(slot_free, 1)


def experts(nc, n, W1, b1, W2, b2):
    B, C, NP, NX, HID = n.B, n.C, n.NP, n.NX, n.HID
    CW = 384
    NCH = NP // CW
    PARTS = 3
    with ExitStack() as ctx:
        def sb(name, shape, dt=F32):
            return ctx.enter_context(nc.sbuf_tensor(name, shape, dt))

        def pb(name):
            return ctx.enter_context(nc.psum_tensor(name, [P, 512], F32))

        def sem(name):
            return ctx.enter_context(nc.semaphore(name))
        w1 = sb("w1", [2 * C, NX, HID])
        w1p = sb("w1p", [2 * C, PARTS, NX, HID], BF16)
        w2 = sb("w2", [HID, NX, C])
        b1r = sb("b1r", [NX, HID])
        b1t = sb("b1t", [HID, NX])
        b2r = sb("b2r", [2 * NX, C])
        b2p = sb("b2p", [2 * NX, PARTS, C], BF16)
        pickf = sb("pickf", [2 * NX, NX, HID])
        pick = sb("pick", [2 * NX, NX, HID], BF16)
        tn = sb("tne", [2 * C, 2, NP], F16)
        x2 = sb("x2e", [C, 2, NP])
        g = sb("ge", [2 * NX, 2, NP], F16)
        hid = sb("hid", [HID, 4, CW])
        hg = sb("hg", [HID, 4, CW])
        half = sb("ehalf", [C, CW])
        res = sb("res", [C, 2, NP])
        up = [pb(f"up{i}") for i in range(3)]
        gb = [pb(f"gb{i}") for i in range(3)]
        acc = [pb("eacc0"), pb("eacc1")]
        w_in = sem("ew_in")
        pk = sem("pk")
        pe_b = sem("pe_b")
        v_b = sem("v_b")
        v_w = sem("v_w")
        in_ = [sem("e_in0"), sem("e_in1")]
        pe_up = sem("pe_up")
        a_hid = sem("a_hid")
        v_hg = sem("v_hg")
        pe_dn = sem("pe_dn")
        v_half = sem("v_half")
        v_res = sem("v_res")
        free = sem("efree")
        left = sem("eleft")
        passed = sem("epassed")
        r_out = [sem("r_out0"), sem("r_out1")]
        block = ctx.enter_context(nc.Block())
        STEPS = NCH * NX

        @block.sync
        def _(sp):
            for h in (0, C):
                sp.dma_start(w1[h:h + C, :, :], W1.rearrange("e c h -> c e h")).then_inc(w_in, 16)
            sp.dma_start(w2[:, :, :], W2.rearrange("e h c -> h e c")).then_inc(w_in, 16)
            sp.dma_start(b1r[:, :], b1).then_inc(w_in, 16)
            for h in (0, NX):
                sp.dma_start(b2r[h:h + NX, :], b2).then_inc(w_in, 16)
            with sp.Fori(0, B // 2) as ii:
                for par in range(2):
                    b = ii * 2 + par
                    sp.wait_ge(free, b + 1)
                    one = lambda t: t[bass.ds(b, 1), :, :].rearrange("a c p -> (a c) p")
                    sp.dma_start(tn[:, par, :], one(n.tn)).then_inc(in_[par], 16)
                    sp.dma_start(x2[:, par, :], one(n.x2)).then_inc(in_[par], 16)
                    sp.dma_start(g[:, par, :], n.gates[:, bass.ds(b * NP, NP)]).then_inc(in_[par], 16)

        @block.gpsimd
        def _(pool):
            pool.memset(pickf[:, :, :], 0.0).then_inc(pk, 1)
            for k in range(2):
                pool.wait_ge(pk, k + 1)
                pool.affine_select(out=pickf[:, :, :], in_=pickf[:, :, :], compare_op=ALU.not_equal, fill=1.0 / GSPLIT,
                                   base=-k * NX, pattern=[[-1, NX], [0, HID]], channel_multiplier=1).then_inc(pk, 1)
            pool.wait_ge(pk, 3)
            pool.tensor_copy(pick[:, :, :], pickf[:, :, :]).then_inc(pk, 1)
            with pool.Fori(0, B // 2) as ii:
                for par in range(2):
                    pool.wait_ge(v_res, (ii * 2 + par + 1) * NCH)
                    pool.sem_inc(passed, 1)
                    pool.dma_start(n.of[bass.ds(ii * 2 + par, 1), :, :].rearrange("a c p -> (a c) p"), res[:, par, :]).then_inc(r_out[par], 16)
                for par in range(2):
                    pool.wait_ge(r_out[par], (ii + 1) * 16)
                    pool.sem_inc(passed, 1)
                pool.sem_inc(left, 1)

        @block.tensor
        def _(pe):
            pe.wait_ge(w_in, 96)
            pe.wait_ge(pk, 4)
            pe.transpose(up[0][0:HID, 0:NX], b1r[:, :], n.ident[0:NX, 0:NX]).then_inc(pe_b, 1)
            pe.wait_ge(v_b, 1)
            pe.wait_ge(v_w, 2 * (2 * PARTS - 1))
            with pe.Fori(0, B // 2) as ii:
                for par in range(2):
                    b = ii * 2 + par
                    pe.wait_ge(in_[par], (ii + 1) * 48)
                    for t in range(STEPS + 3):
                        if t < STEPS:
                            c, e = divmod(t, NX)
                            rhs = tn[:, par, c * CW:(c + 1) * CW]
                            if t >= 3:
                                pe.wait_ge(v_hg, b * STEPS + t - 2)
                            for k in range(PARTS):
                                pe.matmul(up[t % 3][:, 0:CW], w1p[:, k, e, :], rhs, start=k == 0, stop=k == PARTS - 1)
                            pe.matmul(gb[t % 3][:, 0:CW], pick[:, e, :], g[:, par, c * CW:(c + 1) * CW], start=True, stop=True).then_inc(pe_up, 1)
                        u = t - 3
                        if u >= 0 and u % 2 == 0:
                            c, e = divmod(u, NX)
                            if e == 0:
                                if c >= 2:
                                    pe.wait_ge(v_res, b * NCH + c - 1)
                                for k in range(PARTS):
                                    pe.matmul(acc[c % 2][0:C, 0:CW], b2p[:, k, :], g[:, par, c * CW:(c + 1) * CW], start=k == 0, stop=False)
                            pe.wait_ge(v_hg, b * STEPS + u + 2)
                            for v in (u, u + 1):
                                h = C * (v % 2)
                                pe.matmul(acc[c % 2][h:h + C, 0:CW], w2[:, v % NX, :], hg[:, v % 4, :], start=v % NX == 1,
                                          stop=v % NX >= NX - 2).then_inc(pe_dn, 1)
                    pe.wait_ge(v_res, (b + 1) * NCH)

        @block.scalar
        def _(act):
            act.wait_ge(v_b, 1)
            with act.Fori(0, B // 2) as ii:
                for par in range(2):
                    b = ii * 2 + par
                    for t in range(STEPS):
                        act.wait_ge(pe_up, b * STEPS + t + 1)
                        if t >= 4:
                            act.wait_ge(v_hg, b * STEPS + t - 3)
                        act.activation(hid[:, t % 4, :], up[t % 3][:, 0:CW], ACT.Gelu, bias=b1t[:, t % NX:t % NX + 1],
                                       scale=1.0 / SPLIT).then_inc(a_hid, 1)

        @block.vector
        def _(dve):
            dve.wait_ge(pe_b, 1)
            dve.tensor_copy(b1t[:, :], up[0][0:HID, 0:NX]).then_inc(v_b, 1)
            dve.tensor_scalar(b2r[:, :], b2r[:, :], 1.0 / GSPLIT, None, ALU.mult).then_inc(v_b, 1)
            dve.wait_ge(v_b, 2)
            done = 0
            for full, parts, at in ((w1, w1p, lambda k: w1p[:, k, :, :].rearrange("c e h -> c (e h)")), (b2r, b2p, lambda k: b2p[:, k, :])):
                rest = w1[:, :, :].rearrange("c e h -> c (e h)") if full is w1 else b2r[:, :]
                for k in range(PARTS):
                    dve.tensor_copy(at(k), rest).then_inc(v_w, 1)
                    done += 1
                    dve.wait_ge(v_w, done)
                    if k < PARTS - 1:
                        dve.tensor_tensor(rest, rest, at(k), ALU.subtract).then_inc(v_w, 1)
                        done += 1
                        dve.wait_ge(v_w, done)
            dve.sem_inc(free, 2)
            dve.sem_inc(left, 1)

            def sums(b, par, c):
                cols = slice(c * CW, (c + 1) * CW)
                dve.wait_ge(pe_dn, b * STEPS + (c + 1) * NX)
                dve.tensor_tensor(half[:, :], acc[c % 2][0:C, 0:CW], x2[:, par, cols], ALU.add).then_inc(v_half, 1)
                dve.wait_ge(v_half, b * NCH + c + 1)
                dve.tensor_tensor(res[:, par, cols], acc[c % 2][C:2 * C, 0:CW], half[:, :], ALU.add).then_inc(v_res, 1)
            with dve.Fori(0, B // 2) as ii:
                dve.wait_ge(left, ii + 1)
                for par in range(2):
                    b = ii * 2 + par
                    for t in range(STEPS):
                        c, e = divmod(t, NX)
                        dve.wait_ge(a_hid, b * STEPS + t + 1)
                        if t >= 4:
                            dve.wait_ge(pe_dn, b * STEPS + t - 3)
                        dve.tensor_tensor(hg[:, t % 4, :], gb[t % 3][:, 0:CW], hid[:, t % 4, :], ALU.mult).then_inc(v_hg, 1)
                        if e == 2 and c:
                            sums(b, par, c - 1)
                    sums(b, par, NCH - 1)
                    dve.wait_ge(v_res, (b + 1) * NCH)
                    dve.sem_inc(free, 1)


_INS = ["x", "L0_conv_Wc", "L0_conv_bc", "L0_ffn_W_gat", "L0_ffn_att_src", "L0_ffn_att_dst", "L0_ffn_b_gat", "L0_ffn_ln_gamma",
        "L0_ffn_ln_beta", "L0_ffn_W1", "L0_ffn_b1", "L0_ffn_W2", "L0_ffn_b2", "L0_ffn_edge_index"]


def kernel(**inputs):
    import concourse.bacc as bacc
    from concourse.bass_utils import run_bass_kernel_spmd

    nc = bacc.Bacc("TRN2", target_bir_lowering=False, num_devices=1)
    arrays = {f"in_{name}": np.ascontiguousarray(inputs[name]) for name in _INS}
    args = [nc.dram_tensor(k, a.shape, mybir.dt.from_np(a.dtype), kind="ExternalInput").ap() for k, a in arrays.items()]
    out = nc.dram_tensor("out_0", inputs["x"].shape, F32, kind="ExternalOutput").ap()
    kernel_program(nc, *args, out)
    return run_bass_kernel_spmd(nc, [arrays], core_ids=[0]).results[0]["out_0"]
```
